# Optimizing a Trainium2 kernel written in Bass

```python
import numpy as np
import jax
import jax.numpy as jnp

def _softmax(x, axis=-1):
    return jax.nn.softmax(x, axis=axis)

def _gelu(x):
    return jax.nn.gelu(x, approximate=True)

def _silu(x):
    return jax.nn.silu(x)

def _sigmoid(x):
    return jax.nn.sigmoid(x)

def _layernorm(x, axis=-1, eps=1e-05):
    m = jnp.mean(x, axis=axis, keepdims=True)
    v = jnp.var(x, axis=axis, keepdims=True)
    return (x - m) / jnp.sqrt(v + eps)

def _scatter_add(tgt, idx, src, axis=0):
    return tgt.at[idx].add(src)

def _segment_sum(src, seg, n):
    return jax.ops.segment_sum(src, seg, n)
kernel_name = 'mk_vit_tower_d2_tok_img768_r4_90d567'

def setup_inputs(seed: int=0):
    np.random.seed(seed)
    _w = jnp.asarray

    def _rec_inputs():
        import jax
        import jax.numpy as jnp
        _rk = jax.random.key(seed)
        x = -0.000356955 + 1 * jax.random.normal(jax.random.fold_in(_rk, 1), (64, 3, 224, 224), jnp.float32)
        return x
    x = _rec_inputs()

    def _L0_tok_setup():
        import jax, jax.numpy as jnp
        import numpy as np
        C, H, W_IMG = (3, 224, 224)
        NP = 14
        PS = H // NP
        D_IN = C * PS * PS
        D = 192
        SEQ = NP * NP + 1
        B = 128

        def _sinusoidal_pos_embed(seq_len, d):
            i = np.arange(seq_len, dtype=np.float64)[:, None]
            j = np.arange(d, dtype=np.float64)[None, :]
            angle = i / np.power(10000.0, (j - j % 2) / d)
            pe = np.where(j % 2 == 0, np.sin(angle), np.cos(angle))
            return jnp.asarray(pe, dtype=jnp.float32)
        key = jax.random.key(seed)
        kx, kw, kc = jax.random.split(key, 3)
        x = jax.random.normal(kx, (B, C, H, W_IMG), dtype=jnp.float32)
        W = jax.random.normal(kw, (D, D_IN), dtype=jnp.float32) * 0.02
        b = jnp.zeros((D,), dtype=jnp.float32)
        class_token = jax.random.uniform(kc, (1, D), dtype=jnp.float32)
        pos_embed = _sinusoidal_pos_embed(SEQ, D)
        return {'x': x, 'W': W, 'b': b, 'class_token': class_token, 'pos_embed': pos_embed}
    _L0_tok_all = _L0_tok_setup()
    _L0_tok_in = {k: v for k, v in _L0_tok_all.items() if k in ('W', 'b', 'class_token', 'pos_embed')}
    del _L0_tok_all

    def _L0_attn_setup():
        import jax, jax.numpy as jnp
        import numpy as np
        B, N, C = (64, 80, 192)
        NUM_HEADS = 12
        LENS_Z = 64
        SCALE = (C // NUM_HEADS) ** (-0.5)
        key = jax.random.key(seed)
        k1, k2, k3 = jax.random.split(key, 3)
        x = jax.random.normal(k1, (B, N, C), dtype=jnp.float32)
        proj_w = jax.random.normal(k2, (C, C), dtype=jnp.float32) * 0.02
        proj_b = jax.random.normal(k3, (C,), dtype=jnp.float32) * 0.02
        return {'x': x, 'proj_w': proj_w, 'proj_b': proj_b}
    _L0_attn_all = _L0_attn_setup()
    _L0_attn_in = {k: v for k, v in _L0_attn_all.items() if k in ('proj_w', 'proj_b')}
    del _L0_attn_all

    def _L0_ffn_setup():
        import math
        import jax, jax.numpy as jnp
        import numpy as np
        EMBED_CHOICES = [96, 144, 192]
        RATIO_CHOICES = [2, 3, 4]
        E_MAX = 192
        H_MAX = 768

        def new_gelu(x):
            c = math.sqrt(2.0 / math.pi)
            return 0.5 * x * (1.0 + jnp.tanh(c * (x + 0.044715 * x * x * x)))

        def _mixed_coeffs(alpha_e, alpha_r):
            h_idx = jnp.arange(H_MAX)
            d_idx = jnp.arange(E_MAX)
            C0 = jnp.zeros((H_MAX, E_MAX), jnp.float32)
            c0b = jnp.zeros((H_MAX,), jnp.float32)
            C1 = jnp.zeros((E_MAX, H_MAX), jnp.float32)
            c1b = jnp.zeros((E_MAX,), jnp.float32)
            for i, e in enumerate(EMBED_CHOICES):
                m_in = (d_idx < e).astype(jnp.float32)
                for j, r in enumerate(RATIO_CHOICES):
                    a = alpha_e[i] * alpha_r[j]
                    m_out = (h_idx < r * e).astype(jnp.float32)
                    C0 = C0 + a * (m_out[:, None] * m_in[None, :])
                    c0b = c0b + a * m_out
                    C1 = C1 + a * (m_in[:, None] * m_out[None, :])
                    c1b = c1b + a * m_in
            return (C0, c0b, C1, c1b)
        key = jax.random.key(seed)
        ks = jax.random.split(key, 6)
        x = jax.random.normal(ks[0], (8, 512, E_MAX), jnp.float32)
        w_fc = jax.random.normal(ks[1], (H_MAX, E_MAX), jnp.float32) * 0.02
        b_fc = jnp.zeros((H_MAX,), jnp.float32)
        w_proj = jax.random.normal(ks[2], (E_MAX, H_MAX), jnp.float32) * 0.02
        b_proj = jnp.zeros((E_MAX,), jnp.float32)
        alpha_e = jax.nn.softmax(jax.random.normal(ks[3], (3,), jnp.float32))
        alpha_r = jax.nn.softmax(jax.random.normal(ks[4], (3,), jnp.float32))
        return {'x': x, 'w_fc': w_fc, 'b_fc': b_fc, 'w_proj': w_proj, 'b_proj': b_proj, 'alpha_e': alpha_e, 'alpha_r': alpha_r}
    _L0_ffn_all = _L0_ffn_setup()
    _L0_ffn_in = {k: v for k, v in _L0_ffn_all.items() if k in ('w_fc', 'b_fc', 'w_proj', 'b_proj', 'alpha_e', 'alpha_r')}
    del _L0_ffn_all

    def _L1_attn_setup():
        import jax, jax.numpy as jnp
        import numpy as np
        HEADS = 12
        DIM_HEAD = 64
        PATCHES = 196
        DIM = 192
        BATCH = 8
        FRAMES = 16
        TOKENS = FRAMES * PATCHES + 1

        def _mhsa(q, k, v, scale):
            s = jnp.einsum('ghid,ghjd->ghij', q, k) * scale
            a = jax.nn.softmax(s, axis=-1)
            return jnp.einsum('ghij,ghjd->ghid', a, v)
        key = jax.random.key(seed)
        k1, k2, k3 = jax.random.split(key, 3)
        x = jax.random.normal(k1, (BATCH, TOKENS, DIM), dtype=jnp.float32)
        W_qkv = jax.random.normal(k2, (DIM, 3 * HEADS * DIM_HEAD), dtype=jnp.float32) * 0.02
        W_0 = jax.random.normal(k3, (HEADS * DIM_HEAD, DIM), dtype=jnp.float32) * 0.02
        return {'x': x, 'W_qkv': W_qkv, 'W_0': W_0}
    _L1_attn_all = _L1_attn_setup()
    _L1_attn_in = {k: v for k, v in _L1_attn_all.items() if k in ('W_qkv', 'W_0')}
    del _L1_attn_all

    def _L1_ffn_setup():
        import jax, jax.numpy as jnp
        import numpy as np
        QN, QP = (-8, 7)

        def round_pass(x):
            return x + jax.lax.stop_gradient(jnp.round(x) - x)

        def _quant_act(x, alpha_a):
            a = alpha_a.mean()
            return round_pass(jnp.clip(x / a, QN, QP))

        def _quant_w(w, alpha_w):
            return round_pass(jnp.clip(w / alpha_w[:, None], QN, QP))
        key = jax.random.key(seed)
        ks = jax.random.split(key, 9)
        B, S, D, H = (16, 256, 192, 768)

        def unif(k, shape):
            return jax.random.uniform(k, shape, jnp.float32, 0.02, 0.1)
        return {'x0': jax.random.normal(ks[0], (B, S, D), jnp.float32), 'w1': jax.random.normal(ks[1], (H, D), jnp.float32) * 0.02, 'b1': jax.random.normal(ks[2], (H,), jnp.float32) * 0.02, 'alpha_w1': unif(ks[3], (H,)), 'alpha_a1': unif(ks[4], (D,)), 'w2': jax.random.normal(ks[5], (D, H), jnp.float32) * 0.02, 'b2': jax.random.normal(ks[6], (D,), jnp.float32) * 0.02, 'alpha_w2': unif(ks[7], (D,)), 'alpha_a2': unif(ks[8], (H,))}
    _L1_ffn_all = _L1_ffn_setup()
    _L1_ffn_in = {k: v for k, v in _L1_ffn_all.items() if k in ('w1', 'b1', 'alpha_w1', 'alpha_a1', 'w2', 'b2', 'alpha_w2', 'alpha_a2')}
    del _L1_ffn_all
    return {'x': x, 'L0_tok_W': _L0_tok_in['W'], 'L0_tok_b': _L0_tok_in['b'], 'L0_tok_class_token': _L0_tok_in['class_token'], 'L0_tok_pos_embed': _L0_tok_in['pos_embed'], 'L0_attn_proj_w': _L0_attn_in['proj_w'], 'L0_attn_proj_b': _L0_attn_in['proj_b'], 'L0_ffn_w_fc': _L0_ffn_in['w_fc'], 'L0_ffn_b_fc': _L0_ffn_in['b_fc'], 'L0_ffn_w_proj': _L0_ffn_in['w_proj'], 'L0_ffn_b_proj': _L0_ffn_in['b_proj'], 'L0_ffn_alpha_e': _L0_ffn_in['alpha_e'], 'L0_ffn_alpha_r': _L0_ffn_in['alpha_r'], 'L1_attn_W_qkv': _L1_attn_in['W_qkv'], 'L1_attn_W_0': _L1_attn_in['W_0'], 'L1_ffn_w1': _L1_ffn_in['w1'], 'L1_ffn_b1': _L1_ffn_in['b1'], 'L1_ffn_alpha_w1': _L1_ffn_in['alpha_w1'], 'L1_ffn_alpha_a1': _L1_ffn_in['alpha_a1'], 'L1_ffn_w2': _L1_ffn_in['w2'], 'L1_ffn_b2': _L1_ffn_in['b2'], 'L1_ffn_alpha_w2': _L1_ffn_in['alpha_w2'], 'L1_ffn_alpha_a2': _L1_ffn_in['alpha_a2']}

def reference(x, L0_tok_W, L0_tok_b, L0_tok_class_token, L0_tok_pos_embed, L0_attn_proj_w, L0_attn_proj_b, L0_ffn_w_fc, L0_ffn_b_fc, L0_ffn_w_proj, L0_ffn_b_proj, L0_ffn_alpha_e, L0_ffn_alpha_r, L1_attn_W_qkv, L1_attn_W_0, L1_ffn_w1, L1_ffn_b1, L1_ffn_alpha_w1, L1_ffn_alpha_a1, L1_ffn_w2, L1_ffn_b2, L1_ffn_alpha_w2, L1_ffn_alpha_a2):
    import jax
    import jax.numpy as jnp

    def _L0_tok_ref(x, W, b, class_token, pos_embed):
        import jax, jax.numpy as jnp
        import numpy as np
        C, H, W_IMG = (3, 224, 224)
        NP = 14
        PS = H // NP
        D_IN = C * PS * PS
        D = 192
        SEQ = NP * NP + 1
        B = 128

        def _sinusoidal_pos_embed(seq_len, d):
            i = np.arange(seq_len, dtype=np.float64)[:, None]
            j = np.arange(d, dtype=np.float64)[None, :]
            angle = i / np.power(10000.0, (j - j % 2) / d)
            pe = np.where(j % 2 == 0, np.sin(angle), np.cos(angle))
            return jnp.asarray(pe, dtype=jnp.float32)
        n = x.shape[0]
        p = x.reshape(n, C, NP, PS, NP, PS)
        p = p.transpose(0, 2, 4, 1, 3, 5).reshape(n, NP * NP, D_IN)
        tokens = jnp.einsum('npd,hd->nph', p, W) + b
        cls = jnp.broadcast_to(class_token[None], (n, 1, D))
        tokens = jnp.concatenate([cls, tokens], axis=1)
        return tokens + pos_embed[None]

    def _L0_attn_ref(x, proj_w, proj_b):
        import jax, jax.numpy as jnp
        import numpy as np
        B, N, C = (64, 80, 192)
        NUM_HEADS = 12
        LENS_Z = 64
        SCALE = (C // NUM_HEADS) ** (-0.5)
        q = x[:, :LENS_Z]
        k = x[:, LENS_Z:]
        v = k
        attn = jnp.einsum('bqc,bkc->bqk', q, k) * SCALE
        attn = jax.nn.softmax(attn, axis=-1)
        out = jnp.einsum('bqk,bkc->bqc', attn, v)
        out = jnp.transpose(out, (0, 2, 1)).reshape(out.shape[0], -1, C)
        out = out @ proj_w.T + proj_b
        return jnp.concatenate([out, k], axis=1)

    def _L0_ffn_ref(x, w_fc, b_fc, w_proj, b_proj, alpha_e, alpha_r):
        import math
        import jax, jax.numpy as jnp
        import numpy as np
        EMBED_CHOICES = [96, 144, 192]
        RATIO_CHOICES = [2, 3, 4]
        E_MAX = 192
        H_MAX = 768

        def new_gelu(x):
            c = math.sqrt(2.0 / math.pi)
            return 0.5 * x * (1.0 + jnp.tanh(c * (x + 0.044715 * x * x * x)))

        def _mixed_coeffs(alpha_e, alpha_r):
            h_idx = jnp.arange(H_MAX)
            d_idx = jnp.arange(E_MAX)
            C0 = jnp.zeros((H_MAX, E_MAX), jnp.float32)
            c0b = jnp.zeros((H_MAX,), jnp.float32)
            C1 = jnp.zeros((E_MAX, H_MAX), jnp.float32)
            c1b = jnp.zeros((E_MAX,), jnp.float32)
            for i, e in enumerate(EMBED_CHOICES):
                m_in = (d_idx < e).astype(jnp.float32)
                for j, r in enumerate(RATIO_CHOICES):
                    a = alpha_e[i] * alpha_r[j]
                    m_out = (h_idx < r * e).astype(jnp.float32)
                    C0 = C0 + a * (m_out[:, None] * m_in[None, :])
                    c0b = c0b + a * m_out
                    C1 = C1 + a * (m_in[:, None] * m_out[None, :])
                    c1b = c1b + a * m_in
            return (C0, c0b, C1, c1b)
        C0, c0b, C1, c1b = _mixed_coeffs(alpha_e, alpha_r)
        W0 = w_fc * C0
        b0 = b_fc * c0b
        h = jnp.einsum('bte,he->bth', x, W0) + b0
        h = new_gelu(h)
        W1 = w_proj * C1
        b1 = b_proj * c1b
        out = jnp.einsum('bth,eh->bte', h, W1) + b1
        return out

    def _L1_attn_ref(x, W_qkv, W_0):
        import jax, jax.numpy as jnp
        import numpy as np
        HEADS = 12
        DIM_HEAD = 64
        PATCHES = 196
        DIM = 192
        BATCH = 8
        FRAMES = 16
        TOKENS = FRAMES * PATCHES + 1

        def _mhsa(q, k, v, scale):
            s = jnp.einsum('ghid,ghjd->ghij', q, k) * scale
            a = jax.nn.softmax(s, axis=-1)
            return jnp.einsum('ghij,ghjd->ghid', a, v)
        b, t, _ = x.shape
        h, dh, p = (HEADS, DIM_HEAD, PATCHES)
        scale = dh ** (-0.5)
        qkv = x @ W_qkv
        qkv = qkv.reshape(b, t, dh, 3, h)
        q = jnp.transpose(qkv[:, :, :, 0, :], (0, 3, 1, 2))
        k = jnp.transpose(qkv[:, :, :, 1, :], (0, 3, 1, 2))
        v = jnp.transpose(qkv[:, :, :, 2, :], (0, 3, 1, 2))
        cls_q, q3 = (q[:, :, :1], q[:, :, 1:])
        out_cls = _mhsa(cls_q, k, v, scale)
        cls_k, k3 = (k[:, :, :1], k[:, :, 1:])
        cls_v, v3 = (v[:, :, :1], v[:, :, 1:])
        f = (t - 1) // p

        def space_rearrange(z):
            z = z.reshape(b, h, f, p, dh)
            return jnp.transpose(z, (0, 2, 1, 3, 4)).reshape(b * f, h, p, dh)
        q_sep = space_rearrange(q3)
        k_sep = space_rearrange(k3)
        v_sep = space_rearrange(v3)
        cls_k = jnp.repeat(cls_k, f, axis=0)
        cls_v = jnp.repeat(cls_v, f, axis=0)
        kk = jnp.concatenate((cls_k, k_sep), axis=2)
        vv = jnp.concatenate((cls_v, v_sep), axis=2)
        out_sp = _mhsa(q_sep, kk, vv, scale)
        out_sp = out_sp.reshape(b, f, h, p, dh)
        out_sp = jnp.transpose(out_sp, (0, 2, 1, 3, 4)).reshape(b, h, f * p, dh)
        out = jnp.concatenate((out_cls, out_sp), axis=2)
        out = jnp.transpose(out, (0, 2, 1, 3)).reshape(b, t, h * dh)
        return out @ W_0

    def _L1_ffn_ref(x0, w1, b1, alpha_w1, alpha_a1, w2, b2, alpha_w2, alpha_a2):
        import jax, jax.numpy as jnp
        import numpy as np
        QN, QP = (-8, 7)

        def round_pass(x):
            return x + jax.lax.stop_gradient(jnp.round(x) - x)

        def _quant_act(x, alpha_a):
            a = alpha_a.mean()
            return round_pass(jnp.clip(x / a, QN, QP))

        def _quant_w(w, alpha_w):
            return round_pass(jnp.clip(w / alpha_w[:, None], QN, QP))
        xq = _quant_act(x0, alpha_a1)
        wq1 = _quant_w(w1, alpha_w1)
        x1 = jnp.einsum('bsd,hd->bsh', xq, wq1)
        x1 = x1 * alpha_w1 * alpha_a1.mean() + b1
        x1 = jax.nn.gelu(x1, approximate=False)
        x1 = jnp.clip(x1, -10.0, 10.0)
        hq = _quant_act(x1, alpha_a2)
        wq2 = _quant_w(w2, alpha_w2)
        x2 = jnp.einsum('bsh,dh->bsd', hq, wq2)
        x2 = x2 * alpha_w2 * alpha_a2.mean() + b2
        return x2
    h = _L0_tok_ref(x, L0_tok_W, L0_tok_b, L0_tok_class_token, L0_tok_pos_embed)
    h = h + _L0_attn_ref(_layernorm(h, axis=-1), L0_attn_proj_w, L0_attn_proj_b)
    h = h + _L0_ffn_ref(_layernorm(h, axis=-1), L0_ffn_w_fc, L0_ffn_b_fc, L0_ffn_w_proj, L0_ffn_b_proj, L0_ffn_alpha_e, L0_ffn_alpha_r)
    h = h + _L1_attn_ref(_layernorm(h, axis=-1), L1_attn_W_qkv, L1_attn_W_0)
    h = h + _L1_ffn_ref(_layernorm(h, axis=-1), L1_ffn_w1, L1_ffn_b1, L1_ffn_alpha_w1, L1_ffn_alpha_a1, L1_ffn_w2, L1_ffn_b2, L1_ffn_alpha_w2, L1_ffn_alpha_a2)
    return h

_drawn_inputs = setup_inputs


def setup_inputs(seed=0):
    import zlib

    import numpy as np

    out = dict(_drawn_inputs(seed))
    spreads = {'L0_tok_b': (0.0, 0.1), 'L0_ffn_b_fc': (0.0, 0.639), 'L0_ffn_b_proj': (0.0, 0.324)}
    factors = {'L0_tok_class_token': 11.896,
     'L0_attn_proj_b': 7.585,
     'L0_ffn_alpha_e': 2.892,
     'L0_ffn_alpha_r': 7.047,
     'L1_ffn_w1': 23.352,
     'L1_ffn_b1': 64.0,
     'L1_ffn_alpha_w1': 34.672,
     'L1_ffn_w2': 22.912,
     'L1_ffn_b2': 200.0,
     'L1_ffn_alpha_w2': 37.608,
     'L1_ffn_alpha_a2': 200.0,
     'L1_attn_W_qkv': 8.0,
     'L1_attn_W_0': 8.0}
    for name, (base, spread) in spreads.items():
        noise = np.random.default_rng([zlib.crc32(name.encode()), seed]).standard_normal(out[name].shape)
        drawn = base * np.exp(spread * noise) if base else spread * noise
        out[name] = jnp.asarray(drawn.astype(out[name].dtype))
    for name, factor in factors.items():
        out[name] = (out[name] * factor).astype(out[name].dtype)
    return out
```

```python
from contextlib import ExitStack

import concourse.bass as bass
from concourse import mybir

F32 = mybir.dt.float32
F16 = mybir.dt.float16
BF16 = mybir.dt.bfloat16
ALU = mybir.AluOpType
ACT = mybir.ActivationFunctionType
AX = mybir.AxisListType

P = 128
D = 192
KH = 96
PATCH_K = 6
SEQ = 197
TAIL = SEQ - P
ROWS = (P, TAIL)
COLS = (slice(0, P), slice(P, SEQ))
HID = 768
HC = HID // P
HEADS = 12
DH = 64
PAIRS = HEADS // 2
NQ = 64
NK = SEQ - NQ
NK1 = P - NQ
EPS = 1e-5
ROUND = 12582912.0
PARTS = ((0, 0), (0, 1), (1, 0))
EMBED_CHOICES = (96, 144, 192)
RATIO_CHOICES = (2, 3, 4)


def build(nc, A, out):
    n_img = A["x"].shape[0]
    with ExitStack() as ctx:
        def sb(name, shape, dt=F32):
            return ctx.enter_context(nc.sbuf_tensor(name, shape, dt))

        S = {
            "h": sb("h", [P, n_img, 2, D]),
            "stats": sb("stats", [P, n_img * 2, 6]),
            "mean": sb("mean", [P, n_img * 2]),
            "rstd": sb("rstd", [P, n_img * 2]),
            "ident": sb("ident", [P, P]),
            "ident16": sb("ident16", [P, P], F16),
            "ident_b": sb("ident_b", [P, P], BF16),
            "posb": sb("posb", [P, 2, D]),
            "tok_w": sb("tok_w", [P, PATCH_K, D]),
            "pw": sb("pw", [P, 2, 3, D], F16),
            "pb": sb("pb", [P, D]),
            "fc": sb("fc", [KH, 2, 2, HID], F16),
            "fc_bias": sb("fc_bias", [P, HC]),
            "fp": sb("fp", [P, 2, HC, D], F16),
            "fp_bias": sb("fp_bias", [P, D]),
            "wqkv": sb("wqkv", [KH, 2, 2, 3 * HID], F16),
            "wo": sb("wo", [P, 2, HC, D], F16),
            "q1": sb("q1", [KH, 2, HID], BF16),
            "q2": sb("q2", [P, HC, D], BF16),
            "q1_scale": sb("q1_scale", [P, HC]),
            "q1_bias": sb("q1_bias", [P, HC]),
            "q2_scale": sb("q2_scale", [P, D]),
            "q2_bias": sb("q2_bias", [P, D]),
            "inv_a1": sb("inv_a1", [P, 1]),
            "inv_a2": sb("inv_a2", [P, 1]),
            "q_lo": sb("q_lo", [P, 1]),
            "q_hi": sb("q_hi", [P, 1]),
        }
        prepare_weights(nc, A, S)
        embed_patches(nc, A, S, n_img)
        attention_0(nc, S, n_img)
        mlp_0(nc, S, n_img)
        attention_1(nc, S, n_img)
        mlp_1(nc, S, out, n_img)


def stage_tools(nc, ctx):
    def sb(name, shape, dt=F32):
        return ctx.enter_context(nc.sbuf_tensor(name, shape, dt))

    def ps(name, shape, dt=F32):
        return ctx.enter_context(nc.psum_tensor(name, shape, dt))

    def sem(name):
        return ctx.enter_context(nc.semaphore(name))

    return sb, ps, sem


def prepare_weights(nc, A, S):
    with ExitStack() as ctx:
        sb, ps, sem = stage_tools(nc, ctx)
        free, used = S["h"][:].rearrange("p i c d -> p (i c d)"), [0]
        if free.shape[1] < 18432:
            free = sb("raw_weights", [P, 18432])[:]

        def raw(rows, *shape):
            n = 1
            for k in shape:
                n *= k
            a = free[0:rows, used[0]:used[0] + n]
            used[0] += n
            if len(shape) == 2:
                a = a.rearrange("p (a b) -> p a b", a=shape[0])
            return a

        r_qkv = raw(KH, 2, 3 * HID)
        r_wo = raw(P, HC, D)
        r_pw = raw(P, 3, D)
        r_fc = raw(KH, 2, HID)
        r_fp = raw(KH, 2, HID)
        r_w1 = raw(KH, 2, HID)
        r_w2 = raw(P, HC, D)
        a_w1 = raw(KH, HID)
        a_w1c = raw(P, HC)
        a_w2 = raw(P, D)
        a_a1 = raw(P, D)
        a_a2 = raw(P, HID)
        g = raw(P, 3, HID)
        coef = raw(KH, 2, HID)
        alpha = sb("alpha", [P, 6])
        below = sb("below", [KH, 2, 3])
        c0b = sb("c0b", [1, HID])
        bfc = sb("bfc", [1, HID])
        one = sb("one", [1, 1])
        c1b = sb("c1b", [P, D])
        ar_sum = sb("ar_sum", [P, 1])
        cls_b = sb("cls_b", [P, 2, D])
        m1 = sb("m1", [P, 1])
        m2 = sb("m2", [P, 1])
        bank_t = [ps(f"w_turned{n}", [P, 4, P]) for n in range(3)]
        bank_b = ps("w_bias", [P, HC])
        loaded, qkv_loaded, zeroed, step, act_hi, turned, bias_col, masked = map(
            sem, ("w_loaded", "w_qkv_loaded", "w_zeroed", "w_step", "w_act_hi", "w_turned_done", "w_bias_col", "w_masked"))

        loads = [
            (alpha[:, 0:3], A["alpha_e"]), (alpha[:, 3:6], A["alpha_r"]), (below[:], A["below"]),
            (r_fc[:], A["fc"]), (r_fp[:], A["fproj"]), (bfc[:], A["fc_b"]), (S["fp_bias"][:], A["fproj_b"]),
            (r_w1[:], A["w1"]), (a_w1[:], A["alpha_w1_rows"]), (a_w1c[:], A["alpha_w1_cols"]),
            (r_w2[:], A["w2"]), (a_w2[:], A["alpha_w2"]), (a_a1[:], A["alpha_a1"]), (a_a2[:], A["alpha_a2"]),
            (S["q1_bias"][:], A["b1"]), (S["q2_bias"][:], A["b2"]),
            (S["ident"][:], A["identity"]), (S["posb"][:, 0, :], A["pos"][0:P, :]), (S["posb"][0:TAIL, 1, :], A["pos"][P:SEQ, :]),
            (cls_b[:, 0, :], A["cls_bias"][0:P, :]), (cls_b[0:TAIL, 1, :], A["cls_bias"][P:SEQ, :]),
            (S["tok_w"][:], A["tok_w"]), (S["pb"][:], A["proj_b"]),
            (r_pw[0:NQ], A["proj_w"]), (r_pw[NQ:P], A["proj_w"]), (r_wo[:], A["wo"]),
        ]
        with nc.Block() as block:
            @block.sync
            def _(sp):
                for dst, src in loads:
                    sp.dma_start(dst, src).then_inc(loaded, 16)
                sp.dma_start(r_qkv[:], A["wqkv"]).then_inc(qkv_loaded, 16)

            @block.scalar
            def _(act):
                act.wait_ge(loaded, 16 * len(loads))
                nc.scalar.activation(S["wo"][:, 0], r_wo[:], ACT.Copy).then_inc(act_hi, 1)
                nc.scalar.activation(S["pw"][:, 0], r_pw[:], ACT.Copy).then_inc(act_hi, 1)
                nc.scalar.activation(S["ident16"][:], S["ident"][:], ACT.Copy).then_inc(act_hi, 1)
                nc.scalar.activation(S["ident_b"][:], S["ident"][:], ACT.Copy).then_inc(act_hi, 1)
                act.wait_ge(qkv_loaded, 16)
                nc.scalar.activation(S["wqkv"][:, 0], r_qkv[:], ACT.Copy).then_inc(act_hi, 1)

            @block.vector
            def _(dve):
                done = [0]

                def then(ins):
                    done[0] += 1
                    ins.then_inc(step, 1)
                    dve.wait_ge(step, done[0])

                v = nc.vector
                v.memset(g[:], 0.0)
                v.memset(c1b[:], 0.0)
                then(v.memset(one[:], 1.0))
                dve.wait_ge(loaded, 16 * len(loads))
                for i, e in enumerate(EMBED_CHOICES):
                    for j, r in enumerate(RATIO_CHOICES):
                        then(v.tensor_scalar(g[:, i, 0:r * e], g[:, i, 0:r * e], alpha[:, 3 + j:4 + j], None, ALU.add))
                    then(v.tensor_scalar(g[:, i, :], g[:, i, :], alpha[:, i:i + 1], None, ALU.mult))
                for k in range(2):
                    then(v.tensor_scalar(coef[:, k, :], g[0:KH, 0, :], below[:, k, 0:1], None, ALU.mult))
                    for i in (1, 2):
                        then(v.scalar_tensor_tensor(out=coef[:, k, :], in0=g[0:KH, i, :], scalar=below[:, k, i:i + 1],
                                                    in1=coef[:, k, :], op0=ALU.mult, op1=ALU.add))
                then(v.tensor_tensor(c0b[:], g[0:1, 0, :], g[0:1, 1, :], ALU.add))
                then(v.tensor_tensor(c0b[:], c0b[:], g[0:1, 2, :], ALU.add))
                then(v.tensor_tensor(bfc[:], bfc[:], c0b[:], ALU.mult))
                then(v.tensor_tensor(r_fc[:], r_fc[:], coef[:], ALU.mult))
                v.tensor_tensor(r_fp[:], r_fp[:], coef[:], ALU.mult).then_inc(masked, 1)
                then(v.tensor_copy(S["fc"][:, 0], r_fc[:]))
                then(v.tensor_tensor(S["fc"][:, 1], r_fc[:], S["fc"][:, 0], ALU.subtract))
                then(v.reduce_sum(ar_sum[:], alpha[:, 3:6], AX.X))
                for i, e in enumerate(EMBED_CHOICES):
                    then(v.tensor_scalar(c1b[:, 0:e], c1b[:, 0:e], alpha[:, i:i + 1], None, ALU.add))
                then(v.tensor_scalar(c1b[:], c1b[:], ar_sum[:, 0:1], None, ALU.mult))
                then(v.tensor_tensor(S["fp_bias"][:], S["fp_bias"][:], c1b[:], ALU.mult))
                then(v.tensor_tensor(S["posb"][:, 0, :], S["posb"][:, 0, :], cls_b[:, 0, :], ALU.add))
                then(v.tensor_tensor(S["posb"][0:TAIL, 1, :], S["posb"][0:TAIL, 1, :], cls_b[0:TAIL, 1, :], ALU.add))
                then(v.reduce_sum(m1[:], a_a1[:], AX.X))
                then(v.tensor_scalar(m1[:], m1[:], 1.0 / D, None, ALU.mult))
                then(v.reciprocal(S["inv_a1"][:], m1[:]))
                then(v.reduce_sum(m2[:], a_a2[:], AX.X))
                then(v.tensor_scalar(m2[:], m2[:], 1.0 / HID, None, ALU.mult))
                then(v.reciprocal(S["inv_a2"][:], m2[:]))
                then(v.tensor_scalar(S["q_lo"][:], S["inv_a2"][:], -10.0, -8.0, ALU.mult, ALU.max))
                then(v.tensor_scalar(S["q_hi"][:], S["inv_a2"][:], 10.0, 7.0, ALU.mult, ALU.min))
                then(v.tensor_scalar(S["q1_scale"][:], a_w1c[:], m1[:, 0:1], None, ALU.mult))
                then(v.tensor_scalar(S["q2_scale"][:], a_w2[:], m2[:, 0:1], None, ALU.mult))
                then(v.reciprocal(a_w1[:], a_w1[:]))
                then(v.reciprocal(a_w2[:], a_w2[:]))
                for k in range(2):
                    then(v.tensor_tensor(r_w1[:, k], r_w1[:, k], a_w1[:], ALU.mult))
                for k in range(HC):
                    then(v.tensor_tensor(r_w2[:, k], r_w2[:, k], a_w2[:], ALU.mult))
                for r, q in ((r_w1, S["q1"]), (r_w2, S["q2"])):
                    then(v.tensor_scalar(r[:], r[:], -8.0, 7.0, ALU.max, ALU.min))
                    then(v.tensor_scalar(q[:], r[:], ROUND, -ROUND, ALU.add, ALU.add))
                dve.wait_ge(turned, 1)
                for n in range(3):
                    hi = S["fp"][:, 0, 2 * n:2 * n + 2, :].rearrange("p f (k d) -> p (f k) d", k=2)
                    lo = S["fp"][:, 1, 2 * n:2 * n + 2, :].rearrange("p f (k d) -> p (f k) d", k=2)
                    then(v.tensor_copy(hi, bank_t[n][:, :, 0:KH]))
                    then(v.tensor_tensor(lo, bank_t[n][:, :, 0:KH], hi, ALU.subtract))
                dve.wait_ge(bias_col, 1)
                then(v.tensor_copy(S["fc_bias"][:], bank_b[:]))
                dve.wait_ge(act_hi, 5)
                v.tensor_tensor(S["wo"][:, 1], r_wo[:], S["wo"][:, 0], ALU.subtract)
                v.tensor_tensor(S["pw"][:, 1], r_pw[:], S["pw"][:, 0], ALU.subtract)
                v.tensor_tensor(S["wqkv"][:, 1], r_qkv[:], S["wqkv"][:, 0], ALU.subtract)

            @block.tensor
            def _(pe):
                pe.wait_ge(masked, 1)
                for n in range(3):
                    for f in range(2):
                        for k in range(2):
                            last = nc.tensor.transpose(bank_t[n][:, 2 * f + k, 0:KH],
                                                       r_fp[:, k, (2 * n + f) * P:(2 * n + f + 1) * P],
                                                       S["ident"][0:KH, 0:KH])
                last.then_inc(turned, 1)
                for f in range(HC):
                    last = nc.tensor.matmul(bank_b[:, f:f + 1], bfc[:, f * P:(f + 1) * P], one[:], start=True, stop=True)
                last.then_inc(bias_col, 1)


def embed_patches(nc, A, S, n_img):
    h, BUF = S["h"], 4
    with ExitStack() as ctx:
        sb, ps, sem = stage_tools(nc, ctx)
        patches = [sb(f"patches{b}", [P, PATCH_K, SEQ]) for b in range(BUF)]
        tokens = [ps(f"tokens{b}", [P, 512]) for b in range(BUF)]
        zeroed, h_written = sem("t_zeroed"), sem("t_h_written")
        loaded = [sem(f"t_loaded{b}") for b in range(BUF)]
        made = [sem(f"t_made{b}") for b in range(BUF)]
        taken = [sem(f"t_taken{b}") for b in range(BUF)]

        def rounds(eng, fn):
            fn(0)
            if n_img > BUF:
                with eng.Fori(1, n_img // BUF) as g:
                    fn(g)

        with nc.Block() as block:
            @block.sync
            def _(sp):
                def load(g):
                    for b in range(BUF):
                        sp.wait_ge(made[b], g)
                        sp.dma_start(patches[b][:, :, 1:SEQ], A["x"][g * BUF + b]).then_inc(loaded[b], 16)

                rounds(sp, load)

            @block.gpsimd
            def _(pool):
                for b in range(BUF):
                    last = nc.gpsimd.memset(patches[b][:, :, 0:1], 0.0)
                last.then_inc(zeroed, 1)

            @block.tensor
            def _(pe):
                pe.wait_ge(zeroed, 1)
                def multiply(g):
                    for b in range(BUF):
                        pe.wait_ge(loaded[b], 16 * (g + 1))
                        pe.wait_ge(taken[b], g)
                        for c in range(2):
                            for k in range(PATCH_K):
                                last = nc.tensor.matmul(tokens[b][0:ROWS[c], c * D:(c + 1) * D], patches[b][:, k, COLS[c]],
                                                        S["tok_w"][:, k, :], start=(k == 0), stop=(k == PATCH_K - 1))
                        last.then_inc(made[b], 1)

                rounds(pe, multiply)

            @block.vector
            def _(dve):
                nc.vector.memset(S["stats"][:], 0.0)

                def add_position(g):
                    for b in range(BUF):
                        i = g * BUF + b
                        dve.wait_ge(made[b], g + 1)
                        for c in range(2):
                            last = nc.vector.tensor_tensor(h[0:ROWS[c], i, c, :], tokens[b][0:ROWS[c], c * D:(c + 1) * D],
                                                           S["posb"][0:ROWS[c], c, :], ALU.add)
                        last.then_inc(taken[b], 1)
                        dve.wait_ge(taken[b], g + 1)
                        for c in range(2):
                            nc.vector.bn_stats(S["stats"][0:ROWS[c], 2 * i + c, :], h[0:ROWS[c], i, c, :])

                rounds(dve, add_position)


def norm_tables(nc, sb, sem, S, tag):
    n = S["mean"].shape[1]
    tmp = [sb(f"{tag}_tmp{k}", [P, n]) for k in range(3)]
    step, var_ready, root_ready = sem(f"{tag}_step"), sem(f"{tag}_var_ready"), sem(f"{tag}_root_ready")
    st = S["stats"]
    mean, rstd = S["mean"], S["rstd"]
    half = D / 2

    def vector(dve):
        done = [0]

        def then(ins):
            done[0] += 1
            ins.then_inc(step, 1)
            dve.wait_ge(step, done[0])

        v = nc.vector
        then(v.tensor_tensor(mean[:], st[:, :, 1], st[:, :, 4], ALU.add))
        then(v.tensor_scalar(mean[:], mean[:], 0.5, None, ALU.mult))
        then(v.tensor_tensor(tmp[0][:], st[:, :, 1], st[:, :, 4], ALU.subtract))
        then(v.scalar_tensor_tensor(out=tmp[0][:], in0=tmp[0][:], scalar=half / 2, in1=tmp[0][:], op0=ALU.mult, op1=ALU.mult))
        then(v.tensor_tensor(tmp[1][:], st[:, :, 2], st[:, :, 5], ALU.add))
        then(v.tensor_tensor(tmp[0][:], tmp[0][:], tmp[1][:], ALU.add))
        v.tensor_scalar(tmp[0][:], tmp[0][:], 1.0 / D, EPS, ALU.mult, ALU.add).then_inc(var_ready, 1)
        dve.wait_ge(root_ready, 1)
        then(v.reciprocal(rstd[:], tmp[1][:]))
        then(v.tensor_tensor(tmp[2][:], rstd[:], rstd[:], ALU.mult))
        then(v.tensor_tensor(tmp[2][:], tmp[2][:], tmp[0][:], ALU.mult))
        then(v.tensor_scalar(tmp[2][:], tmp[2][:], -0.5, 1.5, ALU.mult, ALU.add))
        then(v.tensor_tensor(rstd[:], rstd[:], tmp[2][:], ALU.mult))

    def scalar(act):
        act.wait_ge(var_ready, 1)
        nc.scalar.activation(tmp[1][:], tmp[0][:], ACT.Sqrt).then_inc(root_ready, 1)

    return vector, scalar


def pipeline(eng, turns, order):
    for t in (-2, -1):
        for fn, ahead in order:
            if t + ahead >= 0:
                fn(0, t + ahead)
    def both(u):
        for b in range(2):
            for fn, ahead in order:
                fn(u + (b + ahead) // 2, (b + ahead) % 2)

    if turns > 1:
        both(0)
    if turns > 2:
        with eng.Fori(1, turns - 1) as u:
            both(u)
    for b in range(2):
        for fn, ahead in order:
            if b + ahead < 2:
                fn(turns - 1, b + ahead)


def attention_0(nc, S, n_img):
    h, mean, rstd = S["h"], S["mean"], S["rstd"]
    turns = n_img // 4
    SP = SEQ + 1
    SCALE = float(16) ** -0.5
    with ExitStack() as ctx:
        sb, ps, sem = stage_tools(nc, ctx)
        xn = [sb(f"xn{b}", [P, 2, 2, D]) for b in range(2)]
        xs = [sb(f"xs{b}", [P, 2, 2, 2, D], F16) for b in range(2)]
        xt = [sb(f"xt{b}", [KH, 2, 2, 2, SP], F16) for b in range(2)]
        pr = [sb(f"pr{b}", [P, NK]) for b in range(2)]
        prs = [sb(f"prs{b}", [P, 2, NK], F16) for b in range(2)]
        pt = [sb(f"pt{b}", [P, 2, 2 * P], F16) for b in range(2)]
        o = [sb(f"o{b}", [P, D]) for b in range(2)]
        os_ = [sb(f"os{b}", [P, 2, D], F16) for b in range(2)]
        mx = [sb(f"mx{b}", [P, 1]) for b in range(2)]
        nmx = [sb(f"nmx{b}", [P, 1]) for b in range(2)]
        rsum = [sb(f"rsum{b}", [P, 1]) for b in range(2)]
        rinv = [sb(f"rinv{b}", [P, 1]) for b in range(2)]
        bank_x = [ps(f"bank_x{p}", [KH, 2, 2, 256], F16) for p in range(2)]
        bank_s = ps("bank_s", [P, 512])
        bank_p = ps("bank_p", [P, 2, 512], F16)
        bank_o = ps("bank_o", [P, 512])
        bank_r = [ps(f"bank_r{m}", [P, 512]) for m in range(2)]
        two = lambda name: [sem(f"a_{name}{b}") for b in range(2)]
        xn_made, xn_hi, xn_split = two("xn_made"), two("xn_hi"), two("xn_split")
        turned_x, xt_hi, xt_lo = two("turned_x"), two("xt_hi"), two("xt_lo")
        keys_added, upper_added, scored, max_found, max_made, exp_made = two("keys_added"), two("upper_added"), two("scored"), two("max_found"), two("max_made"), two("exp_made")
        sum_inverted, pr_hi, pr_split = two("sum_inverted"), two("pr_hi"), two("pr_split")
        turned_p, pt_done = two("turned_p"), two("pt_done")
        mixed, o_made, o_hi, o_split = two("mixed"), two("o_made"), two("o_hi"), two("o_split")
        projected, h_done = two("projected"), two("h_done")
        norm_done = sem("a_norm_done")
        norm_v, norm_s = norm_tables(nc, sb, sem, S, "n0")

        def image(u, b, m):
            return 4 * u + 2 * b + m

        with nc.Block() as block:
            @block.vector
            def _(dve):
                v = nc.vector
                norm_v(dve)

                def normalise(u, b):
                    dve.wait_ge(keys_added[b], u)
                    dve.wait_ge(xn_split[b], u)
                    for m in range(2):
                        i = image(u, b, m)
                        for c in range(2):
                            last = v.tensor_scalar(xn[b][0:ROWS[c], m, c, :], h[0:ROWS[c], i, c, :],
                                                   mean[0:ROWS[c], bass.ds(2 * i + c, 1)], rstd[0:ROWS[c], bass.ds(2 * i + c, 1)],
                                                   ALU.subtract, ALU.mult)
                    last.then_inc(xn_made[b], 1)
                    dve.wait_ge(xn_hi[b], u + 1)
                    for c in range(2):
                        last = v.tensor_tensor(xs[b][0:ROWS[c], 1, :, c, :], xn[b][0:ROWS[c], :, c, :],
                                               xs[b][0:ROWS[c], 0, :, c, :], ALU.subtract)
                    last.then_inc(xn_split[b], 1)

                def take_turned_x(u, b):
                    dve.wait_ge(turned_x[b], u + 1)
                    v.tensor_copy(xt[b][:, 1, :, :, 0:SEQ], bank_x[1][:, :, :, 0:SEQ]).then_inc(xt_lo[b], 1)

                def maximum(u, b):
                    dve.wait_ge(scored[b], u + 1)
                    v.reduce_max(mx[b][:], bank_s[:, 0:NK], AX.X).then_inc(max_found[b], 1)
                    dve.wait_ge(max_found[b], u + 1)
                    v.tensor_scalar(nmx[b][:], mx[b][:], -SCALE, None, ALU.mult).then_inc(max_made[b], 1)

                def split_probabilities(u, b):
                    dve.wait_ge(exp_made[b], u + 1)
                    v.reciprocal(rinv[b][:], rsum[b][:]).then_inc(sum_inverted[b], 1)
                    v.tensor_copy(prs[b][:, 0, :], pr[b][:]).then_inc(pr_hi[b], 1)
                    dve.wait_ge(pr_hi[b], u + 1)
                    v.tensor_tensor(prs[b][:, 1, :], pr[b][:], prs[b][:, 0, :], ALU.subtract).then_inc(pr_split[b], 1)

                def take_turned_p(u, b):
                    dve.wait_ge(turned_p[b], u + 1)
                    v.tensor_copy(pt[b][NK1:P, :, 0:P], bank_p[NK1:P, :, 0:P])
                    v.tensor_copy(pt[b][0:TAIL, :, P:2 * P], bank_p[0:TAIL, :, P:2 * P]).then_inc(pt_done[b], 1)

                def split_o(u, b):
                    dve.wait_ge(o_made[b], u + 1)
                    v.tensor_copy(os_[b][:, 0, :], o[b][:]).then_inc(o_hi[b], 1)
                    dve.wait_ge(o_hi[b], u + 1)
                    v.tensor_tensor(os_[b][:, 1, :], o[b][:], os_[b][:, 0, :], ALU.subtract).then_inc(o_split[b], 1)

                def finish(u, b):
                    dve.wait_ge(projected[b], u + 1)
                    dve.wait_ge(keys_added[b], u + 1)
                    for m in range(2):
                        i = image(u, b, m)
                        last = v.tensor_tensor(h[0:NQ, i, 0, :], bank_r[m][0:NQ, 0:D], h[0:NQ, i, 0, :], ALU.add)
                    last.then_inc(h_done[b], 1)
                    dve.wait_ge(h_done[b], u + 1)
                    for m in range(2):
                        i = image(u, b, m)
                        for c in range(2):
                            v.bn_stats(S["stats"][0:ROWS[c], 2 * i + c, :], h[0:ROWS[c], i, c, :])

                pipeline(dve, turns, [(maximum, 1), (split_o, 0), (normalise, 2), (split_probabilities, 1), (take_turned_x, 2),
                                      (take_turned_p, 1), (finish, 0)])

            @block.gpsimd
            def _(pool):
                def add_keys(u, b):
                    pool.wait_ge(xn_made[b], u + 1)
                    pool.wait_ge(keys_added[1 - b], u + b)
                    for m in range(2):
                        i = image(u, b, m)
                        last = nc.gpsimd.tensor_tensor(h[NK1:P, i, 0, :], h[NK1:P, i, 0, :], xn[b][NK1:P, m, 0, :], ALU.add)
                    last.then_inc(upper_added[b], 1)
                    pool.wait_ge(upper_added[b], u + 1)
                    for m in range(2):
                        i = image(u, b, m)
                        nc.gpsimd.tensor_tensor(h[0:TAIL, i, 1, :], h[0:TAIL, i, 1, :], xn[b][0:TAIL, m, 1, :], ALU.add)
                        last = nc.gpsimd.tensor_tensor(h[0:NQ, i, 0, :], h[0:NQ, i, 0, :], S["pb"][0:NQ, :], ALU.add)
                    last.then_inc(keys_added[b], 1)

                pipeline(pool, turns, [(add_keys, 2)])

            @block.scalar
            def _(act):
                norm_s(act)

                def split_x(u, b):
                    act.wait_ge(xn_made[b], u + 1)
                    act.wait_ge(mixed[b], u)
                    for c in range(2):
                        last = nc.scalar.activation(xs[b][0:ROWS[c], 0, :, c, :], xn[b][0:ROWS[c], :, c, :], ACT.Copy)
                    last.then_inc(xn_hi[b], 1)

                def take_turned_x(u, b):
                    act.wait_ge(turned_x[b], u + 1)
                    nc.scalar.activation(xt[b][:, 0, :, :, 0:SEQ], bank_x[0][:, :, :, 0:SEQ], ACT.Copy).then_inc(xt_hi[b], 1)

                def exponentials(u, b):
                    act.wait_ge(max_made[b], u + 1)
                    nc.scalar.activation(pr[b][:], bank_s[:, 0:NK], ACT.Exp, bias=nmx[b][:, 0:1], scale=SCALE,
                                         accum_out=rsum[b][:, 0:1]).then_inc(exp_made[b], 1)

                def scale_o(u, b):
                    act.wait_ge(mixed[b], u + 1)
                    act.wait_ge(sum_inverted[b], u + 1)
                    nc.scalar.activation(o[b][:], bank_o[:, 0:D], ACT.Copy, scale=rinv[b][:, 0:1]).then_inc(o_made[b], 1)

                pipeline(act, turns, [(exponentials, 1), (scale_o, 0), (split_x, 2), (take_turned_x, 2)])

            @block.tensor
            def _(pe):
                t = nc.tensor

                def turn_x(u, b):
                    pe.wait_ge(xn_split[b], u + 1)
                    pe.wait_ge(xt_hi[1 - b], u + b)
                    pe.wait_ge(xt_lo[1 - b], u + b)
                    for part in range(2):
                        for m in range(2):
                            for c in range(2):
                                for k in range(2):
                                    last = t.transpose(bank_x[part][:, k, m, COLS[c]], xs[b][0:ROWS[c], part, m, c, k * KH:(k + 1) * KH],
                                                       S["ident16"][0:ROWS[c], 0:ROWS[c]])
                    last.then_inc(turned_x[b], 1)

                def score(u, b):
                    pe.wait_ge(xt_hi[b], u + 1)
                    pe.wait_ge(xt_lo[b], u + 1)
                    pe.wait_ge(exp_made[1 - b], u + b)
                    for k in range(2):
                        for n, (pa, pb) in enumerate(PARTS):
                            for m in range(2):
                                last = t.matmul(bank_s[m * NQ:(m + 1) * NQ, 0:NK], xt[b][:, pa, k, m, 0:NQ], xt[b][:, pb, k, m, NQ:SEQ],
                                                start=(k == 0 and n == 0), stop=(k == 1 and n == 2))
                    last.then_inc(scored[b], 1)

                def turn_p(u, b):
                    pe.wait_ge(pr_split[b], u + 1)
                    pe.wait_ge(pt_done[1 - b], u + b)
                    for part in range(2):
                        t.transpose(bank_p[0:TAIL, part, P:2 * P], prs[b][:, part, NK1:NK], S["ident16"][:])
                        last = t.transpose(bank_p[NK1:P, part, 0:P], prs[b][:, part, 0:NK1], S["ident16"][:])
                    last.then_inc(turned_p[b], 1)

                def mix(u, b):
                    pe.wait_ge(pt_done[b], u + 1)
                    pe.wait_ge(o_made[1 - b], u + b)
                    for m in range(2):
                        for n, (pa, pb) in enumerate(PARTS):
                            t.matmul(bank_o[m * NQ:(m + 1) * NQ, 0:D], pt[b][0:TAIL, pa, P + m * NQ:P + (m + 1) * NQ],
                                     xs[b][0:TAIL, pb, m, 1, :], start=(n == 0), stop=False)
                        for n, (pa, pb) in enumerate(PARTS):
                            last = t.matmul(bank_o[m * NQ:(m + 1) * NQ, 0:D], pt[b][NK1:P, pa, m * NQ:(m + 1) * NQ],
                                            xs[b][NK1:P, pb, m, 0, :], start=False, stop=(n == 2))
                    last.then_inc(mixed[b], 1)

                def project(u, b):
                    pe.wait_ge(scored[b], 1)
                    pe.wait_ge(o_split[b], u + 1)
                    pe.wait_ge(h_done[1 - b], u + b)
                    for j in range(3):
                        for n, (pa, pb) in enumerate(PARTS):
                            for m in range(2):
                                rows = slice(m * NQ, (m + 1) * NQ)
                                last = t.matmul(bank_r[m][0:NQ, 0:D], os_[b][rows, pa, j:D:3], S["pw"][rows, pb, j, :],
                                                start=(j == 0 and n == 0), stop=(j == 2 and n == 2))
                    last.then_inc(projected[b], 1)

                pipeline(pe, turns, [(score, 1), (mix, 0), (turn_p, 1), (turn_x, 2), (project, 0)])


def mlp_0(nc, S, n_img):
    h, mean, rstd = S["h"], S["mean"], S["rstd"]
    turns = n_img // 4
    PAIR = 2 * SEQ
    with ExitStack() as ctx:
        sb, ps, sem = stage_tools(nc, ctx)
        xn = [sb(f"m_xn{b}", [P, 2, 2, D]) for b in range(2)]
        xt = [sb(f"m_xt{b}", [KH, 2, 2, PAIR], F16) for b in range(2)]
        act_out = [sb(f"m_act{r}", [P, PAIR]) for r in range(2)]
        hid = [sb(f"m_hid{b}", [P, 2, HC, PAIR], F16) for b in range(2)]
        bank_x = [ps(f"m_bank_x{k}", [KH, 512]) for k in range(2)]
        bank_h = [ps(f"m_bank_h{r}", [P, 512]) for r in range(4)]
        bank_y = [ps(f"m_bank_y{m}", [P, 512]) for m in range(2)]
        two = lambda name: [sem(f"m_{name}{b}") for b in range(2)]
        xn_made, turned, xt_hi, xt_split, made_y, h_done, bias_added = (
            two("xn_made"), two("turned"), two("xt_hi"), two("xt_split"), two("made_y"), two("h_done"), two("bias_added"))
        fc_made, gelu_made, hid_hi, hid_split = sem("m_fc_made"), sem("m_gelu_made"), sem("m_hid_hi"), sem("m_hid_split")
        norm_v, norm_s = norm_tables(nc, sb, sem, S, "n1")

        def image(u, b, m):
            return 4 * u + 2 * b + m

        def chunks_before(u, b):
            return (2 * u + b) * HC

        with nc.Block() as block:
            @block.vector
            def _(dve):
                v = nc.vector
                norm_v(dve)

                def normalise(u, b):
                    for m in range(2):
                        i = image(u, b, m)
                        for c in range(2):
                            last = v.tensor_scalar(xn[b][0:ROWS[c], m, c, :], h[0:ROWS[c], i, c, :],
                                                   mean[0:ROWS[c], bass.ds(2 * i + c, 1)], rstd[0:ROWS[c], bass.ds(2 * i + c, 1)],
                                                   ALU.subtract, ALU.mult)
                    last.then_inc(xn_made[b], 1)

                def split_x(u, b):
                    dve.wait_ge(xt_hi[b], u + 1)
                    for k in range(2):
                        last = v.tensor_tensor(xt[b][:, 1, k, :], bank_x[k][:, 0:PAIR], xt[b][:, 0, k, :], ALU.subtract)
                    last.then_inc(xt_split[b], 1)

                def split_hidden(u, b):
                    for f in range(HC):
                        n = chunks_before(u, b) + f + 1
                        dve.wait_ge(gelu_made, n)
                        v.tensor_copy(hid[b][:, 0, f, :], act_out[f % 2][:]).then_inc(hid_hi, 1)
                        dve.wait_ge(hid_hi, n)
                        v.tensor_tensor(hid[b][:, 1, f, :], act_out[f % 2][:], hid[b][:, 0, f, :], ALU.subtract)\
                            .then_inc(hid_split, 1)

                def finish(u, b):
                    dve.wait_ge(made_y[b], u + 1)
                    dve.wait_ge(bias_added[b], u + 1)
                    for m in range(2):
                        i = image(u, b, m)
                        for c in range(2):
                            last = v.tensor_tensor(h[0:ROWS[c], i, c, :], bank_y[m][0:ROWS[c], c * D:(c + 1) * D],
                                                   h[0:ROWS[c], i, c, :], ALU.add)
                    last.then_inc(h_done[b], 1)
                    dve.wait_ge(h_done[b], u + 1)
                    for m in range(2):
                        i = image(u, b, m)
                        for c in range(2):
                            v.bn_stats(S["stats"][0:ROWS[c], 2 * i + c, :], h[0:ROWS[c], i, c, :])

                pipeline(dve, turns, [(normalise, 2), (split_hidden, 1), (split_x, 2), (finish, 0)])

            @block.gpsimd
            def _(pool):
                def add_bias(u, b):
                    pool.wait_ge(xn_made[b], u + 1)
                    for m in range(2):
                        i = image(u, b, m)
                        for c in range(2):
                            last = nc.gpsimd.tensor_tensor(h[0:ROWS[c], i, c, :], h[0:ROWS[c], i, c, :],
                                                           S["fp_bias"][0:ROWS[c], :], ALU.add)
                    last.then_inc(bias_added[b], 1)

                pipeline(pool, turns, [(add_bias, 2)])

            @block.scalar
            def _(act):
                norm_s(act)

                def split_x(u, b):
                    act.wait_ge(turned[b], u + 1)
                    for k in range(2):
                        last = nc.scalar.activation(xt[b][:, 0, k, :], bank_x[k][:, 0:PAIR], ACT.Copy)
                    last.then_inc(xt_hi[b], 1)

                def gelu(u, b):
                    for f in range(HC):
                        n = chunks_before(u, b) + f
                        act.wait_ge(fc_made, n + 1)
                        if f >= 2:
                            act.wait_ge(hid_split, n - 1)
                        else:
                            act.wait_ge(hid_split, chunks_before(u, b))
                        nc.scalar.activation(act_out[f % 2][:], bank_h[(2 * b + f) % 4][:, 0:PAIR], ACT.Gelu_apprx_tanh,
                                             bias=S["fc_bias"][:, f:f + 1]).then_inc(gelu_made, 1)

                pipeline(act, turns, [(gelu, 1), (split_x, 2)])

            @block.tensor
            def _(pe):
                t = nc.tensor

                def turn_x(u, b):
                    pe.wait_ge(xn_made[b], u + 1)
                    pe.wait_ge(xt_split[1 - b], u + b)
                    for k in range(2):
                        for m in range(2):
                            for c in range(2):
                                last = t.transpose(bank_x[k][:, m * SEQ + c * P:m * SEQ + c * P + ROWS[c]],
                                                   xn[b][0:ROWS[c], m, c, k * KH:(k + 1) * KH],
                                                   S["ident"][0:ROWS[c], 0:ROWS[c]])
                    last.then_inc(turned[b], 1)

                def up(u, b):
                    pe.wait_ge(xt_split[b], u + 1)
                    for f in range(HC):
                        n = chunks_before(u, b) + f
                        if f >= 4:
                            pe.wait_ge(gelu_made, n - 3)
                        else:
                            pe.wait_ge(gelu_made, chunks_before(u, b))
                        for k in range(2):
                            for j, (pa, pb) in enumerate(PARTS):
                                last = t.matmul(bank_h[(2 * b + f) % 4][:, 0:PAIR], S["fc"][:, pa, k, f * P:(f + 1) * P],
                                                xt[b][:, pb, k, :], start=(k == 0 and j == 0), stop=(k == 1 and j == 2))
                        last.then_inc(fc_made, 1)

                def down(u, b):
                    pe.wait_ge(hid_split, chunks_before(u, b) + HC)
                    pe.wait_ge(h_done[1 - b], u + b)
                    for m in range(2):
                        for c in range(2):
                            lo = m * SEQ + c * P
                            for f in range(HC):
                                for j, (pa, pb) in enumerate(PARTS):
                                    last = t.matmul(bank_y[m][0:ROWS[c], c * D:(c + 1) * D], hid[b][:, pa, f, lo:lo + ROWS[c]],
                                                    S["fp"][:, pb, f, :], start=(f == 0 and j == 0), stop=(f == HC - 1 and j == 2))
                    last.then_inc(made_y[b], 1)

                pipeline(pe, turns, [(up, 1), (turn_x, 2), (down, 0)])


def attention_1(nc, S, n_img):
    h, mean, rstd = S["h"], S["mean"], S["rstd"]
    SCALE = float(DH) ** -0.5
    VH = 2 * D
    SLOT = {"x'": 0, "q0'": 1, "q1'": 2, "q2'": 3, "q3'": 0, "q4'": 1, "q5'": 2, "v0'": 3, "v1'": 0, "w": 1, "v2'": 2, "v3'": 3}
    for p in range(PAIRS):
        SLOT[f"s{p}"] = 2 * (p % 2)
    ORDER = ("s0 s1 s2 t0 s3 t1 m0 s4 t2 m1 s5 t3 m2 x' q0' q1' t4 m3 q2' q3' t5 m4 q4' q5' m5 v0' v1' w v2' v3'").split()
    PROLOGUE = [s for s in ORDER if s.endswith("'")]

    def turns_of(order):
        used, before = [0] * 4, {}
        for s in order:
            if s in SLOT:
                k = SLOT[s]
                before[s] = used[k]
                used[k] += 1
                if s[0] == "s":
                    assert used[k + 1] == used[k] - 1 or True
                    before[s + "b"] = used[k + 1]
                    used[k + 1] += 1
        return before, used

    BEFORE_P, USED_P = turns_of(PROLOGUE)
    BEFORE, USED = turns_of(ORDER)
    BEFORE_L, _ = turns_of([s for s in ORDER if not s.endswith("'")])

    with ExitStack() as ctx:
        sb, ps, sem = stage_tools(nc, ctx)
        xn = sb("b_xn", [P, 2, D])
        xt = sb("b_xt", [KH, 2, 2, SEQ], F16)
        qk = sb("b_qk", [P, 2, PAIRS, 2, SEQ], F16)
        val = sb("b_val", [P, 2, 2, HID], F16)
        pr = [sb(f"b_pr{r}", [P, 2, 2, SEQ]) for r in range(2)]
        pt = [sb(f"b_pt{r}", [P, 2, 2, 2 * SEQ], F16) for r in range(2)]
        ot = sb("b_ot", [P, 2, PAIRS, SEQ], F16)
        mx = [sb(f"b_mx{r}", [P, 2, 2]) for r in range(2)]
        nmx = [sb(f"b_nmx{r}", [P, 2, 2]) for r in range(2)]
        rsum = [sb(f"b_rsum{r}", [P, 2, 2]) for r in range(2)]
        rinv = [sb(f"b_rinv{r}", [P, 2, 2]) for r in range(2)]
        slots = ps("b_slots", [P, 4, 512])
        bank_t = ps("b_bank_t", [P, 2, 512])
        bank_o = ps("b_bank_o", [P, 2, 512])
        ready = [sem(f"b_ready{k}") for k in range(4)]
        freed = [sem(f"b_freed{k}") for k in range(4)]
        (xn_made, xt_hi, xt_split, qk_hi, qk_split, v_hi, v_split, max_found, max_made, inverted, prob_made,
         t_ready, pt_hi, pt_split, o_ready, ot_hi, ot_split, h_updated, filled) = map(sem, (
             "b_xn_made", "b_xt_hi", "b_xt_split", "b_qk_hi", "b_qk_split", "b_v_hi", "b_v_split", "b_max_found",
             "b_max_made", "b_inverted", "b_prob_made", "b_t_ready", "b_pt_hi", "b_pt_split", "b_o_ready", "b_ot_hi",
             "b_ot_split", "b_h_updated", "b_filled"))
        norm_v, norm_s = norm_tables(nc, sb, sem, S, "n2")

        def uses(s, i, mode):
            if mode == "prologue":
                return BEFORE_P[s]
            before = BEFORE if mode == "body" else BEFORE_L
            k = SLOT[s[:2]] + 1 if s.endswith("b") else SLOT[s]
            return i * USED[k] + USED_P[k] + before[s]

        def run(eng, order, step):
            for s in order:
                if s.endswith("'"):
                    step(s, -1, "prologue")
            if n_img > 1:
                for s in order:
                    step(s, 0, "body")
            if n_img > 2:
                with eng.Fori(1, n_img - 1) as i:
                    for s in order:
                        step(s, i, "body")
            for s in order:
                if not s.endswith("'"):
                    step(s, n_img - 1, "last")

        with nc.Block() as block:
            @block.tensor
            def _(pe):
                t = nc.tensor

                def step(s, i, mode):
                    kind, n = s[0], (int(s[1]) if s[1:2].isdigit() else 0)
                    nxt = i + 1
                    if s in SLOT:
                        k = SLOT[s]
                        before = uses(s, i, mode)
                        pe.wait_ge(freed[k], before)
                        out = slots[:, k, :]
                    if kind == "x":
                        pe.wait_ge(xn_made, nxt + 1)
                        for hf in range(2):
                            for c in range(2):
                                last = t.transpose(out[0:KH, hf * SEQ + c * P:hf * SEQ + c * P + ROWS[c]],
                                                   xn[0:ROWS[c], c, hf * KH:(hf + 1) * KH], S["ident"][0:ROWS[c], 0:ROWS[c]])
                        last.then_inc(ready[k], 1)
                    elif kind == "q":
                        pe.wait_ge(xt_split, nxt + 1)
                        for g in range(2):
                            for hf in range(2):
                                for j, (pa, pb) in enumerate(PARTS):
                                    last = t.matmul(out[:, g * SEQ:(g + 1) * SEQ], S["wqkv"][:, pa, hf, (2 * n + g) * P:(2 * n + g + 1) * P],
                                                    xt[:, pb, hf, :], start=(hf == 0 and j == 0), stop=(hf == 1 and j == 2))
                        last.then_inc(ready[k], 1)
                    elif kind == "v":
                        pe.wait_ge(xt_split, nxt + 1)
                        c, col = n // 2, 2 * HID + (n % 2) * VH
                        for hf in range(2):
                            for j, (pa, pb) in enumerate(PARTS):
                                last = t.matmul(out[0:ROWS[c], 0:VH], xt[:, pa, hf, COLS[c]], S["wqkv"][:, pb, hf, col:col + VH],
                                                start=(hf == 0 and j == 0), stop=(hf == 1 and j == 2))
                        last.then_inc(ready[k], 1)
                    elif kind == "s":
                        pe.wait_ge(freed[k + 1], uses(s + "b", i, mode))
                        pe.wait_ge(qk_split, PAIRS * i + n + 1)
                        for c in range(2):
                            for j, (pa, pb) in enumerate(PARTS):
                                for e in range(2):
                                    rows = slice(e * DH, (e + 1) * DH)
                                    last = t.matmul(slots[0:ROWS[c], k + e, c * SEQ:(c + 1) * SEQ], qk[rows, pa, n, 0, COLS[c]],
                                                    qk[rows, pb, n, 1, :], start=(j == 0), stop=(j == 2))
                                    if c == 1 and j == 2:
                                        last.then_inc(ready[k + e], 1)
                    elif kind == "t":
                        pe.wait_ge(prob_made, PAIRS * i + n + 1)
                        pe.wait_ge(pt_split, PAIRS * i + n)
                        for kc in range(2):
                            for e in range(2):
                                for c in range(2):
                                    last = t.transpose(bank_t[0:ROWS[kc], kc, e * SEQ + c * P:e * SEQ + c * P + ROWS[c]],
                                                       pr[n % 2][0:ROWS[c], c, e, COLS[kc]], S["ident"][0:ROWS[c], 0:ROWS[c]])
                        last.then_inc(t_ready, 1)
                    elif kind == "m":
                        pe.wait_ge(pt_split, PAIRS * i + n + 1)
                        if n == 0:
                            pe.wait_ge(v_split, 4 * (i + 1))
                            pe.wait_ge(ot_split, 3 * i)
                        if n == 4:
                            pe.wait_ge(ot_split, 3 * i + 1)
                        b, lo = (n // 2) % 2, (n % 2) * SEQ
                        for kc in range(2):
                            for j, (pa, pb) in enumerate(PARTS):
                                for e in range(2):
                                    head = 2 * n + e
                                    last = t.matmul(bank_o[e * DH:(e + 1) * DH, b, lo:lo + SEQ],
                                                    val[0:ROWS[kc], pa, kc, head * DH:(head + 1) * DH],
                                                    pt[n % 2][0:ROWS[kc], pb, kc, e * SEQ:(e + 1) * SEQ],
                                                    start=(kc == 0 and j == 0), stop=(kc == 1 and j == 2))
                        if n % 2 == 1:
                            last.then_inc(o_ready, 1)
                    elif kind == "w":
                        pe.wait_ge(ot_split, 3 * (i + 1))
                        for c in range(2):
                            for f in range(PAIRS):
                                for j, (pa, pb) in enumerate(PARTS):
                                    last = t.matmul(out[0:ROWS[c], c * D:(c + 1) * D], ot[:, pa, f, COLS[c]], S["wo"][:, pb, f, :],
                                                    start=(f == 0 and j == 0), stop=(f == PAIRS - 1 and j == 2))
                        last.then_inc(ready[k], 1)

                run(pe, ORDER, step)

            ACT_ORDER = "e0 e1 t0 e2 t1 e3 t2 e4 o0 t3 e5 x' q0' q1' t4 o1 q2' q3' t5 q4' q5' o2 v0' v1' v2' v3'".split()

            @block.scalar
            def _(act):
                norm_s(act)

                def copy(dst, src):
                    return nc.scalar.activation(dst, src, ACT.Copy)

                def step(s, i, mode):
                    kind, n = s[0], (int(s[1]) if s[1:2].isdigit() else 0)
                    if s in SLOT:
                        k = SLOT[s]
                        act.wait_ge(ready[k], uses(s, i, mode) + 1)
                    if kind == "x":
                        copy(xt[:, 0], slots[0:KH, k, 0:2 * SEQ].rearrange("p (h t) -> p h t", h=2)).then_inc(xt_hi, 1)
                    elif kind == "q":
                        copy(qk[:, 0, n], slots[:, k, 0:2 * SEQ].rearrange("p (g t) -> p g t", g=2)).then_inc(qk_hi, 1)
                    elif kind == "v":
                        c, col = n // 2, (n % 2) * VH
                        copy(val[0:ROWS[c], 0, c, col:col + VH], slots[0:ROWS[c], k, 0:VH]).then_inc(v_hi, 1)
                    elif kind == "e":
                        act.wait_ge(max_made, PAIRS * i + n + 1)
                        k = SLOT[f"s{n}"]
                        for e in range(2):
                            for c in range(2):
                                last = nc.scalar.activation(pr[n % 2][0:ROWS[c], c, e, :], slots[0:ROWS[c], k + e, c * SEQ:(c + 1) * SEQ],
                                                            ACT.Exp, bias=nmx[n % 2][0:ROWS[c], c, e:e + 1], scale=SCALE,
                                                            accum_out=rsum[n % 2][0:ROWS[c], c, e:e + 1])
                            last.then_inc(freed[k + e], 1)
                    elif kind == "t":
                        act.wait_ge(t_ready, PAIRS * i + n + 1)
                        for kc in range(2):
                            last = copy(pt[n % 2][0:ROWS[kc], 0, kc, :], bank_t[0:ROWS[kc], kc, 0:2 * SEQ])
                        last.then_inc(pt_hi, 1)
                    elif kind == "o":
                        act.wait_ge(o_ready, 3 * i + n + 1)
                        copy(ot[:, 0, 2 * n:2 * n + 2, :], bank_o[:, n % 2, 0:2 * SEQ].rearrange("p (f t) -> p f t", f=2)).then_inc(ot_hi, 1)

                run(act, ACT_ORDER, step)

            DVE_ORDER = "m0 m1 n' r0 m2 r1 t0 m3 r2 t1 m4 r3 t2 m5 r4 o0 t3 r5 x' q0' q1' t4 o1 q2' q3' t5 q4' q5' o2 v0' v1' w v2' v3'".split()

            @block.vector
            def _(dve):
                v = nc.vector
                norm_v(dve)
                for r in range(2):
                    v.memset(mx[r][:], 0.0)
                    last = v.memset(rsum[r][:], 1.0)
                last.then_inc(filled, 1)
                dve.wait_ge(filled, 1)

                def low(dst, src, high):
                    return v.tensor_tensor(dst, src, high, ALU.subtract)

                def step(s, i, mode):
                    kind, n = s[0], (int(s[1]) if s[1:2].isdigit() else 0)
                    nxt = i + 1
                    if s in SLOT:
                        k = SLOT[s]
                        turn = uses(s, i, mode) + 1
                    if kind == "n":
                        for c in range(2):
                            last = v.tensor_scalar(xn[0:ROWS[c], c, :], h[0:ROWS[c], nxt, c, :], mean[0:ROWS[c], bass.ds(2 * nxt + c, 1)],
                                                   rstd[0:ROWS[c], bass.ds(2 * nxt + c, 1)], ALU.subtract, ALU.mult)
                        last.then_inc(xn_made, 1)
                    elif kind == "x":
                        dve.wait_ge(xt_hi, nxt + 1)
                        low(xt[:, 1], slots[0:KH, k, 0:2 * SEQ].rearrange("p (h t) -> p h t", h=2), xt[:, 0]).then_inc(xt_split, 1)
                        dve.wait_ge(xt_split, nxt + 1)
                        dve.sem_inc(freed[k], 1)
                    elif kind == "q":
                        dve.wait_ge(qk_hi, PAIRS * nxt + n + 1)
                        low(qk[:, 1, n], slots[:, k, 0:2 * SEQ].rearrange("p (g t) -> p g t", g=2), qk[:, 0, n]).then_inc(qk_split, 1)
                        dve.wait_ge(qk_split, PAIRS * nxt + n + 1)
                        dve.sem_inc(freed[k], 1)
                    elif kind == "v":
                        dve.wait_ge(v_hi, 4 * nxt + n + 1)
                        c, col = n // 2, (n % 2) * VH
                        low(val[0:ROWS[c], 1, c, col:col + VH], slots[0:ROWS[c], k, 0:VH], val[0:ROWS[c], 0, c, col:col + VH]).then_inc(v_split, 1)
                        dve.wait_ge(v_split, 4 * nxt + n + 1)
                        dve.sem_inc(freed[k], 1)
                    elif kind == "m":
                        k = SLOT[f"s{n}"]
                        dve.wait_ge(ready[k], uses(f"s{n}", i, mode) + 1)
                        dve.wait_ge(ready[k + 1], uses(f"s{n}b", i, mode) + 1)
                        for c in range(2):
                            last = v.reduce_max(mx[n % 2][0:ROWS[c], c, :], slots[0:ROWS[c], k:k + 2, c * SEQ:(c + 1) * SEQ], AX.X)
                        last.then_inc(max_found, 1)
                        dve.wait_ge(max_found, PAIRS * i + n + 1)
                        v.tensor_scalar(nmx[n % 2][:], mx[n % 2][:], -SCALE, None, ALU.mult).then_inc(max_made, 1)
                    elif kind == "r":
                        k = SLOT[f"s{n}"]
                        dve.wait_ge(freed[k + 1], uses(f"s{n}b", i, mode) + 1)
                        v.reciprocal(rinv[n % 2][:], rsum[n % 2][:]).then_inc(inverted, 1)
                    elif kind == "t":
                        dve.wait_ge(pt_hi, PAIRS * i + n + 1)
                        for kc in range(2):
                            last = low(pt[n % 2][0:ROWS[kc], 1, kc, :], bank_t[0:ROWS[kc], kc, 0:2 * SEQ], pt[n % 2][0:ROWS[kc], 0, kc, :])
                        last.then_inc(pt_split, 1)
                    elif kind == "o":
                        dve.wait_ge(ot_hi, 3 * i + n + 1)
                        low(ot[:, 1, 2 * n:2 * n + 2, :], bank_o[:, n % 2, 0:2 * SEQ].rearrange("p (f t) -> p f t", f=2),
                            ot[:, 0, 2 * n:2 * n + 2, :]).then_inc(ot_split, 1)
                    elif kind == "w":
                        dve.wait_ge(ready[k], turn)
                        for c in range(2):
                            last = v.tensor_tensor(h[0:ROWS[c], i, c, :], slots[0:ROWS[c], k, c * D:(c + 1) * D], h[0:ROWS[c], i, c, :], ALU.add)
                        last.then_inc(freed[k], 1)
                        dve.wait_ge(freed[k], turn)
                        for c in range(2):
                            v.bn_stats(S["stats"][0:ROWS[c], 2 * i + c, :], h[0:ROWS[c], i, c, :])

                run(dve, DVE_ORDER, step)

            @block.gpsimd
            def _(pool):
                def step(s, i, mode):
                    n = int(s[1])
                    pool.wait_ge(inverted, PAIRS * i + n + 1)
                    for c in range(2):
                        p = pr[n % 2][0:ROWS[c], c]
                        inv = rinv[n % 2][0:ROWS[c], c, :].unsqueeze(2).to_broadcast([ROWS[c], 2, SEQ])
                        last = nc.gpsimd.tensor_tensor(p, p, inv, ALU.mult)
                    last.then_inc(prob_made, 1)

                run(pool, [f"p{n}" for n in range(PAIRS)], step)


def mlp_1(nc, S, out, n_img):
    h, mean, rstd = S["h"], S["mean"], S["rstd"]
    turns = n_img // 4
    PAIR = 2 * SEQ
    SP = SEQ + 1
    with ExitStack() as ctx:
        sb, ps, sem = stage_tools(nc, ctx)
        xn = [sb(f"z_xn{b}", [P, 2, 2, D]) for b in range(2)]
        xq = [sb(f"z_xq{b}", [P, 2, 2, D], BF16) for b in range(2)]
        xt = [sb(f"z_xt{b}", [KH, 2, 2, SEQ], BF16) for b in range(2)]
        act_out = [sb(f"z_act{r}", [P, PAIR]) for r in range(3)]
        hid = [sb(f"z_hid{b}", [P, HC, PAIR], BF16) for b in range(2)]
        res = [sb(f"z_res{b}", [P, 2, 2, D]) for b in range(2)]
        bank_x = ps("z_bank_x", [KH, 2, 2, 256], BF16)
        bank_h = [ps(f"z_bank_h{r}", [P, 512]) for r in range(4)]
        bank_y = [ps(f"z_bank_y{m}", [P, 512]) for m in range(2)]
        two = lambda name: [sem(f"z_{name}{b}") for b in range(2)]
        xn_made, clipped, quantised, turned, xt_done, bias_added, made_y, scaled, h_done, stored = (
            two("xn_made"), two("clipped"), two("quantised"), two("turned"), two("xt_done"), two("bias_added"),
            two("made_y"), two("scaled"), two("h_done"), two("stored"))
        fc_made, gelu_made, over_a2, bounded, hid_done = map(sem, ("z_fc_made", "z_gelu_made", "z_over_a2", "z_bounded", "z_hid_done"))
        norm_v, norm_s = norm_tables(nc, sb, sem, S, "n3")

        def image(u, b, m):
            return 4 * u + 2 * b + m

        def chunks_before(u, b):
            return (2 * u + b) * HC

        with nc.Block() as block:
            @block.vector
            def _(dve):
                v = nc.vector
                norm_v(dve)

                def quantise(u, b):
                    dve.wait_ge(quantised[b], u)
                    for m in range(2):
                        i = image(u, b, m)
                        for c in range(2):
                            last = v.tensor_scalar(xn[b][0:ROWS[c], m, c, :], h[0:ROWS[c], i, c, :],
                                                   mean[0:ROWS[c], bass.ds(2 * i + c, 1)], rstd[0:ROWS[c], bass.ds(2 * i + c, 1)],
                                                   ALU.subtract, ALU.mult)
                    last.then_inc(xn_made[b], 1)
                    dve.wait_ge(xn_made[b], u + 1)
                    for c in range(2):
                        x = xn[b][0:ROWS[c], :, c, :]
                        last = v.tensor_scalar(x, x, S["inv_a1"][0:ROWS[c], 0:1], 7.0, ALU.mult, ALU.min)
                    last.then_inc(clipped[b], 1)
                    dve.wait_ge(clipped[b], 2 * u + 1)
                    for c in range(2):
                        x = xn[b][0:ROWS[c], :, c, :]
                        last = v.tensor_scalar(x, x, -8.0, ROUND, ALU.max, ALU.add)
                    last.then_inc(clipped[b], 1)
                    dve.wait_ge(clipped[b], 2 * u + 2)
                    for c in range(2):
                        last = v.tensor_scalar(xq[b][0:ROWS[c], :, c, :], xn[b][0:ROWS[c], :, c, :], ROUND, None, ALU.subtract)
                    last.then_inc(quantised[b], 1)

                def take_turned_x(u, b):
                    dve.wait_ge(turned[b], u + 1)
                    v.tensor_copy(xt[b][:], bank_x[:, :, :, 0:SEQ]).then_inc(xt_done[b], 1)

                def quantise_hidden(u, b):
                    for f in range(HC):
                        n = chunks_before(u, b) + f + 1
                        a = act_out[f % 3][:]
                        dve.wait_ge(gelu_made, n)
                        v.tensor_scalar(a, a, S["inv_a2"][:, 0:1], S["q_hi"][:, 0:1], ALU.mult, ALU.min).then_inc(over_a2, 1)
                        dve.wait_ge(over_a2, n)
                        v.tensor_scalar(a, a, S["q_lo"][:, 0:1], ROUND, ALU.max, ALU.add).then_inc(bounded, 1)

                def finish(u, b):
                    dve.wait_ge(made_y[b], u + 1)
                    dve.wait_ge(bias_added[b], u + 1)
                    dve.wait_ge(stored[b], 32 * u)
                    for m in range(2):
                        for c in range(2):
                            last = v.tensor_tensor(res[b][0:ROWS[c], m, c, :], bank_y[m][0:ROWS[c], c * D:(c + 1) * D],
                                                   S["q2_scale"][0:ROWS[c], :], ALU.mult)
                    last.then_inc(scaled[b], 1)

                pipeline(dve, turns, [(quantise, 2), (quantise_hidden, 1), (take_turned_x, 2), (finish, 0)])

            @block.gpsimd
            def _(pool):
                def add_bias(u, b):
                    pool.wait_ge(xn_made[b], u + 1)
                    for m in range(2):
                        i = image(u, b, m)
                        for c in range(2):
                            last = nc.gpsimd.tensor_tensor(h[0:ROWS[c], i, c, :], h[0:ROWS[c], i, c, :],
                                                           S["q2_bias"][0:ROWS[c], :], ALU.add)
                    last.then_inc(bias_added[b], 1)

                def add_stream(u, b):
                    pool.wait_ge(scaled[b], u + 1)
                    pool.wait_ge(bias_added[b], u + 1)
                    for m in range(2):
                        i = image(u, b, m)
                        for c in range(2):
                            r = res[b][0:ROWS[c], m, c, :]
                            last = nc.gpsimd.tensor_tensor(r, h[0:ROWS[c], i, c, :], r, ALU.add)
                    last.then_inc(h_done[b], 1)

                pipeline(pool, turns, [(add_bias, 2), (add_stream, 0)])

            @block.sync
            def _(sp):
                def store(u, b):
                    sp.wait_ge(h_done[b], u + 1)
                    i = image(u, b, 0)
                    for c in range(2):
                        sp.dma_start(out[bass.ds(i, 2), c * P:c * P + ROWS[c], :].rearrange("m t d -> t m d"),
                                     res[b][0:ROWS[c], :, c, :]).then_inc(stored[b], 16)

                pipeline(sp, turns, [(store, 0)])
                for b in range(2):
                    sp.wait_ge(stored[b], 32 * turns)

            @block.scalar
            def _(act):
                norm_s(act)

                def gelu(u, b):
                    for f in range(HC + 1):
                        n = chunks_before(u, b) + f
                        if f < HC:
                            act.wait_ge(fc_made, n + 1)
                            act.wait_ge(hid_done, n - 2 if f >= 3 else chunks_before(u, b))
                            nc.scalar.activation(act_out[f % 3][:], bank_h[(2 * b + f) % 4][:, 0:PAIR], ACT.Gelu,
                                                 bias=S["q1_bias"][:, f:f + 1], scale=S["q1_scale"][:, f:f + 1]).then_inc(gelu_made, 1)
                        if f >= 1:
                            act.wait_ge(bounded, n)
                            nc.scalar.activation(hid[b][:, f - 1, :], act_out[(f - 1) % 3][:], ACT.Copy, bias=-ROUND).then_inc(hid_done, 1)

                pipeline(act, turns, [(gelu, 1)])

            @block.tensor
            def _(pe):
                t = nc.tensor

                def turn_x(u, b):
                    pe.wait_ge(quantised[b], u + 1)
                    pe.wait_ge(xt_done[1 - b], u + b)
                    for k in range(2):
                        for m in range(2):
                            for c in range(2):
                                last = t.transpose(bank_x[:, k, m, COLS[c]], xq[b][0:ROWS[c], m, c, k * KH:(k + 1) * KH],
                                                   S["ident_b"][0:ROWS[c], 0:ROWS[c]])
                    last.then_inc(turned[b], 1)

                def up(u, b):
                    pe.wait_ge(xt_done[b], u + 1)
                    for f in range(HC):
                        n = chunks_before(u, b) + f
                        pe.wait_ge(gelu_made, n - 3 if f >= 4 else chunks_before(u, b))
                        for k in range(2):
                            last = t.matmul(bank_h[(2 * b + f) % 4][:, 0:PAIR], S["q1"][:, k, f * P:(f + 1) * P],
                                            xt[b][:, k].rearrange("p m t -> p (m t)"), start=(k == 0), stop=(k == 1))
                        last.then_inc(fc_made, 1)

                def down(u, b):
                    pe.wait_ge(hid_done, chunks_before(u, b) + HC)
                    pe.wait_ge(scaled[1 - b], u + b)
                    for m in range(2):
                        for c in range(2):
                            lo = m * SEQ + c * P
                            for f in range(HC):
                                last = t.matmul(bank_y[m][0:ROWS[c], c * D:(c + 1) * D], hid[b][:, f, lo:lo + ROWS[c]],
                                                S["q2"][:, f, :], start=(f == 0), stop=(f == HC - 1))
                    last.then_inc(made_y[b], 1)

                pipeline(pe, turns, [(up, 1), (turn_x, 2), (down, 0)])


def laid_out(inp):
    import numpy as np

    f = {k: np.asarray(v) for k, v in inp.items()}
    x = f["x"]
    n = x.shape[0]
    npat = 14

    def halves(a):
        return a.reshape(2, KH, -1).transpose(1, 0, 2)

    def chunks(a):
        return a.reshape(HC, P, -1).transpose(1, 0, 2)

    def rows(a, m=P):
        return np.broadcast_to(a.reshape(1, -1), (m, a.size))

    qkv = f["L1_attn_W_qkv"].reshape(D, DH, 3, HEADS).transpose(0, 2, 3, 1)
    qk = qkv[:, 0:2].reshape(D, 2, PAIRS, P).transpose(0, 2, 1, 3).reshape(D, 2 * HID)
    cls_bias = np.concatenate([f["L0_tok_class_token"].reshape(1, D), rows(f["L0_tok_b"], SEQ - 1)], axis=0)
    below = np.array([[[float(k * KH + p < e) for e in EMBED_CHOICES] for k in range(2)] for p in range(KH)], np.float32)
    return {
        "x": x.reshape(n, 3, npat, 2, 8, npat, 16).transpose(0, 4, 6, 1, 3, 2, 5).reshape(n, P, PATCH_K, npat * npat),
        "tok_w": f["L0_tok_W"].reshape(D, 3, 2, 8, 16).transpose(3, 4, 1, 2, 0).reshape(P, PATCH_K, D),
        "pos": f["L0_tok_pos_embed"],
        "cls_bias": cls_bias,
        "proj_w": f["L0_attn_proj_w"].T.reshape(3, NQ, D).transpose(1, 0, 2),
        "proj_b": rows(f["L0_attn_proj_b"]),
        "fc": halves(f["L0_ffn_w_fc"].T),
        "fc_b": f["L0_ffn_b_fc"].reshape(1, HID),
        "fproj": halves(f["L0_ffn_w_proj"]),
        "fproj_b": rows(f["L0_ffn_b_proj"]),
        "alpha_e": rows(f["L0_ffn_alpha_e"]),
        "alpha_r": rows(f["L0_ffn_alpha_r"]),
        "below": below,
        "identity": np.eye(P, dtype=np.float32),
        "wqkv": halves(np.concatenate([qk, qkv[:, 2].reshape(D, HID)], axis=1)),
        "wo": chunks(f["L1_attn_W_0"]),
        "w1": halves(f["L1_ffn_w1"].T),
        "alpha_w1_rows": rows(f["L1_ffn_alpha_w1"], KH),
        "alpha_w1_cols": f["L1_ffn_alpha_w1"].reshape(HC, P).T,
        "b1": f["L1_ffn_b1"].reshape(HC, P).T,
        "w2": chunks(f["L1_ffn_w2"].T),
        "alpha_w2": rows(f["L1_ffn_alpha_w2"]),
        "b2": rows(f["L1_ffn_b2"]),
        "alpha_a1": rows(f["L1_ffn_alpha_a1"]),
        "alpha_a2": rows(f["L1_ffn_alpha_a2"]),
    }


def kernel(**inputs):
    import numpy as np
    import concourse.bacc as bacc
    from concourse.bass_utils import run_bass_kernel_spmd

    nc = bacc.Bacc("TRN2", target_bir_lowering=False, num_devices=1)
    arrays, A = {}, {}
    for name, a in laid_out(inputs).items():
        a = np.ascontiguousarray(a)
        arrays[f"in_{name}"] = a
        A[name] = nc.dram_tensor(f"in_{name}", a.shape, mybir.dt.from_np(a.dtype), kind="ExternalInput").ap()
    n = A["x"].shape[0]
    out = nc.dram_tensor("out_0", (n, SEQ, D), F32, kind="ExternalOutput").ap()
    build(nc, A, out)
    r = run_bass_kernel_spmd(nc, [arrays], core_ids=[0])
    return r.results[0]["out_0"]
```

```python
from contextlib import ExitStack

import concourse.bass as bass
from concourse import mybir

F32 = mybir.dt.float32
F16 = mybir.dt.float16
BF16 = mybir.dt.bfloat16
ALU = mybir.AluOpType
ACT = mybir.ActivationFunctionType
AX = mybir.AxisListType

P = 128
D = 192
KH = 96
LO = D - P
PATCH_K = 6
SEQ = 197
TAIL = SEQ - P
ROWS = (P, TAIL)
COLS = (slice(0, P), slice(P, SEQ))
HID = 768
HC = HID // P
HEADS = 12
DH = 64
PAIRS = HEADS // 2
NQ = 64
NK = SEQ - NQ
NK1 = P - NQ
EPS = 1e-5
ROUND = 12582912.0
PARTS = ((0, 0), (0, 1), (1, 0))
EMBED_CHOICES = (96, 144, 192)
RATIO_CHOICES = (2, 3, 4)


def build(nc, A, out):
    n_img = A["x"].shape[0]
    with ExitStack() as ctx:
        def sb(name, shape, dt=F32):
            return ctx.enter_context(nc.sbuf_tensor(name, shape, dt))

        S = {
            "h": sb("h", [P, n_img, 2, D]),
            "stats": sb("stats", [P, n_img * 2, 6]),
            "mean": sb("mean", [P, n_img * 2]),
            "rstd": sb("rstd", [P, n_img * 2]),
            "ident": sb("ident", [P, P]),
            "ident16": sb("ident16", [P, P], F16),
            "ident_b": sb("ident_b", [P, P], BF16),
            "pw": sb("pw", [P, 2, 3, D], F16),
            "pb": sb("pb", [P, D]),
            "fc": sb("fc", [P, 2, 2, HID], F16),
            "fc_bias": sb("fc_bias", [P, HC]),
            "fp": sb("fp", [P, 2, HC, D], F16),
            "fp_bias": sb("fp_bias", [P, D]),
            "wqkv": sb("wqkv", [P, 2, 2, 3 * HID], F16),
            "wo": sb("wo", [P, 2, HC, D], F16),
            "q1": sb("q1", [KH, 2, HID], BF16),
            "q2": sb("q2", [P, HC, D], BF16),
            "q1_scale": sb("q1_scale", [P, HC]),
            "q1_bias": sb("q1_bias", [P, HC]),
            "q2_scale": sb("q2_scale", [P, D]),
            "q2_bias": sb("q2_bias", [P, D]),
            "inv_a1": sb("inv_a1", [P, 1]),
            "inv_a2": sb("inv_a2", [P, 1]),
            "q_lo": sb("q_lo", [P, 1]),
            "q_hi": sb("q_hi", [P, 1]),
        }
        with ExitStack() as embedding:
            S["posb"] = embedding.enter_context(nc.sbuf_tensor("posb", [P, 2, D], F32))
            S["tok_w"] = embedding.enter_context(nc.sbuf_tensor("tok_w", [P, PATCH_K, D], F32))
            prepare_weights(nc, A, S)
            embed_patches(nc, A, S, n_img)
        attention_0(nc, S, n_img)
        mlp_0(nc, S, n_img)
        attention_1(nc, S, n_img)
        mlp_1(nc, S, out, n_img)


def stacked_products(w, x):
    high, both, low = (x[:, k] for k in range(3))
    return [(w[:, 0, 0], high), (w[:, 0, 0], low), (w[:, 1, 0], high), (w[:, 0, 1], both), (w[:, 1, 1], both)]


def normalise_twice(nc, S, dst, j, rows, i, c):
    h, scalars = S["h"], [S[k][0:rows, bass.ds(j, 1)] for k in ("mean", "rstd")]
    nc.vector.tensor_scalar(dst[:, 0:P], h[0:rows, i, c, 0:P], *scalars, ALU.subtract, ALU.mult)
    twice = h[0:rows, i, c, P:D].unsqueeze(1).to_broadcast([rows, 2, LO])
    return nc.vector.tensor_scalar(dst[:, P:2 * P].rearrange("p (a b) -> p a b", a=2), twice, *scalars, ALU.subtract, ALU.mult)


def stage_tools(nc, ctx):
    def sb(name, shape, dt=F32):
        return ctx.enter_context(nc.sbuf_tensor(name, shape, dt))

    def ps(name, shape, dt=F32):
        return ctx.enter_context(nc.psum_tensor(name, shape, dt))

    def sem(name):
        return ctx.enter_context(nc.semaphore(name))

    return sb, ps, sem


def prepare_weights(nc, A, S):
    with ExitStack() as ctx:
        sb, ps, sem = stage_tools(nc, ctx)
        free, used = S["h"][:].rearrange("p i c d -> p (i c d)"), [0]
        if free.shape[1] < 18432:
            free = sb("raw_weights", [P, 18432])[:]

        def raw(rows, *shape):
            n = 1
            for k in shape:
                n *= k
            a = free[0:rows, used[0]:used[0] + n]
            used[0] += n
            if len(shape) == 2:
                a = a.rearrange("p (a b) -> p a b", a=shape[0])
            return a

        r_qkv = raw(P, 2, 3 * HID)
        r_wo = raw(P, HC, D)
        r_pw = raw(P, 3, D)
        r_fc = raw(P, 2, HID)
        r_fp = raw(P, 2, HID)
        r_w1 = raw(KH, 2, HID)
        r_w2 = raw(P, HC, D)
        a_w1 = raw(KH, HID)
        a_w1c = raw(P, HC)
        a_w2 = raw(P, D)
        a_a1 = raw(P, D)
        a_a2 = raw(P, HID)
        g = raw(P, 3, HID)
        coef = raw(P, 2, HID)
        alpha = sb("alpha", [P, 6])
        below = sb("below", [P, 2, 3])
        c0b = sb("c0b", [1, HID])
        bfc = sb("bfc", [1, HID])
        one = sb("one", [1, 1])
        c1b = sb("c1b", [P, D])
        ar_sum = sb("ar_sum", [P, 1])
        cls_b = sb("cls_b", [P, 2, D])
        m1 = sb("m1", [P, 1])
        m2 = sb("m2", [P, 1])
        bank_t = [ps(f"w_turned{n}", [P, 2, D]) for n in range(3)]
        bank_b = ps("w_bias", [P, HC])
        loaded, qkv_loaded, zeroed, step, act_hi, turned, bias_col, masked = map(
            sem, ("w_loaded", "w_qkv_loaded", "w_zeroed", "w_step", "w_act_hi", "w_turned_done", "w_bias_col", "w_masked"))

        loads = [
            (alpha[:, 0:3], A["alpha_e"]), (alpha[:, 3:6], A["alpha_r"]), (below[:], A["below"]),
            (r_fc[:], A["fc"]), (r_fp[:], A["fproj"]), (bfc[:], A["fc_b"]), (S["fp_bias"][:], A["fproj_b"]),
            (r_w1[:], A["w1"]), (a_w1[:], A["alpha_w1_rows"]), (a_w1c[:], A["alpha_w1_cols"]),
            (r_w2[:], A["w2"]), (a_w2[:], A["alpha_w2"]), (a_a1[:], A["alpha_a1"]), (a_a2[:], A["alpha_a2"]),
            (S["q1_bias"][:], A["b1"]), (S["q2_bias"][:], A["b2"]),
            (S["ident"][:], A["identity"]), (S["posb"][:, 0, :], A["pos"][0:P, :]), (S["posb"][0:TAIL, 1, :], A["pos"][P:SEQ, :]),
            (cls_b[:, 0, :], A["cls_bias"][0:P, :]), (cls_b[0:TAIL, 1, :], A["cls_bias"][P:SEQ, :]),
            (S["tok_w"][:], A["tok_w"]), (S["pb"][:], A["proj_b"]),
            (r_pw[0:NQ], A["proj_w"]), (r_pw[NQ:P], A["proj_w"]), (r_wo[:], A["wo"]),
        ]
        with nc.Block() as block:
            @block.sync
            def _(sp):
                for dst, src in loads:
                    sp.dma_start(dst, src).then_inc(loaded, 16)
                sp.dma_start(r_qkv[:], A["wqkv"]).then_inc(qkv_loaded, 16)

            @block.scalar
            def _(act):
                act.wait_ge(loaded, 16 * len(loads))
                nc.scalar.activation(S["wo"][:, 0], r_wo[:], ACT.Copy).then_inc(act_hi, 1)
                nc.scalar.activation(S["pw"][:, 0], r_pw[:], ACT.Copy).then_inc(act_hi, 1)
                nc.scalar.activation(S["ident16"][:], S["ident"][:], ACT.Copy).then_inc(act_hi, 1)
                nc.scalar.activation(S["ident_b"][:], S["ident"][:], ACT.Copy).then_inc(act_hi, 1)
                act.wait_ge(qkv_loaded, 16)
                nc.scalar.activation(S["wqkv"][:, 0], r_qkv[:], ACT.Copy).then_inc(act_hi, 1)

            @block.vector
            def _(dve):
                done = [0]

                def then(ins):
                    done[0] += 1
                    ins.then_inc(step, 1)
                    dve.wait_ge(step, done[0])

                v = nc.vector
                v.memset(g[:], 0.0)
                v.memset(c1b[:], 0.0)
                then(v.memset(one[:], 1.0))
                dve.wait_ge(loaded, 16 * len(loads))
                for i, e in enumerate(EMBED_CHOICES):
                    for j, r in enumerate(RATIO_CHOICES):
                        then(v.tensor_scalar(g[:, i, 0:r * e], g[:, i, 0:r * e], alpha[:, 3 + j:4 + j], None, ALU.add))
                    then(v.tensor_scalar(g[:, i, :], g[:, i, :], alpha[:, i:i + 1], None, ALU.mult))
                for k in range(2):
                    then(v.tensor_scalar(coef[:, k, :], g[:, 0, :], below[:, k, 0:1], None, ALU.mult))
                    for i in (1, 2):
                        then(v.scalar_tensor_tensor(out=coef[:, k, :], in0=g[:, i, :], scalar=below[:, k, i:i + 1],
                                                    in1=coef[:, k, :], op0=ALU.mult, op1=ALU.add))
                then(v.tensor_tensor(c0b[:], g[0:1, 0, :], g[0:1, 1, :], ALU.add))
                then(v.tensor_tensor(c0b[:], c0b[:], g[0:1, 2, :], ALU.add))
                then(v.tensor_tensor(bfc[:], bfc[:], c0b[:], ALU.mult))
                then(v.tensor_tensor(r_fc[:], r_fc[:], coef[:], ALU.mult))
                v.tensor_tensor(r_fp[:], r_fp[:], coef[:], ALU.mult).then_inc(masked, 1)
                then(v.tensor_copy(S["fc"][:, 0], r_fc[:]))
                then(v.tensor_tensor(S["fc"][:, 1], r_fc[:], S["fc"][:, 0], ALU.subtract))
                then(v.reduce_sum(ar_sum[:], alpha[:, 3:6], AX.X))
                for i, e in enumerate(EMBED_CHOICES):
                    then(v.tensor_scalar(c1b[:, 0:e], c1b[:, 0:e], alpha[:, i:i + 1], None, ALU.add))
                then(v.tensor_scalar(c1b[:], c1b[:], ar_sum[:, 0:1], None, ALU.mult))
                then(v.tensor_tensor(S["fp_bias"][:], S["fp_bias"][:], c1b[:], ALU.mult))
                then(v.tensor_tensor(S["posb"][:, 0, :], S["posb"][:, 0, :], cls_b[:, 0, :], ALU.add))
                then(v.tensor_tensor(S["posb"][0:TAIL, 1, :], S["posb"][0:TAIL, 1, :], cls_b[0:TAIL, 1, :], ALU.add))
                then(v.reduce_sum(m1[:], a_a1[:], AX.X))
                then(v.tensor_scalar(m1[:], m1[:], 1.0 / D, None, ALU.mult))
                then(v.reciprocal(S["inv_a1"][:], m1[:]))
                then(v.reduce_sum(m2[:], a_a2[:], AX.X))
                then(v.tensor_scalar(m2[:], m2[:], 1.0 / HID, None, ALU.mult))
                then(v.reciprocal(S["inv_a2"][:], m2[:]))
                then(v.tensor_scalar(S["q_lo"][:], S["inv_a2"][:], -10.0, -8.0, ALU.mult, ALU.max))
                then(v.tensor_scalar(S["q_hi"][:], S["inv_a2"][:], 10.0, 7.0, ALU.mult, ALU.min))
                then(v.tensor_scalar(S["q1_scale"][:], a_w1c[:], m1[:, 0:1], None, ALU.mult))
                then(v.tensor_scalar(S["q2_scale"][:], a_w2[:], m2[:, 0:1], None, ALU.mult))
                then(v.reciprocal(a_w1[:], a_w1[:]))
                then(v.reciprocal(a_w2[:], a_w2[:]))
                for k in range(2):
                    then(v.tensor_tensor(r_w1[:, k], r_w1[:, k], a_w1[:], ALU.mult))
                for k in range(HC):
                    then(v.tensor_tensor(r_w2[:, k], r_w2[:, k], a_w2[:], ALU.mult))
                for r, q in ((r_w1, S["q1"]), (r_w2, S["q2"])):
                    then(v.tensor_scalar(r[:], r[:], -8.0, 7.0, ALU.max, ALU.min))
                    then(v.tensor_scalar(q[:], r[:], ROUND, -ROUND, ALU.add, ALU.add))
                dve.wait_ge(turned, 1)
                for n in range(3):
                    hi, lo = (S["fp"][:, part, 2 * n:2 * n + 2, :] for part in range(2))
                    then(v.tensor_copy(hi, bank_t[n][:]))
                    then(v.tensor_tensor(lo, bank_t[n][:], hi, ALU.subtract))
                dve.wait_ge(bias_col, 1)
                then(v.tensor_copy(S["fc_bias"][:], bank_b[:]))
                dve.wait_ge(act_hi, 5)
                v.tensor_tensor(S["wo"][:, 1], r_wo[:], S["wo"][:, 0], ALU.subtract)
                v.tensor_tensor(S["pw"][:, 1], r_pw[:], S["pw"][:, 0], ALU.subtract)
                v.tensor_tensor(S["wqkv"][:, 1], r_qkv[:], S["wqkv"][:, 0], ALU.subtract)

            @block.tensor
            def _(pe):
                pe.wait_ge(masked, 1)
                for n in range(3):
                    for f in range(2):
                        hidden = slice((2 * n + f) * P, (2 * n + f + 1) * P)
                        nc.tensor.transpose(bank_t[n][:, f, 0:P], r_fp[:, 0, hidden], S["ident"][:])
                        last = nc.tensor.transpose(bank_t[n][:, f, P:D], r_fp[0:LO, 1, hidden], S["ident"][0:LO, 0:LO])
                last.then_inc(turned, 1)
                for f in range(HC):
                    last = nc.tensor.matmul(bank_b[:, f:f + 1], bfc[:, f * P:(f + 1) * P], one[:], start=True, stop=True)
                last.then_inc(bias_col, 1)


def embed_patches(nc, A, S, n_img):
    h, BUF = S["h"], 4
    with ExitStack() as ctx:
        sb, ps, sem = stage_tools(nc, ctx)
        patches = [sb(f"patches{b}", [P, PATCH_K, SEQ]) for b in range(BUF)]
        tokens = [ps(f"tokens{b}", [P, 512]) for b in range(BUF)]
        zeroed, h_written = sem("t_zeroed"), sem("t_h_written")
        loaded = [sem(f"t_loaded{b}") for b in range(BUF)]
        made = [sem(f"t_made{b}") for b in range(BUF)]
        taken = [sem(f"t_taken{b}") for b in range(BUF)]

        def rounds(eng, fn):
            fn(0)
            if n_img > BUF:
                with eng.Fori(1, n_img // BUF) as g:
                    fn(g)

        with nc.Block() as block:
            @block.sync
            def _(sp):
                def load(g):
                    for b in range(BUF):
                        sp.wait_ge(made[b], g)
                        sp.dma_start(patches[b][:, :, 1:SEQ], A["x"][g * BUF + b]).then_inc(loaded[b], 16)

                rounds(sp, load)

            @block.gpsimd
            def _(pool):
                for b in range(BUF):
                    last = nc.gpsimd.memset(patches[b][:, :, 0:1], 0.0)
                last.then_inc(zeroed, 1)

            @block.tensor
            def _(pe):
                pe.wait_ge(zeroed, 1)
                def multiply(g):
                    for b in range(BUF):
                        pe.wait_ge(loaded[b], 16 * (g + 1))
                        pe.wait_ge(taken[b], g)
                        for c in range(2):
                            for k in range(PATCH_K):
                                last = nc.tensor.matmul(tokens[b][0:ROWS[c], c * D:(c + 1) * D], patches[b][:, k, COLS[c]],
                                                        S["tok_w"][:, k, :], start=(k == 0), stop=(k == PATCH_K - 1))
                        last.then_inc(made[b], 1)

                rounds(pe, multiply)

            @block.vector
            def _(dve):
                nc.vector.memset(S["stats"][:], 0.0)

                def add_position(g):
                    for b in range(BUF):
                        i = g * BUF + b
                        dve.wait_ge(made[b], g + 1)
                        for c in range(2):
                            last = nc.vector.tensor_tensor(h[0:ROWS[c], i, c, :], tokens[b][0:ROWS[c], c * D:(c + 1) * D],
                                                           S["posb"][0:ROWS[c], c, :], ALU.add)
                        last.then_inc(taken[b], 1)
                        dve.wait_ge(taken[b], g + 1)
                        for c in range(2):
                            nc.vector.bn_stats(S["stats"][0:ROWS[c], 2 * i + c, :], h[0:ROWS[c], i, c, :])

                rounds(dve, add_position)


def norm_tables(nc, sb, sem, S, tag):
    n = S["mean"].shape[1]
    tmp = [sb(f"{tag}_tmp{k}", [P, n]) for k in range(3)]
    step, var_ready, root_ready = sem(f"{tag}_step"), sem(f"{tag}_var_ready"), sem(f"{tag}_root_ready")
    st = S["stats"]
    mean, rstd = S["mean"], S["rstd"]
    half = D / 2

    def vector(dve):
        done = [0]

        def then(ins):
            done[0] += 1
            ins.then_inc(step, 1)
            dve.wait_ge(step, done[0])

        v = nc.vector
        then(v.tensor_tensor(mean[:], st[:, :, 1], st[:, :, 4], ALU.add))
        then(v.tensor_scalar(mean[:], mean[:], 0.5, None, ALU.mult))
        then(v.tensor_tensor(tmp[0][:], st[:, :, 1], st[:, :, 4], ALU.subtract))
        then(v.scalar_tensor_tensor(out=tmp[0][:], in0=tmp[0][:], scalar=half / 2, in1=tmp[0][:], op0=ALU.mult, op1=ALU.mult))
        then(v.tensor_tensor(tmp[1][:], st[:, :, 2], st[:, :, 5], ALU.add))
        then(v.tensor_tensor(tmp[0][:], tmp[0][:], tmp[1][:], ALU.add))
        v.tensor_scalar(tmp[0][:], tmp[0][:], 1.0 / D, EPS, ALU.mult, ALU.add).then_inc(var_ready, 1)
        dve.wait_ge(root_ready, 1)
        then(v.reciprocal(rstd[:], tmp[1][:]))
        then(v.tensor_tensor(tmp[2][:], rstd[:], rstd[:], ALU.mult))
        then(v.tensor_tensor(tmp[2][:], tmp[2][:], tmp[0][:], ALU.mult))
        then(v.tensor_scalar(tmp[2][:], tmp[2][:], -0.5, 1.5, ALU.mult, ALU.add))
        then(v.tensor_tensor(rstd[:], rstd[:], tmp[2][:], ALU.mult))

    def scalar(act):
        act.wait_ge(var_ready, 1)
        nc.scalar.activation(tmp[1][:], tmp[0][:], ACT.Sqrt).then_inc(root_ready, 1)

    return vector, scalar


def pipeline(eng, turns, order):
    pairs = 2 * turns

    def peeled(t):
        for fn, ahead in order:
            if 0 <= t + ahead < pairs:
                fn((t + ahead) // 2, (t + ahead) % 2)

    for t in range(-2, 2 if turns > 1 else 0):
        peeled(t)
    if turns > 2:
        with eng.Fori(1, turns - 1) as u:
            for b in range(2):
                for fn, ahead in order:
                    fn(u + (b + ahead) // 2, (b + ahead) % 2)
    for t in range(pairs - 2, pairs + 1):
        peeled(t)


def attention_0(nc, S, n_img):
    h, mean, rstd = S["h"], S["mean"], S["rstd"]
    turns = n_img // 4
    SP = SEQ + 1
    SCALE = float(16) ** -0.5
    with ExitStack() as ctx:
        sb, ps, sem = stage_tools(nc, ctx)
        xn = [sb(f"xn{b}", [P, 2, 2, D]) for b in range(2)]
        xs = [sb(f"xs{b}", [P, 2, 2, 2, D], F16) for b in range(2)]
        xt = [sb(f"xt{b}", [KH, 2, 2, 2, SP], F16) for b in range(2)]
        pr = [sb(f"pr{b}", [P, NK]) for b in range(2)]
        prs = [sb(f"prs{b}", [P, 2, NK], F16) for b in range(2)]
        pt = [sb(f"pt{b}", [P, 2, 2 * P], F16) for b in range(2)]
        o = [sb(f"o{b}", [P, D]) for b in range(2)]
        os_ = [sb(f"os{b}", [P, 2, D], F16) for b in range(2)]
        mx = [sb(f"mx{b}", [P, 1]) for b in range(2)]
        nmx = [sb(f"nmx{b}", [P, 1]) for b in range(2)]
        rsum = [sb(f"rsum{b}", [P, 1]) for b in range(2)]
        rinv = [sb(f"rinv{b}", [P, 1]) for b in range(2)]
        bank_x = [ps(f"bank_x{p}", [KH, 2, 2, 256], F16) for p in range(2)]
        bank_s = ps("bank_s", [P, 512])
        bank_p = ps("bank_p", [P, 2, 512], F16)
        bank_o = ps("bank_o", [P, 512])
        bank_r = [ps(f"bank_r{m}", [P, 512]) for m in range(2)]
        two = lambda name: [sem(f"a_{name}{b}") for b in range(2)]
        xn_made, xn_hi, xn_split = two("xn_made"), two("xn_hi"), two("xn_split")
        turned_x, xt_hi, xt_lo = two("turned_x"), two("xt_hi"), two("xt_lo")
        keys_added, upper_added, scored, max_found, max_made, exp_made = two("keys_added"), two("upper_added"), two("scored"), two("max_found"), two("max_made"), two("exp_made")
        sum_inverted, pr_hi, pr_split = two("sum_inverted"), two("pr_hi"), two("pr_split")
        turned_p, pt_done = two("turned_p"), two("pt_done")
        mixed, o_made, o_hi, o_split = two("mixed"), two("o_made"), two("o_hi"), two("o_split")
        projected, h_done = two("projected"), two("h_done")
        norm_done = sem("a_norm_done")
        norm_v, norm_s = norm_tables(nc, sb, sem, S, "n0")

        def image(u, b, m):
            return 4 * u + 2 * b + m

        with nc.Block() as block:
            @block.vector
            def _(dve):
                v = nc.vector
                norm_v(dve)

                def normalise(u, b):
                    dve.wait_ge(keys_added[b], u)
                    for m in range(2):
                        i = image(u, b, m)
                        for c in range(2):
                            last = v.tensor_scalar(xn[b][0:ROWS[c], m, c, :], h[0:ROWS[c], i, c, :],
                                                   mean[0:ROWS[c], bass.ds(2 * i + c, 1)], rstd[0:ROWS[c], bass.ds(2 * i + c, 1)],
                                                   ALU.subtract, ALU.mult)
                    last.then_inc(xn_made[b], 1)

                def split_x(u, b):
                    dve.wait_ge(xn_hi[b], u + 1)
                    for c in range(2):
                        last = v.tensor_tensor(xs[b][0:ROWS[c], 1, :, c, :], xn[b][0:ROWS[c], :, c, :],
                                               xs[b][0:ROWS[c], 0, :, c, :], ALU.subtract)
                    last.then_inc(xn_split[b], 1)

                def take_turned_x(u, b):
                    dve.wait_ge(turned_x[b], u + 1)
                    v.tensor_copy(xt[b][:, 1, :, :, 0:SEQ], bank_x[1][:, :, :, 0:SEQ]).then_inc(xt_lo[b], 1)

                def maximum(u, b):
                    dve.wait_ge(scored[b], u + 1)
                    v.reduce_max(mx[b][:], bank_s[:, 0:NK], AX.X).then_inc(max_found[b], 1)
                    dve.wait_ge(max_found[b], u + 1)
                    v.tensor_scalar(nmx[b][:], mx[b][:], -SCALE, None, ALU.mult).then_inc(max_made[b], 1)

                def split_probabilities(u, b):
                    dve.wait_ge(exp_made[b], u + 1)
                    v.reciprocal(rinv[b][:], rsum[b][:]).then_inc(sum_inverted[b], 1)
                    v.tensor_copy(prs[b][:, 0, :], pr[b][:]).then_inc(pr_hi[b], 1)
                    dve.wait_ge(pr_hi[b], u + 1)
                    v.tensor_tensor(prs[b][:, 1, :], pr[b][:], prs[b][:, 0, :], ALU.subtract).then_inc(pr_split[b], 1)

                def take_turned_p(u, b):
                    dve.wait_ge(turned_p[b], u + 1)
                    v.tensor_copy(pt[b][NK1:P, :, 0:P], bank_p[NK1:P, :, 0:P])
                    v.tensor_copy(pt[b][0:TAIL, :, P:2 * P], bank_p[0:TAIL, :, P:2 * P]).then_inc(pt_done[b], 1)

                def split_o(u, b):
                    dve.wait_ge(o_made[b], u + 1)
                    v.tensor_copy(os_[b][:, 0, :], o[b][:]).then_inc(o_hi[b], 1)
                    dve.wait_ge(o_hi[b], u + 1)
                    v.tensor_tensor(os_[b][:, 1, :], o[b][:], os_[b][:, 0, :], ALU.subtract).then_inc(o_split[b], 1)

                def finish(u, b):
                    dve.wait_ge(projected[b], u + 1)
                    dve.wait_ge(keys_added[b], u + 1)
                    for m in range(2):
                        i = image(u, b, m)
                        last = v.tensor_tensor(h[0:NQ, i, 0, :], bank_r[m][0:NQ, 0:D], h[0:NQ, i, 0, :], ALU.add)
                    last.then_inc(h_done[b], 1)
                    dve.wait_ge(h_done[b], u + 1)
                    for m in range(2):
                        i = image(u, b, m)
                        for c in range(2):
                            v.bn_stats(S["stats"][0:ROWS[c], 2 * i + c, :], h[0:ROWS[c], i, c, :])

                pipeline(dve, turns, [(normalise, 2), (maximum, 1), (finish, -1), (split_x, 2), (split_o, 0),
                                      (split_probabilities, 1), (take_turned_x, 2), (take_turned_p, 1)])

            @block.gpsimd
            def _(pool):
                def add_keys(u, b):
                    pool.wait_ge(xn_made[b], u + 1)
                    pool.wait_ge(keys_added[1 - b], u + b)
                    for m in range(2):
                        i = image(u, b, m)
                        last = nc.gpsimd.tensor_tensor(h[NK1:P, i, 0, :], h[NK1:P, i, 0, :], xn[b][NK1:P, m, 0, :], ALU.add)
                    last.then_inc(upper_added[b], 1)
                    pool.wait_ge(upper_added[b], u + 1)
                    for m in range(2):
                        i = image(u, b, m)
                        nc.gpsimd.tensor_tensor(h[0:TAIL, i, 1, :], h[0:TAIL, i, 1, :], xn[b][0:TAIL, m, 1, :], ALU.add)
                        last = nc.gpsimd.tensor_tensor(h[0:NQ, i, 0, :], h[0:NQ, i, 0, :], S["pb"][0:NQ, :], ALU.add)
                    last.then_inc(keys_added[b], 1)

                pipeline(pool, turns, [(add_keys, 2)])

            @block.scalar
            def _(act):
                norm_s(act)

                def split_x(u, b):
                    act.wait_ge(xn_made[b], u + 1)
                    act.wait_ge(mixed[b], u)
                    for c in range(2):
                        last = nc.scalar.activation(xs[b][0:ROWS[c], 0, :, c, :], xn[b][0:ROWS[c], :, c, :], ACT.Copy)
                    last.then_inc(xn_hi[b], 1)

                def take_turned_x(u, b):
                    act.wait_ge(turned_x[b], u + 1)
                    nc.scalar.activation(xt[b][:, 0, :, :, 0:SEQ], bank_x[0][:, :, :, 0:SEQ], ACT.Copy).then_inc(xt_hi[b], 1)

                def exponentials(u, b):
                    act.wait_ge(max_made[b], u + 1)
                    nc.scalar.activation(pr[b][:], bank_s[:, 0:NK], ACT.Exp, bias=nmx[b][:, 0:1], scale=SCALE,
                                         accum_out=rsum[b][:, 0:1]).then_inc(exp_made[b], 1)

                def scale_o(u, b):
                    act.wait_ge(mixed[b], u + 1)
                    act.wait_ge(sum_inverted[b], u + 1)
                    nc.scalar.activation(o[b][:], bank_o[:, 0:D], ACT.Copy, scale=rinv[b][:, 0:1]).then_inc(o_made[b], 1)

                pipeline(act, turns, [(split_x, 2), (exponentials, 1), (scale_o, 0), (take_turned_x, 2)])

            @block.tensor
            def _(pe):
                t = nc.tensor

                def turn_x(u, b):
                    pe.wait_ge(xn_split[b], u + 1)
                    pe.wait_ge(xt_hi[1 - b], u + b)
                    pe.wait_ge(xt_lo[1 - b], u + b)
                    for part in range(2):
                        for m in range(2):
                            for c in range(2):
                                for k in range(2):
                                    last = t.transpose(bank_x[part][:, k, m, COLS[c]], xs[b][0:ROWS[c], part, m, c, k * KH:(k + 1) * KH],
                                                       S["ident16"][0:ROWS[c], 0:ROWS[c]])
                    last.then_inc(turned_x[b], 1)

                def score(u, b):
                    pe.wait_ge(xt_hi[b], u + 1)
                    pe.wait_ge(xt_lo[b], u + 1)
                    pe.wait_ge(exp_made[1 - b], u + b)
                    for k in range(2):
                        for n, (pa, pb) in enumerate(PARTS):
                            for m in range(2):
                                last = t.matmul(bank_s[m * NQ:(m + 1) * NQ, 0:NK], xt[b][:, pa, k, m, 0:NQ], xt[b][:, pb, k, m, NQ:SEQ],
                                                start=(k == 0 and n == 0), stop=(k == 1 and n == 2))
                    last.then_inc(scored[b], 1)

                def turn_p(u, b):
                    pe.wait_ge(pr_split[b], u + 1)
                    pe.wait_ge(pt_done[1 - b], u + b)
                    for part in range(2):
                        t.transpose(bank_p[0:TAIL, part, P:2 * P], prs[b][:, part, NK1:NK], S["ident16"][:])
                        last = t.transpose(bank_p[NK1:P, part, 0:P], prs[b][:, part, 0:NK1], S["ident16"][:])
                    last.then_inc(turned_p[b], 1)

                def mix(u, b):
                    pe.wait_ge(pt_done[b], u + 1)
                    pe.wait_ge(o_made[1 - b], u + b)
                    for m in range(2):
                        for n, (pa, pb) in enumerate(PARTS):
                            t.matmul(bank_o[m * NQ:(m + 1) * NQ, 0:D], pt[b][0:TAIL, pa, P + m * NQ:P + (m + 1) * NQ],
                                     xs[b][0:TAIL, pb, m, 1, :], start=(n == 0), stop=False)
                        for n, (pa, pb) in enumerate(PARTS):
                            last = t.matmul(bank_o[m * NQ:(m + 1) * NQ, 0:D], pt[b][NK1:P, pa, m * NQ:(m + 1) * NQ],
                                            xs[b][NK1:P, pb, m, 0, :], start=False, stop=(n == 2))
                    last.then_inc(mixed[b], 1)

                def project(u, b):
                    pe.wait_ge(scored[b], 1)
                    pe.wait_ge(o_split[b], u + 1)
                    pe.wait_ge(h_done[1 - b], u + b)
                    for j in range(3):
                        for n, (pa, pb) in enumerate(PARTS):
                            for m in range(2):
                                rows = slice(m * NQ, (m + 1) * NQ)
                                last = t.matmul(bank_r[m][0:NQ, 0:D], os_[b][rows, pa, j:D:3], S["pw"][rows, pb, j, :],
                                                start=(j == 0 and n == 0), stop=(j == 2 and n == 2))
                    last.then_inc(projected[b], 1)

                pipeline(pe, turns, [(score, 1), (mix, 0), (turn_x, 2), (turn_p, 1), (project, 0)])


def mlp_0(nc, S, n_img):
    h, mean, rstd = S["h"], S["mean"], S["rstd"]
    turns = n_img // 4
    PAIR = 2 * SEQ
    with ExitStack() as ctx:
        sb, ps, sem = stage_tools(nc, ctx)
        xn = [sb(f"m_xn{b}", [P, 2, 2, 2 * P]) for b in range(2)]
        xt = [sb(f"m_xt{b}", [P, 3, PAIR], F16) for b in range(2)]
        act_out = [sb(f"m_act{r}", [P, PAIR]) for r in range(2)]
        hid = [sb(f"m_hid{b}", [P, 2, HC, PAIR], F16) for b in range(2)]
        bank_x = [ps(f"m_bank_x{k}", [P, 512]) for k in range(2)]
        bank_h = [ps(f"m_bank_h{r}", [P, 512]) for r in range(4)]
        bank_y = [ps(f"m_bank_y{m}", [P, 512]) for m in range(2)]
        two = lambda name: [sem(f"m_{name}{b}") for b in range(2)]
        xn_made, turned, xt_hi, xt_split, made_y, h_done, bias_added = (
            two("xn_made"), two("turned"), two("xt_hi"), two("xt_split"), two("made_y"), two("h_done"), two("bias_added"))
        fc_made, gelu_made, hid_hi, hid_split = sem("m_fc_made"), sem("m_gelu_made"), sem("m_hid_hi"), sem("m_hid_split")
        norm_v, norm_s = norm_tables(nc, sb, sem, S, "n1")

        def image(u, b, m):
            return 4 * u + 2 * b + m

        def chunks_before(u, b):
            return (2 * u + b) * HC

        with nc.Block() as block:
            @block.vector
            def _(dve):
                v = nc.vector
                norm_v(dve)

                def normalise(u, b):
                    for m in range(2):
                        i = image(u, b, m)
                        for c in range(2):
                            last = normalise_twice(nc, S, xn[b][0:ROWS[c], m, c], 2 * i + c, ROWS[c], i, c)
                    last.then_inc(xn_made[b], 1)

                def split_x(u, b):
                    dve.wait_ge(xt_hi[b], u + 1)
                    v.tensor_tensor(xt[b][:, 2, :], bank_x[0][:, 0:PAIR], xt[b][:, 0, :], ALU.subtract)
                    last = v.tensor_tensor(xt[b][LO:P, 1, :], bank_x[1][LO:P, 0:PAIR], xt[b][LO:P, 1, :], ALU.subtract)
                    last.then_inc(xt_split[b], 1)

                def split_hidden(u, b):
                    for f in range(HC):
                        n = chunks_before(u, b) + f + 1
                        dve.wait_ge(gelu_made, n)
                        v.tensor_copy(hid[b][:, 0, f, :], act_out[f % 2][:]).then_inc(hid_hi, 1)
                        dve.wait_ge(hid_hi, n)
                        v.tensor_tensor(hid[b][:, 1, f, :], act_out[f % 2][:], hid[b][:, 0, f, :], ALU.subtract)\
                            .then_inc(hid_split, 1)

                def finish(u, b):
                    dve.wait_ge(made_y[b], u + 1)
                    dve.wait_ge(bias_added[b], u + 1)
                    for m in range(2):
                        i = image(u, b, m)
                        for c in range(2):
                            last = v.tensor_tensor(h[0:ROWS[c], i, c, :], bank_y[m][0:ROWS[c], c * D:(c + 1) * D],
                                                   h[0:ROWS[c], i, c, :], ALU.add)
                    last.then_inc(h_done[b], 1)
                    dve.wait_ge(h_done[b], u + 1)
                    for m in range(2):
                        i = image(u, b, m)
                        for c in range(2):
                            v.bn_stats(S["stats"][0:ROWS[c], 2 * i + c, :], h[0:ROWS[c], i, c, :])

                pipeline(dve, turns, [(normalise, 2), (split_hidden, 1), (split_x, 2), (finish, 0)])

            @block.gpsimd
            def _(pool):
                def add_bias(u, b):
                    pool.wait_ge(xn_made[b], u + 1)
                    for m in range(2):
                        i = image(u, b, m)
                        for c in range(2):
                            last = nc.gpsimd.tensor_tensor(h[0:ROWS[c], i, c, :], h[0:ROWS[c], i, c, :],
                                                           S["fp_bias"][0:ROWS[c], :], ALU.add)
                    last.then_inc(bias_added[b], 1)

                pipeline(pool, turns, [(add_bias, 2)])

            @block.scalar
            def _(act):
                norm_s(act)

                def split_x(u, b):
                    act.wait_ge(turned[b], u + 1)
                    for k in range(2):
                        last = nc.scalar.activation(xt[b][:, k, :], bank_x[k][:, 0:PAIR], ACT.Copy)
                    last.then_inc(xt_hi[b], 1)

                def gelu(u, b):
                    for f in range(HC):
                        n = chunks_before(u, b) + f
                        act.wait_ge(fc_made, n + 1)
                        if f >= 2:
                            act.wait_ge(hid_split, n - 1)
                        else:
                            act.wait_ge(hid_split, chunks_before(u, b))
                        nc.scalar.activation(act_out[f % 2][:], bank_h[(2 * b + f) % 4][:, 0:PAIR], ACT.Gelu_apprx_tanh,
                                             bias=S["fc_bias"][:, f:f + 1]).then_inc(gelu_made, 1)

                pipeline(act, turns, [(gelu, 1), (split_x, 2)])

            @block.tensor
            def _(pe):
                t = nc.tensor

                def turn_x(u, b):
                    pe.wait_ge(xn_made[b], u + 1)
                    pe.wait_ge(xt_split[1 - b], u + b)
                    for m in range(2):
                        for c in range(2):
                            lo, x = m * SEQ + c * P, xn[b][0:ROWS[c], m, c, :]
                            t.transpose(bank_x[0][:, lo:lo + ROWS[c]], x[:, 0:P], S["ident"][0:ROWS[c], 0:ROWS[c]])
                            last = t.transpose(bank_x[1][:, lo:lo + ROWS[c]], x[:, P:2 * P], S["ident"][0:ROWS[c], 0:ROWS[c]])
                    last.then_inc(turned[b], 1)

                def up(u, b):
                    pe.wait_ge(xt_split[b], u + 1)
                    for f in range(HC):
                        n = chunks_before(u, b) + f
                        if f >= 4:
                            pe.wait_ge(gelu_made, n - 3)
                        else:
                            pe.wait_ge(gelu_made, chunks_before(u, b))
                        for j, (w, x) in enumerate(stacked_products(S["fc"], xt[b])):
                            last = t.matmul(bank_h[(2 * b + f) % 4][:, 0:PAIR], w[:, f * P:(f + 1) * P], x,
                                            start=(j == 0), stop=(j == 4))
                        last.then_inc(fc_made, 1)

                def down(u, b):
                    pe.wait_ge(hid_split, chunks_before(u, b) + HC)
                    pe.wait_ge(h_done[1 - b], u + b)
                    for m in range(2):
                        for c in range(2):
                            lo = m * SEQ + c * P
                            for f in range(HC):
                                for j, (pa, pb) in enumerate(PARTS):
                                    last = t.matmul(bank_y[m][0:ROWS[c], c * D:(c + 1) * D], hid[b][:, pa, f, lo:lo + ROWS[c]],
                                                    S["fp"][:, pb, f, :], start=(f == 0 and j == 0), stop=(f == HC - 1 and j == 2))
                    last.then_inc(made_y[b], 1)

                pipeline(pe, turns, [(up, 1), (turn_x, 2), (down, 0)])


def attention_1(nc, S, n_img):
    h = S["h"]
    SCALE = float(DH) ** -0.5
    VH = 2 * D
    PE_ORDER = ("s0 t4^ v3 m3^ x'  s1 t5^ q0' m4^ q1'  s2 t0 q2' m5^ q3'  "
                "s3 t1 q4' m0 w^  s4 t2 q5' m1 v0'  s5 t3 v1' m2 v2'").split()
    ACT_ORDER = ("t4^ v3 e0 x'  o1^ t5^ q0' e1 q1'  t0 q2' e2 q3'  "
                 "o2^ t1 q4' e3  t2 q5' e4 v0'  o0 t3 v1' e5 v2'").split()
    DVE_ORDER = ("m0 t4^ n' r0 v3 x'  m1 o1^ t5^ r1 q0' q1'  m2 t0 r2 q2' q3'  "
                 "m3 o2^ t1 r3 q4' w^  m4 t2 r4 q5' v0'  m5 o0 t3 r5 v1' v2'").split()
    JOB_BANK = {"v3": 2, "x'": 3, "q0'": 2, "q1'": 3, "q2'": 2, "q3'": 3, "q4'": 2, "w^": 3, "q5'": 2, "v0'": 3, "v1'": 2, "v2'": 3}

    MODES = {"before": lambda s: s.endswith("'"), "first": lambda s: not s.endswith("^"), "body": lambda s: True,
             "last": lambda s: not s.endswith("'"), "after": lambda s: s.endswith("^")}

    SHIFT = {"'": 1, "^": -1}

    def jobs(mode, bank, rounds):
        return [(s, rounds + SHIFT.get(s[-1], 0)) for s in PE_ORDER if MODES[mode](s) and JOB_BANK.get(s) == bank]

    def job_before(s, mode):
        modes = list(MODES)
        earlier = {"before": [], "body": ["body"]}.get(mode, modes[:modes.index(mode)][-1:])
        line = [x for m in earlier for x in jobs(m, JOB_BANK[s], -1)] + jobs(mode, JOB_BANK[s], 0)
        me = line.index((s, SHIFT.get(s[-1], 0)))
        return (line[me - 1][0], line[me - 1][1] - line[me][1]) if me else None

    with ExitStack() as ctx:
        sb, ps, sem = stage_tools(nc, ctx)
        xn = sb("b_xn", [P, 2, 2 * P])
        xt = sb("b_xt", [P, 3, SEQ], F16)
        qk = sb("b_qk", [P, 2, 2, PAIRS, SEQ], F16)
        kst = sb("b_kst", [P, 2, PAIRS, SEQ], F16)
        qst = sb("b_qst", [P, 2, 2, PAIRS, SEQ], F16)
        val = [sb(f"b_val{r}", [P, 2, 2, HID], F16) for r in range(2)]
        pr = [sb(f"b_pr{r}", [P, 2, 2, SEQ]) for r in range(3)]
        pt = [sb(f"b_pt{r}", [P, 2, 2, 2 * SEQ], F16) for r in range(2)]
        ot = sb("b_ot", [P, 2, PAIRS, SEQ], F16)
        mx = [sb(f"b_mx{r}", [P, 2, 2]) for r in range(2)]
        nmx = [sb(f"b_nmx{r}", [P, 2, 2]) for r in range(2)]
        rsum = [sb(f"b_rsum{r}", [P, 2, 2]) for r in range(2)]
        rinv = [sb(f"b_rinv{r}", [P, 2, 2]) for r in range(2)]
        banks = ps("b_banks", [P, 4, 512])
        bank_t = ps("b_bank_t", [P, 2, 512])
        bank_o = ps("b_bank_o", [P, 2, 512])
        stacked = [sem(f"b_stacked{a}") for a in range(2)]
        STACK = 16 * 8
        ready = [sem(f"b_ready{e}") for e in range(2)]
        freed = [sem(f"b_freed{e}") for e in range(2)]
        (xn_made, xt_hi, xt_split, qk_hi, qk_split, v_hi, v_split, max_found, max_made, inverted, prob_made,
         t_ready, pt_hi, pt_split, o_ready, ot_hi, ot_split, filled, x_ready, q_ready, v_ready, w_ready, h_updated) = map(sem, (
             "b_xn_made", "b_xt_hi", "b_xt_split", "b_qk_hi", "b_qk_split", "b_v_hi", "b_v_split", "b_max_found",
             "b_max_made", "b_inverted", "b_prob_made", "b_t_ready", "b_pt_hi", "b_pt_split", "b_o_ready", "b_ot_hi",
             "b_ot_split", "b_filled", "b_x_ready", "b_q_ready", "b_v_ready", "b_w_ready", "b_h_updated"))
        norm_v, norm_s = norm_tables(nc, sb, sem, S, "n2")

        def made(s, img):
            kind, n = s[0], (int(s[1]) if s[1:2].isdigit() else 0)
            return {"x": (x_ready, img + 1), "q": (q_ready, PAIRS * img + n + 1), "v": (v_ready, 4 * img + n + 1),
                    "w": (w_ready, img + 1)}[kind]

        def left(s, img):
            kind, n = s[0], (int(s[1]) if s[1:2].isdigit() else 0)
            return {"x": (xt_split, img + 1), "q": (qk_split, PAIRS * img + n + 1), "v": (v_split, 4 * img + n + 1),
                    "w": (h_updated, img + 1)}[kind]

        def run(eng, order, step):
            def rounds(i, mode, parity):
                for s in order:
                    if MODES[mode](s):
                        shift = SHIFT.get(s[-1], 0)
                        n = int(s[1]) if s[1:2].isdigit() else 0
                        step(s, s[0], n, i, i + shift, mode, (parity + shift) % 2)

            rounds(-1, "before", 1)
            rounds(0, "first", 0)
            if n_img > 2:
                with eng.Fori(0, n_img // 2 - 1) as u:
                    rounds(2 * u + 1, "body", 1)
                    rounds(2 * u + 2, "body", 0)
            rounds(n_img - 1, "last", 1)
            rounds(n_img, "after", 0)

        with nc.Block() as block:
            @block.tensor
            def _(pe):
                t = nc.tensor

                def step(s, kind, n, i, img, mode, odd):
                    if s in JOB_BANK:
                        out, before, job_made = banks[:, JOB_BANK[s], :], job_before(s, mode), made(s, img)[0]
                        if before:
                            pe.wait_ge(*left(before[0], img + before[1]))
                    if kind == "x":
                        pe.wait_ge(xn_made, img + 1)
                        for c in range(2):
                            x, one = xn[0:ROWS[c], c, :], S["ident"][0:ROWS[c], 0:ROWS[c]]
                            t.transpose(out[:, c * P:c * P + ROWS[c]], x[:, 0:P], one)
                            last = t.transpose(out[:, SEQ + c * P:SEQ + c * P + ROWS[c]], x[:, P:2 * P], one)
                        last.then_inc(job_made, 1)
                    elif kind == "q":
                        pe.wait_ge(xt_split, img + 1)
                        for g in range(2):
                            for j, (w, x) in enumerate(stacked_products(S["wqkv"], xt)):
                                last = t.matmul(out[:, g * SEQ:(g + 1) * SEQ], w[:, (2 * n + g) * P:(2 * n + g + 1) * P], x,
                                                start=(j == 0), stop=(j == 4))
                        last.then_inc(job_made, 1)
                    elif kind == "v":
                        c, col = n % 2, 2 * HID + (n // 2) * VH
                        for j, (w, x) in enumerate(stacked_products(S["wqkv"], xt)):
                            last = t.matmul(out[0:ROWS[c], 0:VH], x[:, COLS[c]], w[:, col:col + VH], start=(j == 0), stop=(j == 4))
                        last.then_inc(job_made, 1)
                    elif kind == "s":
                        pe.wait_ge(stacked[n // 3], STACK * (img + 1))
                        for e in range(2):
                            pe.wait_ge(freed[e], PAIRS * img + n)
                            for c in range(2):
                                for part in range(2):
                                    last = t.matmul(banks[0:ROWS[c], e, c * SEQ:(c + 1) * SEQ], qst[:, part, e, n, COLS[c]],
                                                    kst[:, e, n, :], start=(part == 0), stop=(part == 1))
                            last.then_inc(ready[e], 1)
                    elif kind == "t":
                        pe.wait_ge(prob_made, PAIRS * img + n + 1)
                        pe.wait_ge(pt_split, PAIRS * img + n)
                        for kc in range(2):
                            for e in range(2):
                                for c in range(2):
                                    last = t.transpose(bank_t[0:ROWS[kc], kc, e * SEQ + c * P:e * SEQ + c * P + ROWS[c]],
                                                       pr[n % 3][0:ROWS[c], c, e, COLS[kc]], S["ident"][0:ROWS[c], 0:ROWS[c]])
                            last.then_inc(t_ready, 1)
                    elif kind == "m":
                        pe.wait_ge(pt_split, PAIRS * img + n + 1)
                        if n in (0, 3):
                            pe.wait_ge(v_split, 4 * img + (2 if n == 0 else 4))
                        if n % 2 == 0 and (mode != "first" or n == 4):
                            pe.wait_ge(ot_split, 3 * img + n // 2 - 1)
                        b, lo = (odd + n // 2) % 2, (n % 2) * SEQ
                        for kc in range(2):
                            for j, (pa, pb) in enumerate(PARTS):
                                for e in range(2):
                                    head = 2 * n + e
                                    last = t.matmul(bank_o[e * DH:(e + 1) * DH, b, lo:lo + SEQ],
                                                    val[odd][0:ROWS[kc], pa, kc, head * DH:(head + 1) * DH],
                                                    pt[n % 2][0:ROWS[kc], pb, kc, e * SEQ:(e + 1) * SEQ],
                                                    start=(kc == 0 and j == 0), stop=(kc == 1 and j == 2))
                        if n % 2 == 1:
                            last.then_inc(o_ready, 1)
                    elif kind == "w":
                        pe.wait_ge(ot_split, 3 * (img + 1))
                        for c in range(2):
                            for f in range(PAIRS):
                                for j, (pa, pb) in enumerate(PARTS):
                                    last = t.matmul(out[0:ROWS[c], c * D:(c + 1) * D], ot[:, pa, f, COLS[c]], S["wo"][:, pb, f, :],
                                                    start=(f == 0 and j == 0), stop=(f == PAIRS - 1 and j == 2))
                        last.then_inc(job_made, 1)

                run(pe, PE_ORDER, step)

            @block.scalar
            def _(act):
                norm_s(act)

                def copy(dst, src):
                    return nc.scalar.activation(dst, src, ACT.Copy)

                def step(s, kind, n, i, img, mode, odd):
                    if s in JOB_BANK:
                        k = JOB_BANK[s]
                        act.wait_ge(*made(s, img))
                    if kind == "x":
                        copy(xt[:, 0:2], banks[:, k, 0:2 * SEQ].rearrange("p (h t) -> p h t", h=2)).then_inc(xt_hi, 1)
                    elif kind == "q":
                        if n % 3 == 0 and mode != "before":
                            act.wait_ge(stacked[n // 3], STACK * img)
                        copy(qk[:, 0, :, n], banks[:, k, 0:2 * SEQ].rearrange("p (g t) -> p g t", g=2)).then_inc(qk_hi, 1)
                    elif kind == "v":
                        c, col = n % 2, (n // 2) * VH
                        copy(val[odd][0:ROWS[c], 0, c, col:col + VH], banks[0:ROWS[c], k, 0:VH]).then_inc(v_hi, 1)
                    elif kind == "e":
                        act.wait_ge(max_made, PAIRS * img + n + 1)
                        for e in range(2):
                            for c in range(2):
                                last = nc.scalar.activation(pr[n % 3][0:ROWS[c], c, e, :], banks[0:ROWS[c], e, c * SEQ:(c + 1) * SEQ],
                                                            ACT.Exp, bias=nmx[n % 2][0:ROWS[c], c, e:e + 1], scale=SCALE,
                                                            accum_out=rsum[n % 2][0:ROWS[c], c, e:e + 1])
                            last.then_inc(freed[e], 1)
                    elif kind == "t":
                        for kc in range(2):
                            act.wait_ge(t_ready, 2 * (PAIRS * img + n) + kc + 1)
                            copy(pt[n % 2][0:ROWS[kc], 0, kc, :], bank_t[0:ROWS[kc], kc, 0:2 * SEQ]).then_inc(pt_hi, 1)
                    elif kind == "o":
                        act.wait_ge(o_ready, 3 * img + n + 1)
                        if n == 0 and mode != "first":
                            act.wait_ge(*made("w", img - 1))
                        copy(ot[:, 0, 2 * n:2 * n + 2, :], bank_o[:, (odd + n) % 2, 0:2 * SEQ].rearrange("p (f t) -> p f t", f=2)).then_inc(ot_hi, 1)

                run(act, ACT_ORDER, step)

            @block.vector
            def _(dve):
                v = nc.vector
                norm_v(dve)
                for r in range(2):
                    v.memset(mx[r][:], 0.0)
                    last = v.memset(rsum[r][:], 1.0)
                last.then_inc(filled, 1)
                dve.wait_ge(filled, 1)

                def low(dst, src, high):
                    return v.tensor_tensor(dst, src, high, ALU.subtract)

                def step(s, kind, n, i, img, mode, odd):
                    if s in JOB_BANK:
                        k = JOB_BANK[s]
                    if kind == "n":
                        if mode != "before":
                            dve.wait_ge(xt_hi, img)
                        for c in range(2):
                            last = normalise_twice(nc, S, xn[0:ROWS[c], c], 2 * img + c, ROWS[c], img, c)
                        last.then_inc(xn_made, 1)
                    elif kind == "x":
                        dve.wait_ge(xt_hi, img + 1)
                        low(xt[:, 2], banks[:, k, 0:SEQ], xt[:, 0])
                        low(xt[LO:P, 1], banks[LO:P, k, SEQ:2 * SEQ], xt[LO:P, 1]).then_inc(xt_split, 1)
                    elif kind == "q":
                        dve.wait_ge(qk_hi, PAIRS * img + n + 1)
                        low(qk[:, 1, :, n], banks[:, k, 0:2 * SEQ].rearrange("p (g t) -> p g t", g=2), qk[:, 0, :, n]).then_inc(qk_split, 1)
                    elif kind == "v":
                        dve.wait_ge(v_hi, 4 * img + n + 1)
                        c, col = n % 2, (n // 2) * VH
                        low(val[odd][0:ROWS[c], 1, c, col:col + VH], banks[0:ROWS[c], k, 0:VH],
                            val[odd][0:ROWS[c], 0, c, col:col + VH]).then_inc(v_split, 1)
                    elif kind == "m":
                        for e in range(2):
                            dve.wait_ge(ready[e], PAIRS * img + n + 1)
                        for c in range(2):
                            last = v.reduce_max(mx[n % 2][0:ROWS[c], c, :], banks[0:ROWS[c], 0:2, c * SEQ:(c + 1) * SEQ], AX.X)
                        last.then_inc(max_found, 1)
                        dve.wait_ge(max_found, PAIRS * img + n + 1)
                        v.tensor_scalar(nmx[n % 2][:], mx[n % 2][:], -SCALE, None, ALU.mult).then_inc(max_made, 1)
                    elif kind == "r":
                        dve.wait_ge(freed[1], PAIRS * img + n + 1)
                        v.reciprocal(rinv[n % 2][:], rsum[n % 2][:]).then_inc(inverted, 1)
                    elif kind == "t":
                        for kc in range(2):
                            dve.wait_ge(pt_hi, 2 * (PAIRS * img + n) + kc + 1)
                            last = low(pt[n % 2][0:ROWS[kc], 1, kc, :], bank_t[0:ROWS[kc], kc, 0:2 * SEQ], pt[n % 2][0:ROWS[kc], 0, kc, :])
                        last.then_inc(pt_split, 1)
                    elif kind == "o":
                        dve.wait_ge(ot_hi, 3 * img + n + 1)
                        low(ot[:, 1, 2 * n:2 * n + 2, :], bank_o[:, (odd + n) % 2, 0:2 * SEQ].rearrange("p (f t) -> p f t", f=2),
                            ot[:, 0, 2 * n:2 * n + 2, :]).then_inc(ot_split, 1)
                    elif kind == "w":
                        dve.wait_ge(*made(s, img))
                        for c in range(2):
                            last = v.tensor_tensor(h[0:ROWS[c], img, c, :], banks[0:ROWS[c], k, c * D:(c + 1) * D], h[0:ROWS[c], img, c, :], ALU.add)
                        last.then_inc(h_updated, 1)
                        dve.wait_ge(h_updated, img + 1)
                        for c in range(2):
                            v.bn_stats(S["stats"][0:ROWS[c], 2 * img + c, :], h[0:ROWS[c], img, c, :])

                run(dve, DVE_ORDER, step)

            @block.sync
            def _(sp):
                def step(s, kind, a, i, img, mode, odd):
                    if a == 0:
                        sp.wait_ge(qk_split, PAIRS * img + 3)
                    else:
                        sp.wait_ge(v_split, 4 * img + 2)
                    pairs = slice(3 * a, 3 * a + 3)
                    for e in range(2):
                        head = slice(e * DH, (e + 1) * DH)
                        for half in range(2):
                            rows = slice(half * DH, (half + 1) * DH)
                            sp.dma_start(qst[rows, :, e, pairs, :], qk[head, :, 0, pairs, :]).then_inc(stacked[a], 16)
                            sp.dma_start(kst[rows, e, pairs, :], qk[head, half, 1, pairs, :]).then_inc(stacked[a], 16)

                run(sp, ["d0'", "d1'"], step)

            @block.gpsimd
            def _(pool):
                def step(s, kind, n, i, img, mode, odd):
                    pool.wait_ge(inverted, PAIRS * img + n + 1)
                    for c in range(2):
                        p = pr[n % 3][0:ROWS[c], c]
                        inv = rinv[n % 2][0:ROWS[c], c, :].unsqueeze(2).to_broadcast([ROWS[c], 2, SEQ])
                        last = nc.gpsimd.tensor_tensor(p, p, inv, ALU.mult)
                    last.then_inc(prob_made, 1)

                run(pool, [f"p{n}" for n in range(PAIRS)], step)


def mlp_1(nc, S, out, n_img):
    h, mean, rstd = S["h"], S["mean"], S["rstd"]
    turns = n_img // 4
    PAIR = 2 * SEQ
    SP = SEQ + 1
    with ExitStack() as ctx:
        sb, ps, sem = stage_tools(nc, ctx)
        xn = [sb(f"z_xn{b}", [P, 2, 2, D]) for b in range(2)]
        xq = [sb(f"z_xq{b}", [P, 2, 2, D], BF16) for b in range(2)]
        xt = [sb(f"z_xt{b}", [KH, 2, 2, SEQ], BF16) for b in range(2)]
        act_out = [sb(f"z_act{r}", [P, PAIR]) for r in range(3)]
        hid = [sb(f"z_hid{b}", [P, HC, PAIR], BF16) for b in range(2)]
        res = [sb(f"z_res{b}", [P, 2, 2, D]) for b in range(2)]
        bank_x = ps("z_bank_x", [KH, 2, 2, 256], BF16)
        bank_h = [ps(f"z_bank_h{r}", [P, 512]) for r in range(4)]
        bank_y = [ps(f"z_bank_y{m}", [P, 512]) for m in range(2)]
        two = lambda name: [sem(f"z_{name}{b}") for b in range(2)]
        xn_made, clipped, quantised, turned, xt_done, bias_added, made_y, scaled, h_done, stored = (
            two("xn_made"), two("clipped"), two("quantised"), two("turned"), two("xt_done"), two("bias_added"),
            two("made_y"), two("scaled"), two("h_done"), two("stored"))
        fc_made, gelu_made, over_a2, bounded, hid_done = map(sem, ("z_fc_made", "z_gelu_made", "z_over_a2", "z_bounded", "z_hid_done"))
        norm_v, norm_s = norm_tables(nc, sb, sem, S, "n3")

        def image(u, b, m):
            return 4 * u + 2 * b + m

        def chunks_before(u, b):
            return (2 * u + b) * HC

        with nc.Block() as block:
            @block.vector
            def _(dve):
                v = nc.vector
                norm_v(dve)

                def quantise(u, b):
                    dve.wait_ge(quantised[b], u)
                    for m in range(2):
                        i = image(u, b, m)
                        for c in range(2):
                            last = v.tensor_scalar(xn[b][0:ROWS[c], m, c, :], h[0:ROWS[c], i, c, :],
                                                   mean[0:ROWS[c], bass.ds(2 * i + c, 1)], rstd[0:ROWS[c], bass.ds(2 * i + c, 1)],
                                                   ALU.subtract, ALU.mult)
                    last.then_inc(xn_made[b], 1)
                    dve.wait_ge(xn_made[b], u + 1)
                    for c in range(2):
                        x = xn[b][0:ROWS[c], :, c, :]
                        last = v.tensor_scalar(x, x, S["inv_a1"][0:ROWS[c], 0:1], 7.0, ALU.mult, ALU.min)
                    last.then_inc(clipped[b], 1)
                    dve.wait_ge(clipped[b], 2 * u + 1)
                    for c in range(2):
                        x = xn[b][0:ROWS[c], :, c, :]
                        last = v.tensor_scalar(x, x, -8.0, ROUND, ALU.max, ALU.add)
                    last.then_inc(clipped[b], 1)
                    dve.wait_ge(clipped[b], 2 * u + 2)
                    for c in range(2):
                        last = v.tensor_scalar(xq[b][0:ROWS[c], :, c, :], xn[b][0:ROWS[c], :, c, :], ROUND, None, ALU.subtract)
                    last.then_inc(quantised[b], 1)

                def take_turned_x(u, b):
                    dve.wait_ge(turned[b], u + 1)
                    v.tensor_copy(xt[b][:], bank_x[:, :, :, 0:SEQ]).then_inc(xt_done[b], 1)

                def quantise_hidden(u, b):
                    for f in range(HC):
                        n = chunks_before(u, b) + f + 1
                        a = act_out[f % 3][:]
                        dve.wait_ge(gelu_made, n)
                        v.tensor_scalar(a, a, S["inv_a2"][:, 0:1], S["q_hi"][:, 0:1], ALU.mult, ALU.min).then_inc(over_a2, 1)
                        dve.wait_ge(over_a2, n)
                        v.tensor_scalar(a, a, S["q_lo"][:, 0:1], ROUND, ALU.max, ALU.add).then_inc(bounded, 1)

                def finish(u, b):
                    dve.wait_ge(made_y[b], u + 1)
                    dve.wait_ge(bias_added[b], u + 1)
                    dve.wait_ge(stored[b], 32 * u)
                    for m in range(2):
                        for c in range(2):
                            last = v.tensor_tensor(res[b][0:ROWS[c], m, c, :], bank_y[m][0:ROWS[c], c * D:(c + 1) * D],
                                                   S["q2_scale"][0:ROWS[c], :], ALU.mult)
                    last.then_inc(scaled[b], 1)

                pipeline(dve, turns, [(quantise, 2), (quantise_hidden, 1), (take_turned_x, 2), (finish, 0)])

            @block.gpsimd
            def _(pool):
                def add_bias(u, b):
                    pool.wait_ge(xn_made[b], u + 1)
                    for m in range(2):
                        i = image(u, b, m)
                        for c in range(2):
                            last = nc.gpsimd.tensor_tensor(h[0:ROWS[c], i, c, :], h[0:ROWS[c], i, c, :],
                                                           S["q2_bias"][0:ROWS[c], :], ALU.add)
                    last.then_inc(bias_added[b], 1)

                def add_stream(u, b):
                    pool.wait_ge(scaled[b], u + 1)
                    pool.wait_ge(bias_added[b], u + 1)
                    for m in range(2):
                        i = image(u, b, m)
                        for c in range(2):
                            r = res[b][0:ROWS[c], m, c, :]
                            last = nc.gpsimd.tensor_tensor(r, h[0:ROWS[c], i, c, :], r, ALU.add)
                    last.then_inc(h_done[b], 1)

                pipeline(pool, turns, [(add_bias, 2), (add_stream, 0)])

            @block.sync
            def _(sp):
                def store(u, b):
                    sp.wait_ge(h_done[b], u + 1)
                    i = image(u, b, 0)
                    for c in range(2):
                        sp.dma_start(out[bass.ds(i, 2), c * P:c * P + ROWS[c], :].rearrange("m t d -> t m d"),
                                     res[b][0:ROWS[c], :, c, :]).then_inc(stored[b], 16)

                pipeline(sp, turns, [(store, 0)])
                for b in range(2):
                    sp.wait_ge(stored[b], 32 * turns)

            @block.scalar
            def _(act):
                norm_s(act)

                def gelu(u, b):
                    for f in range(HC + 1):
                        n = chunks_before(u, b) + f
                        if f < HC:
                            act.wait_ge(fc_made, n + 1)
                            act.wait_ge(hid_done, n - 2 if f >= 3 else chunks_before(u, b))
                            nc.scalar.activation(act_out[f % 3][:], bank_h[(2 * b + f) % 4][:, 0:PAIR], ACT.Gelu,
                                                 bias=S["q1_bias"][:, f:f + 1], scale=S["q1_scale"][:, f:f + 1]).then_inc(gelu_made, 1)
                        if f >= 1:
                            act.wait_ge(bounded, n)
                            nc.scalar.activation(hid[b][:, f - 1, :], act_out[(f - 1) % 3][:], ACT.Copy, bias=-ROUND).then_inc(hid_done, 1)

                pipeline(act, turns, [(gelu, 1)])

            @block.tensor
            def _(pe):
                t = nc.tensor

                def turn_x(u, b):
                    pe.wait_ge(quantised[b], u + 1)
                    pe.wait_ge(xt_done[1 - b], u + b)
                    for k in range(2):
                        for m in range(2):
                            for c in range(2):
                                last = t.transpose(bank_x[:, k, m, COLS[c]], xq[b][0:ROWS[c], m, c, k * KH:(k + 1) * KH],
                                                   S["ident_b"][0:ROWS[c], 0:ROWS[c]])
                    last.then_inc(turned[b], 1)

                def up(u, b):
                    pe.wait_ge(xt_done[b], u + 1)
                    for f in range(HC):
                        n = chunks_before(u, b) + f
                        pe.wait_ge(gelu_made, n - 3 if f >= 4 else chunks_before(u, b))
                        for k in range(2):
                            last = t.matmul(bank_h[(2 * b + f) % 4][:, 0:PAIR], S["q1"][:, k, f * P:(f + 1) * P],
                                            xt[b][:, k].rearrange("p m t -> p (m t)"), start=(k == 0), stop=(k == 1))
                        last.then_inc(fc_made, 1)

                def down(u, b):
                    pe.wait_ge(hid_done, chunks_before(u, b) + HC)
                    pe.wait_ge(scaled[1 - b], u + b)
                    for m in range(2):
                        for c in range(2):
                            lo = m * SEQ + c * P
                            for f in range(HC):
                                last = t.matmul(bank_y[m][0:ROWS[c], c * D:(c + 1) * D], hid[b][:, f, lo:lo + ROWS[c]],
                                                S["q2"][:, f, :], start=(f == 0), stop=(f == HC - 1))
                    last.then_inc(made_y[b], 1)

                pipeline(pe, turns, [(up, 1), (turn_x, 2), (down, 0)])


def laid_out(inp):
    import numpy as np

    f = {k: np.asarray(v) for k, v in inp.items()}
    x = f["x"]
    n = x.shape[0]
    npat = 14

    def halves(a):
        return a.reshape(2, KH, -1).transpose(1, 0, 2)

    def stacks(a):
        return np.stack([a[0:P], np.concatenate([a[P:D], a[P:D]])], axis=1)

    def chunks(a):
        return a.reshape(HC, P, -1).transpose(1, 0, 2)

    def rows(a, m=P):
        return np.broadcast_to(a.reshape(1, -1), (m, a.size))

    qkv = f["L1_attn_W_qkv"].reshape(D, DH, 3, HEADS).transpose(0, 2, 3, 1)
    qk = qkv[:, 0:2].reshape(D, 2, PAIRS, P).transpose(0, 2, 1, 3).reshape(D, 2 * HID)
    cls_bias = np.concatenate([f["L0_tok_class_token"].reshape(1, D), rows(f["L0_tok_b"], SEQ - 1)], axis=0)
    below = np.array([[[float(q < e) for e in EMBED_CHOICES] for q in (p, P + p % LO)] for p in range(P)], np.float32)
    return {
        "x": x.reshape(n, 3, npat, 2, 8, npat, 16).transpose(0, 4, 6, 1, 3, 2, 5).reshape(n, P, PATCH_K, npat * npat),
        "tok_w": f["L0_tok_W"].reshape(D, 3, 2, 8, 16).transpose(3, 4, 1, 2, 0).reshape(P, PATCH_K, D),
        "pos": f["L0_tok_pos_embed"],
        "cls_bias": cls_bias,
        "proj_w": f["L0_attn_proj_w"].T.reshape(3, NQ, D).transpose(1, 0, 2),
        "proj_b": rows(f["L0_attn_proj_b"]),
        "fc": stacks(f["L0_ffn_w_fc"].T),
        "fc_b": f["L0_ffn_b_fc"].reshape(1, HID),
        "fproj": stacks(f["L0_ffn_w_proj"]),
        "fproj_b": rows(f["L0_ffn_b_proj"]),
        "alpha_e": rows(f["L0_ffn_alpha_e"]),
        "alpha_r": rows(f["L0_ffn_alpha_r"]),
        "below": below,
        "identity": np.eye(P, dtype=np.float32),
        "wqkv": stacks(np.concatenate([qk, qkv[:, 2].reshape(D, HID)], axis=1)),
        "wo": chunks(f["L1_attn_W_0"]),
        "w1": halves(f["L1_ffn_w1"].T),
        "alpha_w1_rows": rows(f["L1_ffn_alpha_w1"], KH),
        "alpha_w1_cols": f["L1_ffn_alpha_w1"].reshape(HC, P).T,
        "b1": f["L1_ffn_b1"].reshape(HC, P).T,
        "w2": chunks(f["L1_ffn_w2"].T),
        "alpha_w2": rows(f["L1_ffn_alpha_w2"]),
        "b2": rows(f["L1_ffn_b2"]),
        "alpha_a1": rows(f["L1_ffn_alpha_a1"]),
        "alpha_a2": rows(f["L1_ffn_alpha_a2"]),
    }


def kernel(**inputs):
    import numpy as np
    import concourse.bacc as bacc
    from concourse.bass_utils import run_bass_kernel_spmd

    nc = bacc.Bacc("TRN2", target_bir_lowering=False, num_devices=1)
    arrays, A = {}, {}
    for name, a in laid_out(inputs).items():
        a = np.ascontiguousarray(a)
        arrays[f"in_{name}"] = a
        A[name] = nc.dram_tensor(f"in_{name}", a.shape, mybir.dt.from_np(a.dtype), kind="ExternalInput").ap()
    n = A["x"].shape[0]
    out = nc.dram_tensor("out_0", (n, SEQ, D), F32, kind="ExternalOutput").ap()
    build(nc, A, out)
    r = run_bass_kernel_spmd(nc, [arrays], core_ids=[0])
    return r.results[0]["out_0"]
```

```python
from contextlib import ExitStack

import concourse.bass as bass
from concourse import mybir

F32 = mybir.dt.float32
F16 = mybir.dt.float16
BF16 = mybir.dt.bfloat16
ALU = mybir.AluOpType
ACT = mybir.ActivationFunctionType
AX = mybir.AxisListType

P = 128
D = 192
KH = 96
LO = D - P
PATCH_K = 6
SEQ = 197
TAIL = SEQ - P
ROWS = (P, TAIL)
COLS = (slice(0, P), slice(P, SEQ))
HID = 768
HC = HID // P
HEADS = 12
DH = 64
PAIRS = HEADS // 2
NQ = 64
NK = SEQ - NQ
NK1 = P - NQ
EPS = 1e-5
ROUND = 12582912.0
PARTS = ((0, 0), (0, 1), (1, 0))
EMBED_CHOICES = (96, 144, 192)
RATIO_CHOICES = (2, 3, 4)


def build(nc, A, out):
    n_img = A["x"].shape[0]
    with ExitStack() as ctx:
        def sb(name, shape, dt=F32):
            return ctx.enter_context(nc.sbuf_tensor(name, shape, dt))

        S = {
            "h": sb("h", [P, n_img, 2, D]),
            "stats": sb("stats", [P, n_img * 2, 6]),
            "mean": sb("mean", [P, n_img * 2]),
            "rstd": sb("rstd", [P, n_img * 2]),
            "ident": sb("ident", [P, P]),
            "ident16": sb("ident16", [P, P], F16),
            "ident_b": sb("ident_b", [P, P], BF16),
            "pw": sb("pw", [P, 2, 3, D], F16),
            "pb": sb("pb", [P, D]),
            "fc": sb("fc", [P, 2, 2, HID], F16),
            "fc_bias": sb("fc_bias", [P, HC]),
            "fp": sb("fp", [P, 2, HC, D], F16),
            "fp_bias": sb("fp_bias", [P, D]),
            "wqkv": sb("wqkv", [P, 2, 2, 3 * HID], F16),
            "wo": sb("wo", [P, 2, HC, D], F16),
            "q1": sb("q1", [KH, 2, HID], BF16),
            "q2": sb("q2", [P, HC, D], BF16),
            "q1_scale": sb("q1_scale", [P, HC]),
            "q1_bias": sb("q1_bias", [P, HC]),
            "q2_scale": sb("q2_scale", [P, D]),
            "q2_bias": sb("q2_bias", [P, D]),
            "inv_a1": sb("inv_a1", [P, 1]),
            "inv_a2": sb("inv_a2", [P, 1]),
            "q_lo": sb("q_lo", [P, 1]),
            "q_hi": sb("q_hi", [P, 1]),
        }
        embed_patches(nc, A, S, n_img)
        attention_0(nc, S, n_img)
        mlp_0(nc, S, n_img)
        attention_1(nc, S, n_img)
        mlp_1(nc, S, out, n_img)


def stacked_products(w, x):
    high, both, low = (x[:, k] for k in range(3))
    return [(w[:, 0, 0], high), (w[:, 0, 0], low), (w[:, 1, 0], high), (w[:, 0, 1], both), (w[:, 1, 1], both)]


def normalise_twice(nc, S, dst, j, rows, i, c):
    h, scalars = S["h"], [S[k][0:rows, bass.ds(j, 1)] for k in ("mean", "rstd")]
    nc.vector.tensor_scalar(dst[:, 0:P], h[0:rows, i, c, 0:P], *scalars, ALU.subtract, ALU.mult)
    twice = h[0:rows, i, c, P:D].unsqueeze(1).to_broadcast([rows, 2, LO])
    return nc.vector.tensor_scalar(dst[:, P:2 * P].rearrange("p (a b) -> p a b", a=2), twice, *scalars, ALU.subtract, ALU.mult)


def stage_tools(nc, ctx):
    def sb(name, shape, dt=F32):
        return ctx.enter_context(nc.sbuf_tensor(name, shape, dt))

    def ps(name, shape, dt=F32):
        return ctx.enter_context(nc.psum_tensor(name, shape, dt))

    def sem(name):
        return ctx.enter_context(nc.semaphore(name))

    return sb, ps, sem


def embed_patches(nc, A, S, n_img):
    h, BUF, RAW_FROM, RAW_SIZE = S["h"], 4, 16, 48 * 2 * D
    with ExitStack() as ctx:
        sb, ps, sem = stage_tools(nc, ctx)
        if n_img * 2 * D >= RAW_FROM * 2 * D + RAW_SIZE:
            free = h[:].rearrange("p i c d -> p (i c d)")[:, RAW_FROM * 2 * D:]
        else:
            free = sb("raw_weights", [P, RAW_SIZE])[:]
        used = [0]

        def raw(rows, *shape):
            n = 1
            for k in shape:
                n *= k
            a = free[0:rows, used[0]:used[0] + n]
            used[0] += n
            if len(shape) == 2:
                a = a.rearrange("p (a b) -> p a b", a=shape[0])
            return a

        r_fc = raw(P, 2, HID)
        r_fp = raw(P, 2, HID)
        g = raw(P, 3, HID)
        coef = raw(P, 2, HID)
        a_a1 = raw(P, D)
        a_a2 = raw(P, HID)
        r_w1 = raw(KH, 2, HID)
        r_w2 = raw(P, HC, D)
        a_w1 = raw(KH, HID)
        a_w1c = raw(P, HC)
        a_w2 = raw(P, D)
        r_wo = raw(P, HC, D)
        r_pw = raw(P, 3, D)
        r_qkv = raw(P, 2, 3 * HID)
        r_tok = sb("r_tok", [P, PATCH_K, D])
        tok_w = sb("tok_w", [P, 2, PATCH_K, D], F16)
        posb = sb("posb", [P, 2, D])
        alpha = sb("alpha", [P, 6])
        below = sb("below", [P, 2, 3])
        c0b = sb("c0b", [1, HID])
        bfc = sb("bfc", [1, HID])
        one = sb("one", [1, 1])
        c1b = sb("c1b", [P, D])
        ar_sum = sb("ar_sum", [P, 1])
        cls_b = sb("cls_b", [P, 2, D])
        m1 = sb("m1", [P, 1])
        m2 = sb("m2", [P, 1])
        patches = [sb(f"patches{b}", [P, PATCH_K, SEQ]) for b in range(BUF)]
        parts = [sb(f"parts{b}", [P, 2, PATCH_K, SEQ + 1], F16) for b in range(BUF)]
        tokens = [ps(f"tokens{b}", [P, 512]) for b in range(BUF)]
        bank_t = [ps(f"w_turned{n}", [P, 2, D]) for n in range(3)]
        bank_b = ps("w_bias", [P, HC])
        tok_loaded, masks_loaded, quantised_loaded, attention_loaded, step, tok_hi, tok_split, masked, weights_hi, turned, bias_col, zeroed = map(
            sem, ("w_tok_loaded", "w_masks_loaded", "w_quantised_loaded", "w_attention_loaded", "w_step", "w_tok_hi", "w_tok_split", "w_masked",
                  "w_weights_hi", "w_turned_done", "w_bias_col", "t_zeroed"))
        loaded, patch_hi, patch_split, made, taken = ([sem(f"t_{name}{b}") for b in range(BUF)] for name in (
            "loaded", "patch_hi", "patch_split", "made", "taken"))

        tok_loads = [(r_tok[:], A["tok_w"]), (posb[:, 0, :], A["pos"][0:P, :]), (posb[0:TAIL, 1, :], A["pos"][P:SEQ, :]),
                     (cls_b[:, 0, :], A["cls_bias"][0:P, :]), (cls_b[0:TAIL, 1, :], A["cls_bias"][P:SEQ, :])]
        mask_loads = [(alpha[:, 0:3], A["alpha_e"]), (alpha[:, 3:6], A["alpha_r"]), (below[:], A["below"]),
                      (r_fc[:], A["fc"]), (r_fp[:], A["fproj"]), (bfc[:], A["fc_b"]), (S["fp_bias"][:], A["fproj_b"]),
                      (S["ident"][:], A["identity"])]
        quantised_loads = [(r_w1[:], A["w1"]), (a_w1[:], A["alpha_w1_rows"]), (a_w1c[:], A["alpha_w1_cols"]),
                           (r_w2[:], A["w2"]), (a_w2[:], A["alpha_w2"]), (a_a1[:], A["alpha_a1"]), (a_a2[:], A["alpha_a2"]),
                           (S["q1_bias"][:], A["b1"]), (S["q2_bias"][:], A["b2"]), (S["pb"][:], A["proj_b"])]
        attention_loads = [(r_pw[0:NQ], A["proj_w"]), (r_pw[NQ:P], A["proj_w"]), (r_wo[:], A["wo"])]
        attention_loads += [(r_qkv[:, k], A["wqkv"][:, k]) for k in range(2)]

        def rounds(eng, fn, between=()):
            peeled = max(1, len(between))
            for g in range(peeled):
                if g < n_img // BUF:
                    for b in range(BUF):
                        fn(g, b)
                if g < len(between) and between[g]:
                    between[g]()
            if n_img > BUF * peeled:
                with eng.Fori(peeled, n_img // BUF) as g:
                    for b in range(BUF):
                        fn(g, b)

        with nc.Block() as block:
            @block.sync
            def _(sp):
                def load(g, b):
                    sp.wait_ge(patch_split[b], g)
                    sp.dma_start(patches[b][:, :, 1:SEQ], A["x"][g * BUF + b]).then_inc(loaded[b], 16)

                for dst, src in tok_loads:
                    sp.dma_start(dst, src).then_inc(tok_loaded, 16)

                def load_masks():
                    for dst, src in mask_loads:
                        sp.dma_start(dst, src).then_inc(masks_loaded, 16)

                def load_quantised():
                    for dst, src in quantised_loads:
                        sp.dma_start(dst, src).then_inc(quantised_loaded, 16)

                def load_attention(first, end):
                    def load_some():
                        for dst, src in attention_loads[first:end]:
                            sp.dma_start(dst, src).then_inc(attention_loaded, 16)
                    return load_some

                rounds(sp, load, [load_masks, load_quantised, load_attention(0, 3), load_attention(3, 4), load_attention(4, 5)])

            @block.gpsimd
            def _(pool):
                for b in range(BUF):
                    last = nc.gpsimd.memset(patches[b][:, :, 0:1], 0.0)
                last.then_inc(zeroed, 1)

                def low_parts(g, b):
                    pool.wait_ge(patch_hi[b], g + 1)
                    p = parts[b]
                    nc.gpsimd.tensor_tensor(p[:, 1, :, 0:SEQ], patches[b][:], p[:, 0, :, 0:SEQ], ALU.subtract).then_inc(patch_split[b], 1)

                rounds(pool, low_parts)

            @block.scalar
            def _(act):
                def copy(dst, src):
                    return nc.scalar.activation(dst, src, ACT.Copy)

                def high_parts(g, b):
                    act.wait_ge(loaded[b], 16 * (g + 1))
                    act.wait_ge(made[b], g)
                    copy(parts[b][:, 0, :, 0:SEQ], patches[b][:]).then_inc(patch_hi[b], 1)

                def masked_weights():
                    act.wait_ge(masked, 1)
                    copy(S["fc"][:, 0], r_fc[:]).then_inc(weights_hi, 1)

                def attention_weights():
                    act.wait_ge(attention_loaded, 16 * len(attention_loads))
                    copy(S["ident16"][:], S["ident"][:])
                    copy(S["ident_b"][:], S["ident"][:])
                    copy(S["wo"][:, 0], r_wo[:])
                    copy(S["pw"][:, 0], r_pw[:])
                    copy(S["wqkv"][:, 0], r_qkv[:]).then_inc(weights_hi, 1)

                act.wait_ge(tok_loaded, 16 * len(tok_loads))
                copy(tok_w[:, 0], r_tok[:]).then_inc(tok_hi, 1)
                act.wait_ge(zeroed, 1)
                rounds(act, high_parts, [None, None, None, masked_weights, None, attention_weights])

            @block.tensor
            def _(pe):
                def multiply(g, b):
                    pe.wait_ge(patch_split[b], g + 1)
                    pe.wait_ge(taken[b], g)
                    for c in range(2):
                        for k in range(PATCH_K):
                            for n, (pa, pb) in enumerate(PARTS):
                                last = nc.tensor.matmul(tokens[b][0:ROWS[c], c * D:(c + 1) * D], parts[b][:, pa, k, COLS[c]],
                                                        tok_w[:, pb, k, :], start=(k == 0 and n == 0), stop=(k == PATCH_K - 1 and n == 2))
                    last.then_inc(made[b], 1)

                def turn_weights():
                    pe.wait_ge(masked, 2)
                    for n in range(3):
                        for f in range(2):
                            hidden = slice((2 * n + f) * P, (2 * n + f + 1) * P)
                            nc.tensor.transpose(bank_t[n][:, f, 0:P], r_fp[:, 0, hidden], S["ident"][:])
                            last = nc.tensor.transpose(bank_t[n][:, f, P:D], r_fp[0:LO, 1, hidden], S["ident"][0:LO, 0:LO])
                    last.then_inc(turned, 1)
                    for f in range(HC):
                        last = nc.tensor.matmul(bank_b[:, f:f + 1], bfc[:, f * P:(f + 1) * P], one[:], start=True, stop=True)
                    last.then_inc(bias_col, 1)

                pe.wait_ge(tok_split, 1)
                rounds(pe, multiply, [None, None, None, turn_weights])

            @block.vector
            def _(dve):
                done = [0]
                v = nc.vector

                def then(ins):
                    done[0] += 1
                    ins.then_inc(step, 1)
                    dve.wait_ge(step, done[0])

                def add_position(g, b):
                    i = g * BUF + b
                    dve.wait_ge(made[b], g + 1)
                    for c in range(2):
                        last = v.tensor_tensor(h[0:ROWS[c], i, c, :], tokens[b][0:ROWS[c], c * D:(c + 1) * D],
                                               posb[0:ROWS[c], c, :], ALU.add)
                    last.then_inc(taken[b], 1)
                    dve.wait_ge(taken[b], g + 1)
                    for c in range(2):
                        v.bn_stats(S["stats"][0:ROWS[c], 2 * i + c, :], h[0:ROWS[c], i, c, :])

                def coefficients():
                    dve.wait_ge(masks_loaded, 16 * len(mask_loads))
                    for i, e in enumerate(EMBED_CHOICES):
                        for j, r in enumerate(RATIO_CHOICES):
                            then(v.tensor_scalar(g[:, i, 0:r * e], g[:, i, 0:r * e], alpha[:, 3 + j:4 + j], None, ALU.add))
                        then(v.tensor_scalar(g[:, i, :], g[:, i, :], alpha[:, i:i + 1], None, ALU.mult))
                    for k in range(2):
                        then(v.tensor_scalar(coef[:, k, :], g[:, 0, :], below[:, k, 0:1], None, ALU.mult))
                        for i in (1, 2):
                            then(v.scalar_tensor_tensor(out=coef[:, k, :], in0=g[:, i, :], scalar=below[:, k, i:i + 1],
                                                        in1=coef[:, k, :], op0=ALU.mult, op1=ALU.add))

                def mask_weights():
                    then(v.tensor_tensor(c0b[:], g[0:1, 0, :], g[0:1, 1, :], ALU.add))
                    then(v.tensor_tensor(c0b[:], c0b[:], g[0:1, 2, :], ALU.add))
                    then(v.tensor_tensor(bfc[:], bfc[:], c0b[:], ALU.mult))
                    v.tensor_tensor(r_fc[:], r_fc[:], coef[:], ALU.mult).then_inc(masked, 1)
                    v.tensor_tensor(r_fp[:], r_fp[:], coef[:], ALU.mult).then_inc(masked, 1)
                    then(v.reduce_sum(ar_sum[:], alpha[:, 3:6], AX.X))
                    for i, e in enumerate(EMBED_CHOICES):
                        then(v.tensor_scalar(c1b[:, 0:e], c1b[:, 0:e], alpha[:, i:i + 1], None, ALU.add))
                    then(v.tensor_scalar(c1b[:], c1b[:], ar_sum[:, 0:1], None, ALU.mult))
                    then(v.tensor_tensor(S["fp_bias"][:], S["fp_bias"][:], c1b[:], ALU.mult))
                def take_turned_weights():
                    dve.wait_ge(weights_hi, 1)
                    v.tensor_tensor(S["fc"][:, 1], r_fc[:], S["fc"][:, 0], ALU.subtract)
                    dve.wait_ge(turned, 1)
                    for n in range(3):
                        hi, lo = (S["fp"][:, part, 2 * n:2 * n + 2, :] for part in range(2))
                        then(v.tensor_copy(hi, bank_t[n][:]))
                        then(v.tensor_tensor(lo, bank_t[n][:], hi, ALU.subtract))
                    dve.wait_ge(bias_col, 1)
                    then(v.tensor_copy(S["fc_bias"][:], bank_b[:]))

                def quantised_steps():
                    dve.wait_ge(quantised_loaded, 16 * len(quantised_loads))
                    then(v.reduce_sum(m1[:], a_a1[:], AX.X))
                    then(v.tensor_scalar(m1[:], m1[:], 1.0 / D, None, ALU.mult))
                    then(v.reciprocal(S["inv_a1"][:], m1[:]))
                    then(v.reduce_sum(m2[:], a_a2[:], AX.X))
                    then(v.tensor_scalar(m2[:], m2[:], 1.0 / HID, None, ALU.mult))
                    then(v.reciprocal(S["inv_a2"][:], m2[:]))
                    for bound, limits in ((S["q_lo"], (-10.0, -8.0, ALU.mult, ALU.max)), (S["q_hi"], (10.0, 7.0, ALU.mult, ALU.min))):
                        then(v.tensor_scalar(bound[:], S["inv_a2"][:], *limits))
                        then(v.tensor_scalar(bound[:], bound[:], ROUND, -ROUND, ALU.add, ALU.add))
                    then(v.tensor_scalar(S["q1_scale"][:], a_w1c[:], m1[:, 0:1], None, ALU.mult))
                    then(v.tensor_scalar(S["q2_scale"][:], a_w2[:], m2[:, 0:1], None, ALU.mult))
                    then(v.reciprocal(a_w1[:], a_w1[:]))
                    then(v.reciprocal(a_w2[:], a_w2[:]))

                def quantised_weights():
                    for k in range(2):
                        then(v.tensor_tensor(r_w1[:, k], r_w1[:, k], a_w1[:], ALU.mult))
                    for k in range(HC):
                        then(v.tensor_tensor(r_w2[:, k], r_w2[:, k], a_w2[:], ALU.mult))
                    for r, q in ((r_w1, S["q1"]), (r_w2, S["q2"])):
                        then(v.tensor_scalar(r[:], r[:], -8.0, 7.0, ALU.max, ALU.min))
                        then(v.tensor_scalar(q[:], r[:], ROUND, -ROUND, ALU.add, ALU.add))

                def low_weights():
                    dve.wait_ge(weights_hi, 2)
                    v.tensor_tensor(S["wo"][:, 1], r_wo[:], S["wo"][:, 0], ALU.subtract)
                    v.tensor_tensor(S["pw"][:, 1], r_pw[:], S["pw"][:, 0], ALU.subtract)
                    then(v.tensor_tensor(S["wqkv"][:, 1], r_qkv[:], S["wqkv"][:, 0], ALU.subtract))

                v.memset(S["stats"][:], 0.0)
                v.memset(g[:], 0.0)
                v.memset(c1b[:], 0.0)
                then(v.memset(one[:], 1.0))
                dve.wait_ge(tok_hi, 1)
                v.tensor_tensor(tok_w[:, 1], r_tok[:], tok_w[:, 0], ALU.subtract).then_inc(tok_split, 1)
                dve.wait_ge(tok_loaded, 16 * len(tok_loads))
                v.tensor_tensor(posb[:, 0, :], posb[:, 0, :], cls_b[:, 0, :], ALU.add)
                then(v.tensor_tensor(posb[0:TAIL, 1, :], posb[0:TAIL, 1, :], cls_b[0:TAIL, 1, :], ALU.add))
                rounds(dve, add_position, [None, coefficients, mask_weights, take_turned_weights, quantised_steps,
                                           quantised_weights, low_weights])


def norm_tables(nc, sb, sem, S, tag):
    n = S["mean"].shape[1]
    tmp = [sb(f"{tag}_tmp{k}", [P, n]) for k in range(3)]
    step, root_ready = sem(f"{tag}_step"), sem(f"{tag}_root_ready")
    VARIANCE = 7
    st = S["stats"]
    mean, rstd = S["mean"], S["rstd"]
    half = D / 2

    def vector(dve):
        done = [0]

        def then(ins):
            done[0] += 1
            ins.then_inc(step, 1)
            dve.wait_ge(step, done[0])

        v = nc.vector
        then(v.tensor_tensor(mean[:], st[:, :, 1], st[:, :, 4], ALU.add))
        then(v.tensor_scalar(mean[:], mean[:], 0.5, None, ALU.mult))
        then(v.tensor_tensor(tmp[0][:], st[:, :, 1], st[:, :, 4], ALU.subtract))
        then(v.scalar_tensor_tensor(out=tmp[0][:], in0=tmp[0][:], scalar=half / 2, in1=tmp[0][:], op0=ALU.mult, op1=ALU.mult))
        then(v.tensor_tensor(tmp[1][:], st[:, :, 2], st[:, :, 5], ALU.add))
        then(v.tensor_tensor(tmp[0][:], tmp[0][:], tmp[1][:], ALU.add))
        then(v.tensor_scalar(tmp[0][:], tmp[0][:], 1.0 / D, EPS, ALU.mult, ALU.add))
        assert done[0] == VARIANCE
        dve.wait_ge(root_ready, 1)
        then(v.reciprocal(rstd[:], tmp[1][:]))
        then(v.tensor_tensor(tmp[2][:], rstd[:], rstd[:], ALU.mult))
        then(v.tensor_tensor(tmp[2][:], tmp[2][:], tmp[0][:], ALU.mult))
        then(v.tensor_scalar(tmp[2][:], tmp[2][:], -0.5, 1.5, ALU.mult, ALU.add))
        then(v.tensor_tensor(rstd[:], rstd[:], tmp[2][:], ALU.mult))

    def scalar(act):
        act.wait_ge(step, VARIANCE)
        nc.scalar.activation(tmp[1][:], tmp[0][:], ACT.Sqrt).then_inc(root_ready, 1)

    return vector, scalar


def pipeline(eng, turns, order):
    pairs = 2 * turns

    def peeled(t):
        for fn, ahead in order:
            if 0 <= t + ahead < pairs:
                fn((t + ahead) // 2, (t + ahead) % 2)

    deepest = max(ahead for _, ahead in order)
    end = turns - (1 + deepest) // 2
    for t in range(-deepest, 2 if end > 0 else 0):
        peeled(t)
    if end > 1:
        with eng.Fori(1, end) as u:
            for b in range(2):
                for fn, ahead in order:
                    fn(u + (b + ahead) // 2, (b + ahead) % 2)
    for t in range(2 * max(end, 0), pairs + 1):
        peeled(t)


def attention_0(nc, S, n_img):
    h, mean, rstd = S["h"], S["mean"], S["rstd"]
    turns = n_img // 4
    SP = SEQ + 1
    SCALE = float(16) ** -0.5
    with ExitStack() as ctx:
        sb, ps, sem = stage_tools(nc, ctx)
        xn = [sb(f"xn{b}", [P, 2, 2, D]) for b in range(2)]
        xs = [sb(f"xs{b}", [P, 2, 2, 2, D], F16) for b in range(2)]
        xt = [sb(f"xt{b}", [KH, 2, 2, 2, SP], F16) for b in range(2)]
        pr = [sb(f"pr{b}", [P, NK]) for b in range(2)]
        prs = [sb(f"prs{b}", [P, 2, NK], F16) for b in range(2)]
        pt = [sb(f"pt{b}", [P, 2, 2 * P], F16) for b in range(2)]
        o = [sb(f"o{b}", [P, 3, 2, NQ], F16) for b in range(2)]
        mx = [sb(f"mx{b}", [P, 1]) for b in range(2)]
        nmx = [sb(f"nmx{b}", [P, 1]) for b in range(2)]
        rsum = [sb(f"rsum{b}", [P, 1]) for b in range(2)]
        rinv = [sb(f"rinv{b}", [P, 1]) for b in range(2)]
        bank_x = [ps(f"bank_x{p}", [KH, 2, 2, 256], F16) for p in range(2)]
        bank_s = ps("bank_s", [P, 512])
        bank_p = ps("bank_p", [P, 2, 512], F16)
        bank_o = ps("bank_o", [P, 512])
        bank_r = ps("bank_r", [P, 512])
        two = lambda name: [sem(f"a_{name}{b}") for b in range(2)]
        xn_made, xn_hi, xn_split = two("xn_made"), two("xn_hi"), two("xn_split")
        turned_x, xt_taken = two("turned_x"), two("xt_taken")
        keys_added, upper_added, scored, max_found, max_made, exp_made = two("keys_added"), two("upper_added"), two("scored"), two("max_found"), two("max_made"), two("exp_made")
        sum_inverted, pr_hi, pr_split = two("sum_inverted"), two("pr_hi"), two("pr_split")
        turned_p, pt_done = two("turned_p"), two("pt_done")
        mixed, o_hi, o_split = two("mixed"), two("o_hi"), two("o_split")
        projected, h_done = two("projected"), two("h_done")
        norm_v, norm_s = norm_tables(nc, sb, sem, S, "n0")

        def image(u, b, m):
            return 4 * u + 2 * b + m

        with nc.Block() as block:
            @block.vector
            def _(dve):
                v = nc.vector
                norm_v(dve)

                def normalise(u, b):
                    dve.wait_ge(keys_added[b], u)
                    for m in range(2):
                        i = image(u, b, m)
                        for c in range(2):
                            last = v.tensor_scalar(xn[b][0:ROWS[c], m, c, :], h[0:ROWS[c], i, c, :],
                                                   mean[0:ROWS[c], bass.ds(2 * i + c, 1)], rstd[0:ROWS[c], bass.ds(2 * i + c, 1)],
                                                   ALU.subtract, ALU.mult)
                    last.then_inc(xn_made[b], 1)

                def split_x(u, b):
                    dve.wait_ge(xn_hi[b], u + 1)
                    for c in range(2):
                        last = v.tensor_tensor(xs[b][0:ROWS[c], 1, :, c, :], xn[b][0:ROWS[c], :, c, :],
                                               xs[b][0:ROWS[c], 0, :, c, :], ALU.subtract)
                    last.then_inc(xn_split[b], 1)

                def maximum(u, b):
                    dve.wait_ge(scored[b], u + 1)
                    v.reduce_max(mx[b][:], bank_s[:, 0:NK], AX.X).then_inc(max_found[b], 1)
                    dve.wait_ge(max_found[b], u + 1)
                    v.tensor_scalar(nmx[b][:], mx[b][:], -SCALE, None, ALU.mult).then_inc(max_made[b], 1)

                def split_probabilities(u, b):
                    dve.wait_ge(exp_made[b], u + 1)
                    v.reciprocal(rinv[b][:], rsum[b][:]).then_inc(sum_inverted[b], 1)
                    dve.wait_ge(pr_hi[b], u + 1)
                    v.tensor_tensor(prs[b][:, 1, :], pr[b][:], prs[b][:, 0, :], ALU.subtract).then_inc(pr_split[b], 1)

                def take_turned_p(u, b):
                    dve.wait_ge(turned_p[b], u + 1)
                    v.tensor_copy(pt[b][NK1:P, :, 0:P], bank_p[NK1:P, :, 0:P])
                    v.tensor_copy(pt[b][0:TAIL, :, P:2 * P], bank_p[0:TAIL, :, P:2 * P]).then_inc(pt_done[b], 1)

                def split_o(u, b):
                    dve.wait_ge(o_hi[b], u + 1)
                    for m in range(2):
                        own, other = (slice(k * NQ, (k + 1) * NQ) for k in (m, 1 - m))
                        last = v.scalar_tensor_tensor(out=o[b][other, :, m], in0=bank_o[own, 0:D].rearrange("p (r j) -> p j r", j=3),
                                                      scalar=rinv[b][own, 0:1], in1=o[b][own, :, m], op0=ALU.mult, op1=ALU.subtract)
                    last.then_inc(o_split[b], 1)

                def finish(u, b):
                    dve.wait_ge(projected[b], u + 1)
                    dve.wait_ge(keys_added[b], u + 1)
                    for m in range(2):
                        i = image(u, b, m)
                        last = v.tensor_tensor(h[0:NQ, i, 0, :], bank_r[m * NQ:(m + 1) * NQ, 0:D], h[0:NQ, i, 0, :], ALU.add)
                    last.then_inc(h_done[b], 1)

                def statistics(u, b):
                    dve.wait_ge(h_done[b], u + 1)
                    for m in range(2):
                        i = image(u, b, m)
                        for c in range(2):
                            v.bn_stats(S["stats"][0:ROWS[c], 2 * i + c, :], h[0:ROWS[c], i, c, :])

                pipeline(dve, turns, [(finish, -1), (split_o, 0), (maximum, 1), (split_x, 2), (split_probabilities, 1),
                                      (statistics, -1), (take_turned_p, 1), (normalise, 3)])

            @block.gpsimd
            def _(pool):
                def add_keys(u, b):
                    pool.wait_ge(xn_made[b], u + 1)
                    pool.wait_ge(keys_added[1 - b], u + b)
                    for m in range(2):
                        i = image(u, b, m)
                        last = nc.gpsimd.tensor_tensor(h[NK1:P, i, 0, :], h[NK1:P, i, 0, :], xn[b][NK1:P, m, 0, :], ALU.add)
                    last.then_inc(upper_added[b], 1)
                    pool.wait_ge(upper_added[b], u + 1)
                    for m in range(2):
                        i = image(u, b, m)
                        nc.gpsimd.tensor_tensor(h[0:TAIL, i, 1, :], h[0:TAIL, i, 1, :], xn[b][0:TAIL, m, 1, :], ALU.add)
                        last = nc.gpsimd.tensor_tensor(h[0:NQ, i, 0, :], h[0:NQ, i, 0, :], S["pb"][0:NQ, :], ALU.add)
                    last.then_inc(keys_added[b], 1)

                pipeline(pool, turns, [(add_keys, 3)])

            @block.scalar
            def _(act):
                norm_s(act)

                def split_x(u, b):
                    act.wait_ge(xn_made[b], u + 1)
                    act.wait_ge(mixed[b], u)
                    for c in range(2):
                        last = nc.scalar.activation(xs[b][0:ROWS[c], 0, :, c, :], xn[b][0:ROWS[c], :, c, :], ACT.Copy)
                    last.then_inc(xn_hi[b], 1)

                def take_turned_x(u, b):
                    act.wait_ge(turned_x[b], u + 1)
                    for part in range(2):
                        last = nc.scalar.activation(xt[b][:, part, :, :, 0:SEQ], bank_x[part][:, :, :, 0:SEQ], ACT.Copy)
                    last.then_inc(xt_taken[b], 1)

                def exponentials(u, b):
                    act.wait_ge(max_made[b], u + 1)
                    nc.scalar.activation(pr[b][:], bank_s[:, 0:NK], ACT.Exp, bias=nmx[b][:, 0:1], scale=SCALE,
                                         accum_out=rsum[b][:, 0:1]).then_inc(exp_made[b], 1)
                    act.wait_ge(exp_made[b], u + 1)
                    nc.scalar.activation(prs[b][:, 0, :], pr[b][:], ACT.Copy).then_inc(pr_hi[b], 1)

                def scale_o(u, b):
                    act.wait_ge(mixed[b], u + 1)
                    act.wait_ge(sum_inverted[b], u + 1)
                    for m in range(2):
                        own = slice(m * NQ, (m + 1) * NQ)
                        last = nc.scalar.activation(o[b][own, :, m], bank_o[own, 0:D].rearrange("p (r j) -> p j r", j=3), ACT.Copy,
                                                    scale=rinv[b][own, 0:1])
                    last.then_inc(o_hi[b], 1)

                pipeline(act, turns, [(scale_o, 0), (split_x, 2), (exponentials, 1), (take_turned_x, 2)])

            @block.tensor
            def _(pe):
                t = nc.tensor

                def turn_x(u, b):
                    pe.wait_ge(xn_split[b], u + 1)
                    pe.wait_ge(xt_taken[1 - b], u + b)
                    for part in range(2):
                        for m in range(2):
                            for c in range(2):
                                for k in range(2):
                                    last = t.transpose(bank_x[part][:, k, m, COLS[c]], xs[b][0:ROWS[c], part, m, c, k * KH:(k + 1) * KH],
                                                       S["ident16"][0:ROWS[c], 0:ROWS[c]])
                    last.then_inc(turned_x[b], 1)

                def score(u, b):
                    pe.wait_ge(xt_taken[b], u + 1)
                    pe.wait_ge(exp_made[1 - b], u + b)
                    for k in range(2):
                        for n, (pa, pb) in enumerate(PARTS):
                            for m in range(2):
                                last = t.matmul(bank_s[m * NQ:(m + 1) * NQ, 0:NK], xt[b][:, pa, k, m, 0:NQ], xt[b][:, pb, k, m, NQ:SEQ],
                                                start=(k == 0 and n == 0), stop=(k == 1 and n == 2))
                    last.then_inc(scored[b], 1)

                def turn_p(u, b):
                    pe.wait_ge(pr_split[b], u + 1)
                    pe.wait_ge(pt_done[1 - b], u + b)
                    for part in range(2):
                        t.transpose(bank_p[0:TAIL, part, P:2 * P], prs[b][:, part, NK1:NK], S["ident16"][:])
                        last = t.transpose(bank_p[NK1:P, part, 0:P], prs[b][:, part, 0:NK1], S["ident16"][:])
                    last.then_inc(turned_p[b], 1)

                def mix(u, b):
                    pe.wait_ge(pt_done[b], u + 1)
                    pe.wait_ge(o_split[1 - b], u + b)
                    for m in range(2):
                        for n, (pa, pb) in enumerate(PARTS):
                            t.matmul(bank_o[m * NQ:(m + 1) * NQ, 0:D], pt[b][0:TAIL, pa, P + m * NQ:P + (m + 1) * NQ],
                                     xs[b][0:TAIL, pb, m, 1, :], start=(n == 0), stop=False)
                        for n, (pa, pb) in enumerate(PARTS):
                            last = t.matmul(bank_o[m * NQ:(m + 1) * NQ, 0:D], pt[b][NK1:P, pa, m * NQ:(m + 1) * NQ],
                                            xs[b][NK1:P, pb, m, 0, :], start=False, stop=(n == 2))
                    last.then_inc(mixed[b], 1)

                def project(u, b):
                    pe.wait_ge(scored[b], 1)
                    pe.wait_ge(o_split[b], u + 1)
                    pe.wait_ge(h_done[1 - b], u + b)
                    for j in range(3):
                        for part in range(2):
                            last = t.matmul(bank_r[:, 0:D], o[b][:, j].rearrange("p m r -> p (m r)"), S["pw"][:, part, j, :],
                                            start=(j == 0 and part == 0), stop=(j == 2 and part == 1))
                    last.then_inc(projected[b], 1)

                pipeline(pe, turns, [(mix, 0), (score, 1), (project, 0), (turn_p, 1), (turn_x, 2)])


def mlp_0(nc, S, n_img):
    h, mean, rstd = S["h"], S["mean"], S["rstd"]
    turns = n_img // 4
    PAIR = 2 * SEQ
    with ExitStack() as ctx:
        sb, ps, sem = stage_tools(nc, ctx)
        xn = [sb(f"m_xn{b}", [P, 2, 2, 2 * P]) for b in range(2)]
        xt = [sb(f"m_xt{b}", [P, 3, PAIR], F16) for b in range(2)]
        act_out = [sb(f"m_act{r}", [P, PAIR]) for r in range(2)]
        hid = [sb(f"m_hid{b}", [P, 2, HC, PAIR], F16) for b in range(2)]
        bank_x = [ps(f"m_bank_x{k}", [P, 512]) for k in range(2)]
        bank_h = [ps(f"m_bank_h{r}", [P, 512]) for r in range(4)]
        bank_y = [ps(f"m_bank_y{m}", [P, 512]) for m in range(2)]
        two = lambda name: [sem(f"m_{name}{b}") for b in range(2)]
        xn_made, turned, xt_hi, xt_split, made_y, h_done, bias_added = (
            two("xn_made"), two("turned"), two("xt_hi"), two("xt_split"), two("made_y"), two("h_done"), two("bias_added"))
        fc_made, gelu_made, hid_hi, hid_split = sem("m_fc_made"), sem("m_gelu_made"), sem("m_hid_hi"), sem("m_hid_split")
        norm_v, norm_s = norm_tables(nc, sb, sem, S, "n1")

        def image(u, b, m):
            return 4 * u + 2 * b + m

        def chunks_before(u, b):
            return (2 * u + b) * HC

        with nc.Block() as block:
            @block.vector
            def _(dve):
                v = nc.vector
                norm_v(dve)

                def normalise(u, b):
                    for m in range(2):
                        i = image(u, b, m)
                        for c in range(2):
                            last = normalise_twice(nc, S, xn[b][0:ROWS[c], m, c], 2 * i + c, ROWS[c], i, c)
                    last.then_inc(xn_made[b], 1)

                def split_x(u, b):
                    dve.wait_ge(xt_hi[b], u + 1)
                    v.tensor_tensor(xt[b][:, 2, :], bank_x[0][:, 0:PAIR], xt[b][:, 0, :], ALU.subtract)
                    last = v.tensor_tensor(xt[b][LO:P, 1, :], bank_x[1][LO:P, 0:PAIR], xt[b][LO:P, 1, :], ALU.subtract)
                    last.then_inc(xt_split[b], 1)

                def split_hidden(u, b):
                    for f in range(HC):
                        n = chunks_before(u, b) + f + 1
                        dve.wait_ge(gelu_made, n)
                        v.tensor_copy(hid[b][:, 0, f, :], act_out[f % 2][:]).then_inc(hid_hi, 1)
                        dve.wait_ge(hid_hi, n)
                        v.tensor_tensor(hid[b][:, 1, f, :], act_out[f % 2][:], hid[b][:, 0, f, :], ALU.subtract)\
                            .then_inc(hid_split, 1)

                def finish(u, b):
                    dve.wait_ge(made_y[b], u + 1)
                    dve.wait_ge(bias_added[b], u + 1)
                    for m in range(2):
                        i = image(u, b, m)
                        for c in range(2):
                            last = v.tensor_tensor(h[0:ROWS[c], i, c, :], bank_y[m][0:ROWS[c], c * D:(c + 1) * D],
                                                   h[0:ROWS[c], i, c, :], ALU.add)
                    last.then_inc(h_done[b], 1)
                    dve.wait_ge(h_done[b], u + 1)
                    for m in range(2):
                        i = image(u, b, m)
                        for c in range(2):
                            v.bn_stats(S["stats"][0:ROWS[c], 2 * i + c, :], h[0:ROWS[c], i, c, :])

                pipeline(dve, turns, [(normalise, 2), (split_hidden, 1), (split_x, 2), (finish, 0)])

            @block.gpsimd
            def _(pool):
                def add_bias(u, b):
                    pool.wait_ge(xn_made[b], u + 1)
                    for m in range(2):
                        i = image(u, b, m)
                        for c in range(2):
                            last = nc.gpsimd.tensor_tensor(h[0:ROWS[c], i, c, :], h[0:ROWS[c], i, c, :],
                                                           S["fp_bias"][0:ROWS[c], :], ALU.add)
                    last.then_inc(bias_added[b], 1)

                pipeline(pool, turns, [(add_bias, 2)])

            @block.scalar
            def _(act):
                norm_s(act)

                def split_x(u, b):
                    act.wait_ge(turned[b], u + 1)
                    for k in range(2):
                        last = nc.scalar.activation(xt[b][:, k, :], bank_x[k][:, 0:PAIR], ACT.Copy)
                    last.then_inc(xt_hi[b], 1)

                def gelu(u, b):
                    for f in range(HC):
                        n = chunks_before(u, b) + f
                        act.wait_ge(fc_made, n + 1)
                        if f >= 2:
                            act.wait_ge(hid_split, n - 1)
                        else:
                            act.wait_ge(hid_split, chunks_before(u, b))
                        nc.scalar.activation(act_out[f % 2][:], bank_h[(2 * b + f) % 4][:, 0:PAIR], ACT.Gelu_apprx_tanh,
                                             bias=S["fc_bias"][:, f:f + 1]).then_inc(gelu_made, 1)

                pipeline(act, turns, [(gelu, 1), (split_x, 2)])

            @block.tensor
            def _(pe):
                t = nc.tensor

                def turn_x(u, b):
                    pe.wait_ge(xn_made[b], u + 1)
                    pe.wait_ge(xt_split[1 - b], u + b)
                    for m in range(2):
                        for c in range(2):
                            lo, x = m * SEQ + c * P, xn[b][0:ROWS[c], m, c, :]
                            t.transpose(bank_x[0][:, lo:lo + ROWS[c]], x[:, 0:P], S["ident"][0:ROWS[c], 0:ROWS[c]])
                            last = t.transpose(bank_x[1][:, lo:lo + ROWS[c]], x[:, P:2 * P], S["ident"][0:ROWS[c], 0:ROWS[c]])
                    last.then_inc(turned[b], 1)

                def up(u, b):
                    pe.wait_ge(xt_split[b], u + 1)
                    for f in range(HC):
                        n = chunks_before(u, b) + f
                        if not (isinstance(n, int) and n < 4):
                            pe.wait_ge(gelu_made, n - 3)
                        for j, (w, x) in enumerate(stacked_products(S["fc"], xt[b])):
                            last = t.matmul(bank_h[(2 * b + f) % 4][:, 0:PAIR], w[:, f * P:(f + 1) * P], x,
                                            start=(j == 0), stop=(j == 4))
                        last.then_inc(fc_made, 1)

                def down(u, b):
                    pe.wait_ge(hid_split, chunks_before(u, b) + HC)
                    pe.wait_ge(h_done[1 - b], u + b)
                    for m in range(2):
                        for c in range(2):
                            lo = m * SEQ + c * P
                            for f in range(HC):
                                for j, (pa, pb) in enumerate(PARTS):
                                    last = t.matmul(bank_y[m][0:ROWS[c], c * D:(c + 1) * D], hid[b][:, pa, f, lo:lo + ROWS[c]],
                                                    S["fp"][:, pb, f, :], start=(f == 0 and j == 0), stop=(f == HC - 1 and j == 2))
                    last.then_inc(made_y[b], 1)

                pipeline(pe, turns, [(up, 1), (turn_x, 2), (down, 0)])


def attention_1(nc, S, n_img):
    h = S["h"]
    SCALE = float(DH) ** -0.5
    VH = 2 * D
    PE_ORDER = ("s0 t4^ v3 m3^ x'  s1 t5^ q0' m4^ q1'  s2 t0 q2' m5^ q3'  "
                "s3 t1 q4' m0 w^  s4 t2 q5' m1 v0'  s5 t3 v1' m2 v2'").split()
    ACT_ORDER = ("t4^ v3 e0 x'  o1^ t5^ q0' e1 q1'  t0 q2' e2 q3'  "
                 "o2^ t1 q4' e3  t2 q5' e4 v0'  o0 t3 v1' e5 v2'").split()
    DVE_ORDER = ("m0 t4^ n' r0 v3 x'  m1 o1^ t5^ r1 q0' q1'  m2 t0 r2 q2' q3'  "
                 "m3 o2^ t1 r3 q4' w^  m4 t2 r4 q5' v0'  m5 o0 t3 r5 v1' v2'").split()
    JOB_BANK = {"v3": 2, "x'": 3, "q0'": 2, "q1'": 3, "q2'": 2, "q3'": 3, "q4'": 2, "w^": 3, "q5'": 2, "v0'": 3, "v1'": 2, "v2'": 3}

    MODES = {"before": lambda s: s.endswith("'"), "first": lambda s: not s.endswith("^"), "body": lambda s: True,
             "last": lambda s: not s.endswith("'"), "after": lambda s: s.endswith("^")}

    SHIFT = {"'": 1, "^": -1}

    def jobs(mode, bank, rounds):
        return [(s, rounds + SHIFT.get(s[-1], 0)) for s in PE_ORDER if MODES[mode](s) and JOB_BANK.get(s) == bank]

    def job_before(s, mode):
        modes = list(MODES)
        earlier = {"before": [], "body": ["body"]}.get(mode, modes[:modes.index(mode)][-1:])
        line = [x for m in earlier for x in jobs(m, JOB_BANK[s], -1)] + jobs(mode, JOB_BANK[s], 0)
        me = line.index((s, SHIFT.get(s[-1], 0)))
        return (line[me - 1][0], line[me - 1][1] - line[me][1]) if me else None

    with ExitStack() as ctx:
        sb, ps, sem = stage_tools(nc, ctx)
        xn = sb("b_xn", [P, 2, 2 * P])
        xt = sb("b_xt", [P, 3, SEQ], F16)
        qk = sb("b_qk", [P, 2, 2, PAIRS, SEQ], F16)
        kst = sb("b_kst", [P, 2, PAIRS, SEQ], F16)
        qst = sb("b_qst", [P, 2, 2, PAIRS, SEQ], F16)
        val = [sb(f"b_val{r}", [P, 2, 2, HID], F16) for r in range(2)]
        pr = [sb(f"b_pr{r}", [P, 2, 2, SEQ]) for r in range(3)]
        pt = [sb(f"b_pt{r}", [P, 2, 2, 2 * SEQ], F16) for r in range(2)]
        ot = sb("b_ot", [P, 2, PAIRS, SEQ], F16)
        mx = [sb(f"b_mx{r}", [P, 2, 2]) for r in range(2)]
        nmx = [sb(f"b_nmx{r}", [P, 2, 2]) for r in range(2)]
        rsum = [sb(f"b_rsum{r}", [P, 2, 2]) for r in range(2)]
        rinv = [sb(f"b_rinv{r}", [P, 2, 2]) for r in range(2)]
        banks = ps("b_banks", [P, 4, 512])
        bank_t = ps("b_bank_t", [P, 2, 512])
        bank_o = ps("b_bank_o", [P, 2, 512])
        stacked = [sem(f"b_stacked{a}") for a in range(2)]
        STACK = 16 * 8
        ready = [sem(f"b_ready{e}") for e in range(2)]
        freed = [sem(f"b_freed{e}") for e in range(2)]
        (xn_made, xt_hi, xt_split, qk_hi, qk_split, v_hi, v_split, max_found, max_made, inverted, prob_made,
         t_ready, pt_hi, pt_split, o_ready, ot_hi, ot_split, filled, x_ready, q_ready, v_ready, w_ready, h_updated) = map(sem, (
             "b_xn_made", "b_xt_hi", "b_xt_split", "b_qk_hi", "b_qk_split", "b_v_hi", "b_v_split", "b_max_found",
             "b_max_made", "b_inverted", "b_prob_made", "b_t_ready", "b_pt_hi", "b_pt_split", "b_o_ready", "b_ot_hi",
             "b_ot_split", "b_filled", "b_x_ready", "b_q_ready", "b_v_ready", "b_w_ready", "b_h_updated"))
        norm_v, norm_s = norm_tables(nc, sb, sem, S, "n2")

        def made(s, img):
            kind, n = s[0], (int(s[1]) if s[1:2].isdigit() else 0)
            return {"x": (x_ready, img + 1), "q": (q_ready, PAIRS * img + n + 1), "v": (v_ready, 4 * img + n + 1),
                    "w": (w_ready, img + 1)}[kind]

        def left(s, img):
            kind, n = s[0], (int(s[1]) if s[1:2].isdigit() else 0)
            return {"x": (xt_split, img + 1), "q": (qk_split, PAIRS * img + n + 1), "v": (v_split, 4 * img + n + 1),
                    "w": (h_updated, img + 1)}[kind]

        def run(eng, order, step):
            def rounds(i, mode, parity):
                for s in order:
                    if MODES[mode](s):
                        shift = SHIFT.get(s[-1], 0)
                        n = int(s[1]) if s[1:2].isdigit() else 0
                        step(s, s[0], n, i, i + shift, mode, (parity + shift) % 2)

            rounds(-1, "before", 1)
            rounds(0, "first", 0)
            if n_img > 2:
                with eng.Fori(0, n_img // 2 - 1) as u:
                    rounds(2 * u + 1, "body", 1)
                    rounds(2 * u + 2, "body", 0)
            rounds(n_img - 1, "last", 1)
            rounds(n_img, "after", 0)

        with nc.Block() as block:
            @block.tensor
            def _(pe):
                t = nc.tensor

                def step(s, kind, n, i, img, mode, odd):
                    if s in JOB_BANK:
                        out, before, job_made = banks[:, JOB_BANK[s], :], job_before(s, mode), made(s, img)[0]
                        if before:
                            pe.wait_ge(*left(before[0], img + before[1]))
                    if kind == "x":
                        pe.wait_ge(xn_made, img + 1)
                        for c in range(2):
                            x, one = xn[0:ROWS[c], c, :], S["ident"][0:ROWS[c], 0:ROWS[c]]
                            t.transpose(out[:, c * P:c * P + ROWS[c]], x[:, 0:P], one)
                            last = t.transpose(out[:, SEQ + c * P:SEQ + c * P + ROWS[c]], x[:, P:2 * P], one)
                        last.then_inc(job_made, 1)
                    elif kind == "q":
                        pe.wait_ge(xt_split, img + 1)
                        for g in range(2):
                            for j, (w, x) in enumerate(stacked_products(S["wqkv"], xt)):
                                last = t.matmul(out[:, g * SEQ:(g + 1) * SEQ], w[:, (2 * n + g) * P:(2 * n + g + 1) * P], x,
                                                start=(j == 0), stop=(j == 4))
                        last.then_inc(job_made, 1)
                    elif kind == "v":
                        c, col = n % 2, 2 * HID + (n // 2) * VH
                        for j, (w, x) in enumerate(stacked_products(S["wqkv"], xt)):
                            last = t.matmul(out[0:ROWS[c], 0:VH], x[:, COLS[c]], w[:, col:col + VH], start=(j == 0), stop=(j == 4))
                        last.then_inc(job_made, 1)
                    elif kind == "s":
                        pe.wait_ge(stacked[n // 3], STACK * (img + 1))
                        for e in range(2):
                            pe.wait_ge(freed[e], PAIRS * img + n)
                            for c in range(2):
                                for part in range(2):
                                    last = t.matmul(banks[0:ROWS[c], e, c * SEQ:(c + 1) * SEQ], qst[:, part, e, n, COLS[c]],
                                                    kst[:, e, n, :], start=(part == 0), stop=(part == 1))
                            last.then_inc(ready[e], 1)
                    elif kind == "t":
                        pe.wait_ge(prob_made, PAIRS * img + n + 1)
                        pe.wait_ge(pt_split, PAIRS * img + n)
                        for kc in range(2):
                            for e in range(2):
                                for c in range(2):
                                    last = t.transpose(bank_t[0:ROWS[kc], kc, e * SEQ + c * P:e * SEQ + c * P + ROWS[c]],
                                                       pr[n % 3][0:ROWS[c], c, e, COLS[kc]], S["ident"][0:ROWS[c], 0:ROWS[c]])
                            last.then_inc(t_ready, 1)
                    elif kind == "m":
                        pe.wait_ge(pt_split, PAIRS * img + n + 1)
                        if n in (0, 3):
                            pe.wait_ge(v_split, 4 * img + (2 if n == 0 else 4))
                        if n % 2 == 0 and (mode != "first" or n == 4):
                            pe.wait_ge(ot_split, 3 * img + n // 2 - 1)
                        b, lo = (odd + n // 2) % 2, (n % 2) * SEQ
                        for kc in range(2):
                            for j, (pa, pb) in enumerate(PARTS):
                                for e in range(2):
                                    head = 2 * n + e
                                    last = t.matmul(bank_o[e * DH:(e + 1) * DH, b, lo:lo + SEQ],
                                                    val[odd][0:ROWS[kc], pa, kc, head * DH:(head + 1) * DH],
                                                    pt[n % 2][0:ROWS[kc], pb, kc, e * SEQ:(e + 1) * SEQ],
                                                    start=(kc == 0 and j == 0), stop=(kc == 1 and j == 2))
                        if n % 2 == 1:
                            last.then_inc(o_ready, 1)
                    elif kind == "w":
                        pe.wait_ge(ot_split, 3 * (img + 1))
                        for c in range(2):
                            for f in range(PAIRS):
                                for j, (pa, pb) in enumerate(PARTS):
                                    last = t.matmul(out[0:ROWS[c], c * D:(c + 1) * D], ot[:, pa, f, COLS[c]], S["wo"][:, pb, f, :],
                                                    start=(f == 0 and j == 0), stop=(f == PAIRS - 1 and j == 2))
                        last.then_inc(job_made, 1)

                run(pe, PE_ORDER, step)

            @block.scalar
            def _(act):
                norm_s(act)

                def copy(dst, src):
                    return nc.scalar.activation(dst, src, ACT.Copy)

                def step(s, kind, n, i, img, mode, odd):
                    if s in JOB_BANK:
                        k = JOB_BANK[s]
                        act.wait_ge(*made(s, img))
                    if kind == "x":
                        copy(xt[:, 0:2], banks[:, k, 0:2 * SEQ].rearrange("p (h t) -> p h t", h=2)).then_inc(xt_hi, 1)
                    elif kind == "q":
                        if n % 3 == 0 and mode != "before":
                            act.wait_ge(stacked[n // 3], STACK * img)
                        copy(qk[:, 0, :, n], banks[:, k, 0:2 * SEQ].rearrange("p (g t) -> p g t", g=2)).then_inc(qk_hi, 1)
                    elif kind == "v":
                        c, col = n % 2, (n // 2) * VH
                        copy(val[odd][0:ROWS[c], 0, c, col:col + VH], banks[0:ROWS[c], k, 0:VH]).then_inc(v_hi, 1)
                    elif kind == "e":
                        act.wait_ge(max_made, PAIRS * img + n + 1)
                        for e in range(2):
                            for c in range(2):
                                last = nc.scalar.activation(pr[n % 3][0:ROWS[c], c, e, :], banks[0:ROWS[c], e, c * SEQ:(c + 1) * SEQ],
                                                            ACT.Exp, bias=nmx[n % 2][0:ROWS[c], c, e:e + 1], scale=SCALE,
                                                            accum_out=rsum[n % 2][0:ROWS[c], c, e:e + 1])
                            last.then_inc(freed[e], 1)
                    elif kind == "t":
                        for kc in range(2):
                            act.wait_ge(t_ready, 2 * (PAIRS * img + n) + kc + 1)
                            copy(pt[n % 2][0:ROWS[kc], 0, kc, :], bank_t[0:ROWS[kc], kc, 0:2 * SEQ]).then_inc(pt_hi, 1)
                    elif kind == "o":
                        act.wait_ge(o_ready, 3 * img + n + 1)
                        if n == 0 and mode != "first":
                            act.wait_ge(*made("w", img - 1))
                        copy(ot[:, 0, 2 * n:2 * n + 2, :], bank_o[:, (odd + n) % 2, 0:2 * SEQ].rearrange("p (f t) -> p f t", f=2)).then_inc(ot_hi, 1)

                run(act, ACT_ORDER, step)

            @block.vector
            def _(dve):
                v = nc.vector
                norm_v(dve)
                for r in range(2):
                    v.memset(mx[r][:], 0.0)
                    last = v.memset(rsum[r][:], 1.0)
                last.then_inc(filled, 1)
                dve.wait_ge(filled, 1)

                def low(dst, src, high):
                    return v.tensor_tensor(dst, src, high, ALU.subtract)

                def step(s, kind, n, i, img, mode, odd):
                    if s in JOB_BANK:
                        k = JOB_BANK[s]
                    if kind == "n":
                        if mode != "before":
                            dve.wait_ge(xt_hi, img)
                        for c in range(2):
                            last = normalise_twice(nc, S, xn[0:ROWS[c], c], 2 * img + c, ROWS[c], img, c)
                        last.then_inc(xn_made, 1)
                    elif kind == "x":
                        dve.wait_ge(xt_hi, img + 1)
                        low(xt[:, 2], banks[:, k, 0:SEQ], xt[:, 0])
                        low(xt[LO:P, 1], banks[LO:P, k, SEQ:2 * SEQ], xt[LO:P, 1]).then_inc(xt_split, 1)
                    elif kind == "q":
                        dve.wait_ge(qk_hi, PAIRS * img + n + 1)
                        low(qk[:, 1, :, n], banks[:, k, 0:2 * SEQ].rearrange("p (g t) -> p g t", g=2), qk[:, 0, :, n]).then_inc(qk_split, 1)
                    elif kind == "v":
                        dve.wait_ge(v_hi, 4 * img + n + 1)
                        c, col = n % 2, (n // 2) * VH
                        low(val[odd][0:ROWS[c], 1, c, col:col + VH], banks[0:ROWS[c], k, 0:VH],
                            val[odd][0:ROWS[c], 0, c, col:col + VH]).then_inc(v_split, 1)
                    elif kind == "m":
                        for e in range(2):
                            dve.wait_ge(ready[e], PAIRS * img + n + 1)
                        for c in range(2):
                            last = v.reduce_max(mx[n % 2][0:ROWS[c], c, :], banks[0:ROWS[c], 0:2, c * SEQ:(c + 1) * SEQ], AX.X)
                        last.then_inc(max_found, 1)
                        dve.wait_ge(max_found, PAIRS * img + n + 1)
                        v.tensor_scalar(nmx[n % 2][:], mx[n % 2][:], -SCALE, None, ALU.mult).then_inc(max_made, 1)
                    elif kind == "r":
                        dve.wait_ge(freed[1], PAIRS * img + n + 1)
                        v.reciprocal(rinv[n % 2][:], rsum[n % 2][:]).then_inc(inverted, 1)
                    elif kind == "t":
                        for kc in range(2):
                            dve.wait_ge(pt_hi, 2 * (PAIRS * img + n) + kc + 1)
                            last = low(pt[n % 2][0:ROWS[kc], 1, kc, :], bank_t[0:ROWS[kc], kc, 0:2 * SEQ], pt[n % 2][0:ROWS[kc], 0, kc, :])
                        last.then_inc(pt_split, 1)
                    elif kind == "o":
                        dve.wait_ge(ot_hi, 3 * img + n + 1)
                        low(ot[:, 1, 2 * n:2 * n + 2, :], bank_o[:, (odd + n) % 2, 0:2 * SEQ].rearrange("p (f t) -> p f t", f=2),
                            ot[:, 0, 2 * n:2 * n + 2, :]).then_inc(ot_split, 1)
                    elif kind == "w":
                        dve.wait_ge(*made(s, img))
                        for c in range(2):
                            last = v.tensor_tensor(h[0:ROWS[c], img, c, :], banks[0:ROWS[c], k, c * D:(c + 1) * D], h[0:ROWS[c], img, c, :], ALU.add)
                        last.then_inc(h_updated, 1)
                        dve.wait_ge(h_updated, img + 1)
                        for c in range(2):
                            v.bn_stats(S["stats"][0:ROWS[c], 2 * img + c, :], h[0:ROWS[c], img, c, :])

                run(dve, DVE_ORDER, step)

            @block.sync
            def _(sp):
                def step(s, kind, a, i, img, mode, odd):
                    if a == 0:
                        sp.wait_ge(qk_split, PAIRS * img + 3)
                    else:
                        sp.wait_ge(v_split, 4 * img + 2)
                    pairs = slice(3 * a, 3 * a + 3)
                    for e in range(2):
                        head = slice(e * DH, (e + 1) * DH)
                        for half in range(2):
                            rows = slice(half * DH, (half + 1) * DH)
                            sp.dma_start(qst[rows, :, e, pairs, :], qk[head, :, 0, pairs, :]).then_inc(stacked[a], 16)
                            sp.dma_start(kst[rows, e, pairs, :], qk[head, half, 1, pairs, :]).then_inc(stacked[a], 16)

                run(sp, ["d0'", "d1'"], step)

            @block.gpsimd
            def _(pool):
                def step(s, kind, n, i, img, mode, odd):
                    pool.wait_ge(inverted, PAIRS * img + n + 1)
                    for c in range(2):
                        p = pr[n % 3][0:ROWS[c], c]
                        inv = rinv[n % 2][0:ROWS[c], c, :].unsqueeze(2).to_broadcast([ROWS[c], 2, SEQ])
                        last = nc.gpsimd.tensor_tensor(p, p, inv, ALU.mult)
                    last.then_inc(prob_made, 1)

                run(pool, [f"p{n}" for n in range(PAIRS)], step)


def mlp_1(nc, S, out, n_img):
    h, mean, rstd = S["h"], S["mean"], S["rstd"]
    turns = n_img // 4
    PAIR = 2 * SEQ
    SP = SEQ + 1
    with ExitStack() as ctx:
        sb, ps, sem = stage_tools(nc, ctx)
        xn = [sb(f"z_xn{b}", [P, 2, 2, D]) for b in range(2)]
        xq = [sb(f"z_xq{b}", [P, 2, 2, D], BF16) for b in range(2)]
        xt = [sb(f"z_xt{b}", [KH, 2, 2, SEQ], BF16) for b in range(2)]
        act_out = [sb(f"z_act{r}", [P, PAIR]) for r in range(4)]
        hid = [sb(f"z_hid{b}", [P, HC, PAIR], BF16) for b in range(2)]
        res = [sb(f"z_res{b}", [P, 2, 2, D]) for b in range(2)]
        bank_x = ps("z_bank_x", [KH, 2, 2, 256], BF16)
        bank_h = [ps(f"z_bank_h{r}", [P, 512]) for r in range(4)]
        bank_y = ps("z_bank_y", [P, 2, 512])
        two = lambda name: [sem(f"z_{name}{b}") for b in range(2)]
        xn_made, quantised, turned, xt_done, bias_added, made_y, scaled, h_done, stored = (
            two("xn_made"), two("quantised"), two("turned"), two("xt_done"), two("bias_added"),
            two("made_y"), two("scaled"), two("h_done"), two("stored"))
        fc_made, gelu_made, over_a2, rounded, hid_done = map(sem, ("z_fc_made", "z_gelu_made", "z_over_a2", "z_rounded", "z_hid_done"))
        scaled_rstd = sem("z_scaled_rstd")
        norm_v, norm_s = norm_tables(nc, sb, sem, S, "n3")

        def image(u, b, m):
            return 4 * u + 2 * b + m

        def chunks_before(u, b):
            return (2 * u + b) * HC

        LAG = 2

        with nc.Block() as block:
            @block.vector
            def _(dve):
                v = nc.vector
                norm_v(dve)
                v.tensor_scalar(rstd[:], rstd[:], S["inv_a1"][:, 0:1], None, ALU.mult).then_inc(scaled_rstd, 1)
                dve.wait_ge(scaled_rstd, 1)

                def quantise(u, b):
                    dve.wait_ge(quantised[b], u)
                    for m in range(2):
                        i = image(u, b, m)
                        for c in range(2):
                            last = v.tensor_scalar(xn[b][0:ROWS[c], m, c, :], h[0:ROWS[c], i, c, :],
                                                   mean[0:ROWS[c], bass.ds(2 * i + c, 1)], rstd[0:ROWS[c], bass.ds(2 * i + c, 1)],
                                                   ALU.subtract, ALU.mult)
                    last.then_inc(xn_made[b], 1)
                    dve.wait_ge(xn_made[b], u + 1)
                    for c in range(2):
                        last = v.tensor_scalar(xq[b][0:ROWS[c], :, c, :], xn[b][0:ROWS[c], :, c, :], ROUND, -ROUND, ALU.add, ALU.add)
                    last.then_inc(quantised[b], 1)

                def take_turned_x(u, b):
                    dve.wait_ge(turned[b], u + 1)
                    v.tensor_scalar(xt[b][:], bank_x[:, :, :, 0:SEQ], 7.0, -8.0, ALU.min, ALU.max).then_inc(xt_done[b], 1)

                def quantise_hidden(*chunks):
                    return lambda u, b: [quantise_chunk(u, b, f) for f in chunks]

                def quantise_chunk(u, b, f):
                    n = chunks_before(u, b) + f
                    if f < HC:
                        a = act_out[f % 4][:]
                        dve.wait_ge(gelu_made, n + 1)
                        v.tensor_scalar(a, a, S["inv_a2"][:, 0:1], ROUND, ALU.mult, ALU.add).then_inc(over_a2, 1)
                    if f >= 1:
                        a = hid[b][:, f - 1, :]
                        dve.wait_ge(rounded, n)
                        v.tensor_scalar(a, a, S["q_hi"][:, 0:1], S["q_lo"][:, 0:1], ALU.min, ALU.max).then_inc(hid_done, 1)

                def finish(u, b):
                    dve.wait_ge(made_y[b], u + 1)
                    dve.wait_ge(stored[b], 32 * u)
                    for c in range(2):
                        scale = S["q2_scale"][0:ROWS[c], :].unsqueeze(1).to_broadcast([ROWS[c], 2, D])
                        last = v.tensor_tensor(res[b][0:ROWS[c], :, c, :], bank_y[0:ROWS[c], :, c * D:(c + 1) * D], scale, ALU.mult)
                    last.then_inc(scaled[b], 1)

                pipeline(dve, turns, [(quantise_hidden(0, 1), 1), (finish, -1), (quantise_hidden(2), 1), (take_turned_x, 2),
                                      (quantise_hidden(3, 4, 5, 6), 1), (quantise, 3)])

            @block.gpsimd
            def _(pool):
                def add_bias(u, b):
                    pool.wait_ge(xn_made[b], u + 1)
                    for m in range(2):
                        i = image(u, b, m)
                        for c in range(2):
                            last = nc.gpsimd.tensor_tensor(h[0:ROWS[c], i, c, :], h[0:ROWS[c], i, c, :],
                                                           S["q2_bias"][0:ROWS[c], :], ALU.add)
                    last.then_inc(bias_added[b], 1)

                def add_stream(u, b):
                    pool.wait_ge(scaled[b], u + 1)
                    pool.wait_ge(bias_added[b], u + 1)
                    for m in range(2):
                        i = image(u, b, m)
                        for c in range(2):
                            r = res[b][0:ROWS[c], m, c, :]
                            last = nc.gpsimd.tensor_tensor(r, h[0:ROWS[c], i, c, :], r, ALU.add)
                    last.then_inc(h_done[b], 1)

                pipeline(pool, turns, [(add_bias, 2), (add_stream, 0)])

            @block.sync
            def _(sp):
                def store(u, b):
                    sp.wait_ge(h_done[b], u + 1)
                    i = image(u, b, 0)
                    for c in range(2):
                        sp.dma_start(out[bass.ds(i, 2), c * P:c * P + ROWS[c], :].rearrange("m t d -> t m d"),
                                     res[b][0:ROWS[c], :, c, :]).then_inc(stored[b], 16)

                pipeline(sp, turns, [(store, 0)])
                for b in range(2):
                    sp.wait_ge(stored[b], 32 * turns)

            @block.scalar
            def _(act):
                norm_s(act)

                def gelu(u, b):
                    for f in range(HC + LAG):
                        n = chunks_before(u, b) + f
                        if f < HC:
                            act.wait_ge(fc_made, n + 1)
                            act.wait_ge(rounded, n - 3 if f >= 4 else chunks_before(u, b))
                            nc.scalar.activation(act_out[f % 4][:], bank_h[(2 * b + f) % 4][:, 0:PAIR], ACT.Gelu,
                                                 bias=S["q1_bias"][:, f:f + 1], scale=S["q1_scale"][:, f:f + 1]).then_inc(gelu_made, 1)
                        if f >= LAG:
                            act.wait_ge(over_a2, n - LAG + 1)
                            nc.scalar.activation(hid[b][:, f - LAG, :], act_out[(f - LAG) % 4][:], ACT.Copy, bias=-ROUND).then_inc(rounded, 1)

                pipeline(act, turns, [(gelu, 1)])

            @block.tensor
            def _(pe):
                t = nc.tensor

                def turn_x(u, b):
                    pe.wait_ge(quantised[b], u + 1)
                    pe.wait_ge(xt_done[1 - b], u + b)
                    for k in range(2):
                        for m in range(2):
                            for c in range(2):
                                last = t.transpose(bank_x[:, k, m, COLS[c]], xq[b][0:ROWS[c], m, c, k * KH:(k + 1) * KH],
                                                   S["ident_b"][0:ROWS[c], 0:ROWS[c]])
                    last.then_inc(turned[b], 1)

                def up(u, b):
                    pe.wait_ge(xt_done[b], u + 1)
                    for f in range(HC):
                        n = chunks_before(u, b) + f
                        if not (isinstance(n, int) and n < 4):
                            pe.wait_ge(gelu_made, n - 3)
                        for k in range(2):
                            last = t.matmul(bank_h[(2 * b + f) % 4][:, 0:PAIR], S["q1"][:, k, f * P:(f + 1) * P],
                                            xt[b][:, k].rearrange("p m t -> p (m t)"), start=(k == 0), stop=(k == 1))
                        last.then_inc(fc_made, 1)

                def down(u, b):
                    pe.wait_ge(hid_done, chunks_before(u, b) + HC)
                    pe.wait_ge(scaled[1 - b], u + b)
                    for m in range(2):
                        for c in range(2):
                            lo = m * SEQ + c * P
                            for f in range(HC):
                                last = t.matmul(bank_y[0:ROWS[c], m, c * D:(c + 1) * D], hid[b][:, f, lo:lo + ROWS[c]],
                                                S["q2"][:, f, :], start=(f == 0), stop=(f == HC - 1))
                    last.then_inc(made_y[b], 1)

                pipeline(pe, turns, [(up, 1), (turn_x, 2), (down, 0)])


def laid_out(inp):
    import numpy as np

    f = {k: np.asarray(v) for k, v in inp.items()}
    x = f["x"]
    n = x.shape[0]
    npat = 14

    def halves(a):
        return a.reshape(2, KH, -1).transpose(1, 0, 2)

    def stacks(a):
        return np.stack([a[0:P], np.concatenate([a[P:D], a[P:D]])], axis=1)

    def chunks(a):
        return a.reshape(HC, P, -1).transpose(1, 0, 2)

    def rows(a, m=P):
        return np.broadcast_to(a.reshape(1, -1), (m, a.size))

    qkv = f["L1_attn_W_qkv"].reshape(D, DH, 3, HEADS).transpose(0, 2, 3, 1)
    qk = qkv[:, 0:2].reshape(D, 2, PAIRS, P).transpose(0, 2, 1, 3).reshape(D, 2 * HID)
    cls_bias = np.concatenate([f["L0_tok_class_token"].reshape(1, D), rows(f["L0_tok_b"], SEQ - 1)], axis=0)
    below = np.array([[[float(q < e) for e in EMBED_CHOICES] for q in (p, P + p % LO)] for p in range(P)], np.float32)
    return {
        "x": x.reshape(n, 3, npat, 2, 8, npat, 16).transpose(0, 4, 6, 1, 3, 2, 5).reshape(n, P, PATCH_K, npat * npat),
        "tok_w": f["L0_tok_W"].reshape(D, 3, 2, 8, 16).transpose(3, 4, 1, 2, 0).reshape(P, PATCH_K, D),
        "pos": f["L0_tok_pos_embed"],
        "cls_bias": cls_bias,
        "proj_w": f["L0_attn_proj_w"].T.reshape(3, NQ, D).transpose(1, 0, 2),
        "proj_b": rows(f["L0_attn_proj_b"]),
        "fc": stacks(f["L0_ffn_w_fc"].T),
        "fc_b": f["L0_ffn_b_fc"].reshape(1, HID),
        "fproj": stacks(f["L0_ffn_w_proj"]),
        "fproj_b": rows(f["L0_ffn_b_proj"]),
        "alpha_e": rows(f["L0_ffn_alpha_e"]),
        "alpha_r": rows(f["L0_ffn_alpha_r"]),
        "below": below,
        "identity": np.eye(P, dtype=np.float32),
        "wqkv": stacks(np.concatenate([qk, qkv[:, 2].reshape(D, HID)], axis=1)),
        "wo": chunks(f["L1_attn_W_0"]),
        "w1": halves(f["L1_ffn_w1"].T),
        "alpha_w1_rows": rows(f["L1_ffn_alpha_w1"], KH),
        "alpha_w1_cols": f["L1_ffn_alpha_w1"].reshape(HC, P).T,
        "b1": f["L1_ffn_b1"].reshape(HC, P).T,
        "w2": chunks(f["L1_ffn_w2"].T),
        "alpha_w2": rows(f["L1_ffn_alpha_w2"]),
        "b2": rows(f["L1_ffn_b2"]),
        "alpha_a1": rows(f["L1_ffn_alpha_a1"]),
        "alpha_a2": rows(f["L1_ffn_alpha_a2"]),
    }


def kernel(**inputs):
    import numpy as np
    import concourse.bacc as bacc
    from concourse.bass_utils import run_bass_kernel_spmd

    nc = bacc.Bacc("TRN2", target_bir_lowering=False, num_devices=1)
    arrays, A = {}, {}
    for name, a in laid_out(inputs).items():
        a = np.ascontiguousarray(a)
        arrays[f"in_{name}"] = a
        A[name] = nc.dram_tensor(f"in_{name}", a.shape, mybir.dt.from_np(a.dtype), kind="ExternalInput").ap()
    n = A["x"].shape[0]
    out = nc.dram_tensor("out_0", (n, SEQ, D), F32, kind="ExternalOutput").ap()
    build(nc, A, out)
    r = run_bass_kernel_spmd(nc, [arrays], core_ids=[0])
    return r.results[0]["out_0"]
```
